# Optimizing a Trainium2 kernel written in Bass

```python
import numpy as np
import jax
import jax.numpy as jnp

def _softmax(x, axis=-1):
    return jax.nn.softmax(x, axis=axis)

def _gelu(x):
    return jax.nn.gelu(x, approximate=True)

def _silu(x):
    return jax.nn.silu(x)

def _sigmoid(x):
    return jax.nn.sigmoid(x)

def _layernorm(x, axis=-1, eps=1e-05):
    m = jnp.mean(x, axis=axis, keepdims=True)
    v = jnp.var(x, axis=axis, keepdims=True)
    return (x - m) / jnp.sqrt(v + eps)

def _scatter_add(tgt, idx, src, axis=0):
    return tgt.at[idx].add(src)

def _segment_sum(src, seg, n):
    return jax.ops.segment_sum(src, seg, n)
kernel_name = 'mk_seq_postln_d2_jaxref_r8_c98a6e'

def setup_inputs(seed: int=0):
    np.random.seed(seed)
    _w = jnp.asarray

    def _L0_attn_setup():
        import jax, jax.numpy as jnp
        import numpy as np
        HEADS = 8
        CHUNK = 32

        def _gammas(heads):
            betas = jnp.linspace(np.log2(1.0 / 32.0), np.log2(1.0 / 512.0), heads)
            return 1.0 - jnp.exp2(betas)
        key = jax.random.key(seed)
        ks = jax.random.split(key, 4)
        H = 256
        x = jax.random.normal(ks[0], (4, 512, H), dtype=jnp.float32)
        sc = 1.0 / np.sqrt(H)
        Wq = jax.random.normal(ks[1], (H, H), dtype=jnp.float32) * sc
        Wk = jax.random.normal(ks[2], (H, H), dtype=jnp.float32) * sc
        Wv = jax.random.normal(ks[3], (H, H), dtype=jnp.float32) * sc
        z = jnp.zeros((H,), dtype=jnp.float32)
        return {'x': x, 'Wq': Wq, 'bq': z, 'Wk': Wk, 'bk': z, 'Wv': Wv, 'bv': z}
    _L0_attn_in = _L0_attn_setup()

    def _L0_ffn_setup():
        import jax, jax.numpy as jnp
        import numpy as np
        BLOCK = 64

        def dequant4bit(q, scale):
            return (q.astype(jnp.float32) - 7.5) * jnp.repeat(scale, BLOCK, axis=1)
        key = jax.random.key(seed)
        ks = jax.random.split(key, 11)
        B, S, D, H, R = (4, 256, 256, 1024, 16)
        return {'x1': jax.random.normal(ks[0], (B, S, D), jnp.float32), 'w_up_q': jax.random.randint(ks[1], (H, D), 0, 16, dtype=jnp.int32), 'w_up_scale': jax.random.uniform(ks[2], (H, D // BLOCK), jnp.float32) * 0.02, 'b_up': jax.random.normal(ks[3], (H,), jnp.float32) * 0.01, 'w_up_lora_a': jax.random.normal(ks[4], (D, R), jnp.float32) * 0.02, 'w_up_lora_b': jax.random.normal(ks[5], (R, H), jnp.float32) * 0.02, 'w_down_q': jax.random.randint(ks[6], (D, H), 0, 16, dtype=jnp.int32), 'w_down_scale': jax.random.uniform(ks[7], (D, H // BLOCK), jnp.float32) * 0.02, 'b_down': jax.random.normal(ks[8], (D,), jnp.float32) * 0.01, 'w_down_lora_a': jax.random.normal(ks[9], (H, R), jnp.float32) * 0.02, 'w_down_lora_b': jax.random.normal(ks[10], (R, D), jnp.float32) * 0.02}
    _L0_ffn_in = _L0_ffn_setup()

    def _L1_attn_setup():
        import jax, jax.numpy as jnp
        import numpy as np
        B, S, HID = (2, 256, 256)
        NH, NKV, HD = (32, 4, 128)
        EPS = 1e-06
        ROPE_THETA = 1000000.0

        def _rms_norm(x, w):
            xf = x.astype(jnp.float32)
            var = jnp.mean(xf * xf, axis=-1, keepdims=True)
            return (w * (xf * jax.lax.rsqrt(var + EPS))).astype(x.dtype)

        def _rope_tables(seq_len, head_dim, dtype):
            inv_freq = 1.0 / ROPE_THETA ** (jnp.arange(0, head_dim, 2, dtype=jnp.float32) / head_dim)
            t = jnp.arange(seq_len, dtype=jnp.float32)
            freqs = jnp.outer(t, inv_freq)
            emb = jnp.concatenate([freqs, freqs], axis=-1)
            return (jnp.cos(emb).astype(dtype), jnp.sin(emb).astype(dtype))

        def _rotate_half(x):
            x1, x2 = jnp.split(x, 2, axis=-1)
            return jnp.concatenate([-x2, x1], axis=-1)

        def _apply_rope(q, k, cos, sin):
            cos = cos[None, None, :, :]
            sin = sin[None, None, :, :]
            q = q * cos + _rotate_half(q) * sin
            k = k * cos + _rotate_half(k) * sin
            return (q, k)
        key = jax.random.key(seed)
        ks = jax.random.split(key, 7)
        s = 0.02
        return {'hidden_states': jax.random.normal(ks[0], (B, S, HID), jnp.float32), 'Wq': jax.random.normal(ks[1], (HID, NH * HD), jnp.float32) * s, 'Wk': jax.random.normal(ks[2], (HID, NKV * HD), jnp.float32) * s, 'Wv': jax.random.normal(ks[3], (HID, NKV * HD), jnp.float32) * s, 'Wo': jax.random.normal(ks[4], (NH * HD, HID), jnp.float32) * s, 'q_norm_w': jnp.ones((HD,), jnp.float32), 'k_norm_w': jnp.ones((HD,), jnp.float32)}
    _L1_attn_in = _L1_attn_setup()

    def _L1_ffn_setup():
        import jax, jax.numpy as jnp
        import numpy as np
        SWIGLU_ALPHA = 1.702
        SWIGLU_LIMIT = 7.0
        B, S, H, E, K, I = (2, 256, 256, 32, 4, 128)
        key = jax.random.key(seed)
        ks = jax.random.split(key, 8)
        return {'hidden_states': jax.random.normal(ks[0], (B, S, H), jnp.float32), 'gate_w': jax.random.normal(ks[1], (E, H), jnp.float32) * 0.02, 'gate_b': jnp.zeros((E,), jnp.float32), 'w_gate': jax.random.normal(ks[2], (E, H, I), jnp.float32) * 0.02, 'b_gate': jnp.zeros((E, I), jnp.float32), 'w_up': jax.random.normal(ks[3], (E, H, I), jnp.float32) * 0.02, 'b_up': jnp.zeros((E, I), jnp.float32), 'w_down': jax.random.normal(ks[4], (E, I, H), jnp.float32) * 0.02, 'b_down': jnp.zeros((E, H), jnp.float32)}
    _L1_ffn_in = _L1_ffn_setup()
    _d = {'L0_attn_x': _L0_attn_in['x'], 'L0_attn_Wq': _L0_attn_in['Wq'], 'L0_attn_bq': _L0_attn_in['bq'], 'L0_attn_Wk': _L0_attn_in['Wk'], 'L0_attn_bk': _L0_attn_in['bk'], 'L0_attn_Wv': _L0_attn_in['Wv'], 'L0_attn_bv': _L0_attn_in['bv'], 'L0_ffn_w_up_q': _L0_ffn_in['w_up_q'], 'L0_ffn_w_up_scale': _L0_ffn_in['w_up_scale'], 'L0_ffn_b_up': _L0_ffn_in['b_up'], 'L0_ffn_w_up_lora_a': _L0_ffn_in['w_up_lora_a'], 'L0_ffn_w_up_lora_b': _L0_ffn_in['w_up_lora_b'], 'L0_ffn_w_down_q': _L0_ffn_in['w_down_q'], 'L0_ffn_w_down_scale': _L0_ffn_in['w_down_scale'], 'L0_ffn_b_down': _L0_ffn_in['b_down'], 'L0_ffn_w_down_lora_a': _L0_ffn_in['w_down_lora_a'], 'L0_ffn_w_down_lora_b': _L0_ffn_in['w_down_lora_b'], 'L1_attn_Wq': _L1_attn_in['Wq'], 'L1_attn_Wk': _L1_attn_in['Wk'], 'L1_attn_Wv': _L1_attn_in['Wv'], 'L1_attn_Wo': _L1_attn_in['Wo'], 'L1_attn_q_norm_w': _L1_attn_in['q_norm_w'], 'L1_attn_k_norm_w': _L1_attn_in['k_norm_w'], 'L1_ffn_gate_w': _L1_ffn_in['gate_w'], 'L1_ffn_gate_b': _L1_ffn_in['gate_b'], 'L1_ffn_w_gate': _L1_ffn_in['w_gate'], 'L1_ffn_b_gate': _L1_ffn_in['b_gate'], 'L1_ffn_w_up': _L1_ffn_in['w_up'], 'L1_ffn_b_up': _L1_ffn_in['b_up'], 'L1_ffn_w_down': _L1_ffn_in['w_down'], 'L1_ffn_b_down': _L1_ffn_in['b_down']}
    _x0 = _d['L0_attn_x']
    _d['L0_attn_x'] = jax.random.normal(jax.random.fold_in(jax.random.key(seed), 1), (1, 1024, 256), dtype=_x0.dtype)
    del _x0
    return _d

def reference(L0_attn_x, L0_attn_Wq, L0_attn_bq, L0_attn_Wk, L0_attn_bk, L0_attn_Wv, L0_attn_bv, L0_ffn_w_up_q, L0_ffn_w_up_scale, L0_ffn_b_up, L0_ffn_w_up_lora_a, L0_ffn_w_up_lora_b, L0_ffn_w_down_q, L0_ffn_w_down_scale, L0_ffn_b_down, L0_ffn_w_down_lora_a, L0_ffn_w_down_lora_b, L1_attn_Wq, L1_attn_Wk, L1_attn_Wv, L1_attn_Wo, L1_attn_q_norm_w, L1_attn_k_norm_w, L1_ffn_gate_w, L1_ffn_gate_b, L1_ffn_w_gate, L1_ffn_b_gate, L1_ffn_w_up, L1_ffn_b_up, L1_ffn_w_down, L1_ffn_b_down):

    def _L0_attn_ref(x, Wq, bq, Wk, bk, Wv, bv):
        import jax, jax.numpy as jnp
        import numpy as np
        HEADS = 8
        CHUNK = 32

        def _gammas(heads):
            betas = jnp.linspace(np.log2(1.0 / 32.0), np.log2(1.0 / 512.0), heads)
            return 1.0 - jnp.exp2(betas)
        B, S, H = x.shape
        h, C = (HEADS, CHUNK)
        d = H // h
        N = S // C
        g = _gammas(h)
        q = x @ Wq + bq
        k = x @ Wk + bk
        v = x @ Wv + bv

        def split(t):
            return t.reshape(B, N, C, h, d).transpose(1, 0, 3, 2, 4)
        qc, kc, vc = (split(q), split(k), split(v))
        idx = jnp.arange(C)
        i, j = (idx[:, None], idx[None, :])
        D = jnp.where(i >= j, g[:, None, None] ** (i - j).astype(jnp.float32), 0.0)
        cross_scale = g[:, None] ** (idx + 1).astype(jnp.float32)
        kv_scale = g[:, None] ** (C - 1 - idx).astype(jnp.float32)
        chunk_decay = g ** C

        def step(Sstate, qkv):
            qi, ki, vi = qkv
            attn = jnp.einsum('bhid,bhjd->bhij', qi, ki) * D
            inner = jnp.einsum('bhij,bhjd->bhid', attn, vi)
            cross = jnp.einsum('bhid,bhde->bhie', qi * cross_scale[:, :, None], Sstate)
            S_new = chunk_decay[:, None, None] * Sstate + jnp.einsum('bhjd,bhje->bhde', ki * kv_scale[:, :, None], vi)
            return (S_new, inner + cross)
        S0 = jnp.zeros((B, h, d, d), dtype=x.dtype)
        _, outs = jax.lax.scan(step, S0, (qc, kc, vc))
        return outs.transpose(1, 0, 3, 2, 4).reshape(B, S, H)

    def _L0_ffn_ref(x1, w_up_q, w_up_scale, b_up, w_up_lora_a, w_up_lora_b, w_down_q, w_down_scale, b_down, w_down_lora_a, w_down_lora_b):
        import jax, jax.numpy as jnp
        import numpy as np
        BLOCK = 64

        def dequant4bit(q, scale):
            return (q.astype(jnp.float32) - 7.5) * jnp.repeat(scale, BLOCK, axis=1)
        w_up = dequant4bit(w_up_q, w_up_scale).T
        y1 = x1 @ w_up + b_up + x1 @ w_up_lora_a @ w_up_lora_b
        x2 = jax.nn.relu(y1)
        w_down = dequant4bit(w_down_q, w_down_scale).T
        y2 = x2 @ w_down + b_down + x2 @ w_down_lora_a @ w_down_lora_b
        return y2

    def _L1_attn_ref(hidden_states, Wq, Wk, Wv, Wo, q_norm_w, k_norm_w):
        import jax, jax.numpy as jnp
        import numpy as np
        B, S, HID = (2, 256, 256)
        NH, NKV, HD = (32, 4, 128)
        EPS = 1e-06
        ROPE_THETA = 1000000.0

        def _rms_norm(x, w):
            xf = x.astype(jnp.float32)
            var = jnp.mean(xf * xf, axis=-1, keepdims=True)
            return (w * (xf * jax.lax.rsqrt(var + EPS))).astype(x.dtype)

        def _rope_tables(seq_len, head_dim, dtype):
            inv_freq = 1.0 / ROPE_THETA ** (jnp.arange(0, head_dim, 2, dtype=jnp.float32) / head_dim)
            t = jnp.arange(seq_len, dtype=jnp.float32)
            freqs = jnp.outer(t, inv_freq)
            emb = jnp.concatenate([freqs, freqs], axis=-1)
            return (jnp.cos(emb).astype(dtype), jnp.sin(emb).astype(dtype))

        def _rotate_half(x):
            x1, x2 = jnp.split(x, 2, axis=-1)
            return jnp.concatenate([-x2, x1], axis=-1)

        def _apply_rope(q, k, cos, sin):
            cos = cos[None, None, :, :]
            sin = sin[None, None, :, :]
            q = q * cos + _rotate_half(q) * sin
            k = k * cos + _rotate_half(k) * sin
            return (q, k)
        b, s, _ = hidden_states.shape
        scaling = HD ** (-0.5)
        q = (hidden_states @ Wq).reshape(b, s, NH, HD)
        k = (hidden_states @ Wk).reshape(b, s, NKV, HD)
        v = (hidden_states @ Wv).reshape(b, s, NKV, HD)
        q = _rms_norm(q, q_norm_w)
        k = _rms_norm(k, k_norm_w)
        q = jnp.transpose(q, (0, 2, 1, 3))
        k = jnp.transpose(k, (0, 2, 1, 3))
        v = jnp.transpose(v, (0, 2, 1, 3))
        cos, sin = _rope_tables(s, HD, q.dtype)
        q, k = _apply_rope(q, k, cos, sin)
        groups = NH // NKV
        k = jnp.repeat(k, groups, axis=1)
        v = jnp.repeat(v, groups, axis=1)
        scores = jnp.einsum('bhqd,bhkd->bhqk', q, k) * scaling
        causal = jnp.tril(jnp.ones((s, s), bool))
        scores = jnp.where(causal[None, None], scores, jnp.finfo(scores.dtype).min)
        attn = jax.nn.softmax(scores.astype(jnp.float32), axis=-1).astype(q.dtype)
        out = jnp.einsum('bhqk,bhkd->bhqd', attn, v)
        out = jnp.transpose(out, (0, 2, 1, 3)).reshape(b, s, NH * HD)
        return out @ Wo

    def _L1_ffn_ref(hidden_states, gate_w, gate_b, w_gate, b_gate, w_up, b_up, w_down, b_down):
        import jax, jax.numpy as jnp
        import numpy as np
        SWIGLU_ALPHA = 1.702
        SWIGLU_LIMIT = 7.0
        B, S, H, E, K, I = (2, 256, 256, 32, 4, 128)
        Bb, Ss, Hh = hidden_states.shape
        x = hidden_states.reshape(-1, Hh)
        logits = x @ gate_w.T + gate_b
        topk_logits, topk_idx = jax.lax.top_k(logits, K)
        topk_weight = jax.nn.softmax(topk_logits.astype(jnp.float32), axis=-1)
        flat_idx = topk_idx.reshape(-1)
        xs = jnp.repeat(x, K, axis=0)
        order = jnp.argsort(flat_idx)
        xt = xs[order]
        gid = flat_idx[order]
        group_sizes = jnp.bincount(flat_idx, length=E).astype(jnp.int32)
        gate = jax.lax.ragged_dot(xt, w_gate, group_sizes) + b_gate[gid]
        up = jax.lax.ragged_dot(xt, w_up, group_sizes) + b_up[gid]
        gate = jnp.minimum(gate, SWIGLU_LIMIT)
        up = jnp.clip(up, -SWIGLU_LIMIT, SWIGLU_LIMIT)
        glu = gate * jax.nn.sigmoid(SWIGLU_ALPHA * gate)
        activated = (up + 1.0) * glu
        outs = jax.lax.ragged_dot(activated, w_down, group_sizes) + b_down[gid]
        inv = jnp.argsort(order)
        outs = outs[inv].reshape(-1, K, Hh)
        y = jnp.sum(outs * topk_weight[..., None], axis=1).astype(x.dtype)
        return y.reshape(Bb, Ss, Hh)
    x = L0_attn_x
    x = _layernorm(x + _L0_attn_ref(x, L0_attn_Wq, L0_attn_bq, L0_attn_Wk, L0_attn_bk, L0_attn_Wv, L0_attn_bv), axis=-1)
    x = _layernorm(x + _L0_ffn_ref(x, L0_ffn_w_up_q, L0_ffn_w_up_scale, L0_ffn_b_up, L0_ffn_w_up_lora_a, L0_ffn_w_up_lora_b, L0_ffn_w_down_q, L0_ffn_w_down_scale, L0_ffn_b_down, L0_ffn_w_down_lora_a, L0_ffn_w_down_lora_b), axis=-1)
    x = _layernorm(x + _L1_attn_ref(x, L1_attn_Wq, L1_attn_Wk, L1_attn_Wv, L1_attn_Wo, L1_attn_q_norm_w, L1_attn_k_norm_w), axis=-1)
    x = _layernorm(x + _L1_ffn_ref(x, L1_ffn_gate_w, L1_ffn_gate_b, L1_ffn_w_gate, L1_ffn_b_gate, L1_ffn_w_up, L1_ffn_b_up, L1_ffn_w_down, L1_ffn_b_down), axis=-1)
    return x

_drawn_inputs = setup_inputs


def setup_inputs(seed=0):
    import zlib

    import numpy as np

    out = dict(_drawn_inputs(seed))
    spreads = {'L0_attn_bq': (0.0, 0.1),
     'L0_attn_bk': (0.0, 0.1),
     'L0_attn_bv': (0.0, 0.1),
     'L1_attn_q_norm_w': (1.0, 0.6),
     'L1_attn_k_norm_w': (1.0, 0.6),
     'L1_ffn_gate_b': (0.0, 0.278),
     'L1_ffn_b_gate': (0.0, 0.8),
     'L1_ffn_b_up': (0.0, 0.8),
     'L1_ffn_b_down': (0.0, 0.1)}
    factors = {'L0_ffn_b_up': 6.28,
     'L0_ffn_b_down': 7.07,
     'L0_ffn_w_down_lora_b': 2.702,
     'L1_ffn_w_gate': 2.751,
     'L1_ffn_w_up': 8.0}
    for name, (base, spread) in spreads.items():
        noise = np.random.default_rng([zlib.crc32(name.encode()), seed]).standard_normal(out[name].shape)
        drawn = base * np.exp(spread * noise) if base else spread * noise
        out[name] = jnp.asarray(drawn.astype(out[name].dtype))
    for name, factor in factors.items():
        out[name] = (out[name] * factor).astype(out[name].dtype)
    return out
```

```python
from contextlib import ExitStack

import concourse.bass as bass
from concourse import mybir

F32 = mybir.dt.float32
F32R = mybir.dt.float32r
I32 = mybir.dt.int32
ALU = mybir.AluOpType
ACT = mybir.ActivationFunctionType
AX = mybir.AxisListType

P = 128
S, D = 1024, 256
NT = S // P
KD = D // P
LN_EPS = 1e-5
RH, RD = 8, 32
FH = 1024
FT = FH // P
LORA = 16
QBLOCK = 64
NH, NKV, HD = 32, 4, 128
SET = 4
SETS_PER_KV = NH // NKV // SET
STEPS = SETS_PER_KV * NT
RMS_EPS = 1e-6
MASKED = -1e30
NE, NI = 32, 128
TOPK = 4
HALF = 512
NHALF = S // HALF
ALPHA, LIMIT = 1.702, 7.0
ABSENT = -3e38


def split_matmul(pe, out, w_h, w_l, x_h, x_l, start, stop, shared=False):
    pe.matmul(out, w_h, x_h, start=start, stop=False, skip_group_check=shared)
    pe.matmul(out, w_h, x_l, start=False, stop=False, skip_group_check=shared)
    return pe.matmul(out, w_l, x_h, start=False, stop=stop, skip_group_check=shared)


class Norm:

    def __init__(self, nc, ctx, tag, x_tok, xT_h, xT_l, ident, banks):
        sb = lambda n, s: ctx.enter_context(nc.sbuf_tensor(f"{tag}_{n}", s, F32))
        sem = lambda n: ctx.enter_context(nc.semaphore(f"{tag}_{n}"))
        self.stats, self.mv = sb("stats", [P, NT, 6]), sb("mv", [P, NT, 2])
        self.var, self.power, self.rstd = sb("var", [P, NT]), sb("power", [P, NT]), sb("rstd", [P, NT])
        self.x, self.xT_h, self.xT_l, self.ident, self.banks = x_tok, xT_h, xT_l, ident, banks
        self.s_stats, self.s_mv, self.s_rstd = sem("stats_done"), sem("mv_done"), sem("rstd_done")
        self.s_x, self.s_tr, self.s_hi, self.s_lo = sem("x_done"), sem("tr_done"), sem("hi_done"), sem("lo_done")

    def dve_norm(self, dve, ready):
        for t in range(NT):
            ready(t)
            dve.bn_stats(self.stats[:, t, :], self.x[:, t, :]).then_inc(self.s_stats, 1)
        for t in range(NT):
            dve.wait_ge(self.s_stats, t + 1)
            dve.bn_aggr(self.mv[:, t, :], self.stats[:, t, :]).then_inc(self.s_mv, 1)
        dve.wait_ge(self.s_rstd, 3)
        for t in range(NT):
            dve.tensor_scalar(self.x[:, t, :], self.x[:, t, :], self.mv[:, t, 0:1], self.rstd[:, t:t + 1],
                              ALU.subtract, ALU.mult).then_inc(self.s_x, 1)

    def pool(self, pool):
        pool.memset(self.power[:], -0.5).then_inc(self.s_rstd, 1)
        pool.wait_ge(self.s_mv, NT)
        pool.tensor_scalar(self.var[:], self.mv[:, :, 1], LN_EPS, None, ALU.add).then_inc(self.s_rstd, 1)
        pool.wait_ge(self.s_rstd, 2)
        pool.tensor_tensor(self.rstd[:], self.var[:], self.power[:], ALU.pow).then_inc(self.s_rstd, 1)

    def tensor(self, pe):
        for t in range(NT):
            pe.wait_ge(self.s_x, t + 1)
            if t >= 2:
                pe.wait_ge(self.s_lo, t - 1)
            for k in range(KD):
                last = pe.transpose(self.banks[t % 2][:, k * P:(k + 1) * P],
                                    self.x[:, t, k * P:(k + 1) * P], self.ident)
            last.then_inc(self.s_tr, 1)

    def bank(self, t):
        return self.banks[t % 2][:, 0:D].rearrange("p (k q) -> p k q", k=KD)

    def scalar_hi(self, act):
        for t in range(NT):
            act.wait_ge(self.s_tr, t + 1)
            act.activation(self.xT_h[:, :, t * P:(t + 1) * P], self.bank(t), ACT.Copy).then_inc(self.s_hi, 1)

    def dve_lo(self, dve):
        for t in range(NT):
            dve.wait_ge(self.s_hi, t + 1)
            dve.tensor_tensor(self.xT_l[:, :, t * P:(t + 1) * P], self.bank(t),
                              self.xT_h[:, :, t * P:(t + 1) * P].bitcast(F32), ALU.subtract).then_inc(self.s_lo, 1)


def retention_stage(nc, ps, x_tok, xT_h, xT_l, ident, masks, d):
    with ExitStack() as ctx:
        sb = lambda n, s, dt=F32: ctx.enter_context(nc.sbuf_tensor(f"r_{n}", s, dt))
        sem = lambda n: ctx.enter_context(nc.semaphore(f"r_{n}"))
        xT = sb("xT", [P, KD, S])
        wqk = sb("wqk", [P, KD, 2 * D])
        wkv = sb("wkv", [P, KD, 2 * D])
        bqk = sb("bqk", [P, 4])
        bkv = sb("bkv", [P, 2 * D])
        decay = sb("decay", [P, 4, 2, P])
        qgain = sb("qgain", [P, 2, P])
        kgain = sb("kgain", [P, D])
        blockdiag = sb("blockdiag", [P, D])
        chunk_gain = sb("chunk_gain", [P, 2])
        qkT = sb("qkT", [P, 4, S])
        qgT = sb("qgT", [P, 2, 2, P])
        kv = sb("kv", [P, 2, 2 * D])
        kg = sb("kg", [P, 2, D])
        aT = sb("aT", [P, 2, 4, 2, P])
        state = sb("state", [P, 2, P])
        fresh = sb("fresh", [P, D])

        loaded = sem("loaded")
        x_loaded = sem("x_loaded")
        qkT_mm, qkT_done = sem("qkT_mm"), sem("qkT_done")
        kv_mm, kv_done, kg_done = sem("kv_mm"), sem("kv_done"), sem("kg_done")
        qg_done, state_zero = sem("qg_done"), sem("state_zero")
        score_mm, aT_done = sem("score_mm"), sem("aT_done")
        out_mm, out_done = sem("out_mm"), sem("out_done")
        state_mm, fresh_done, state_done = sem("state_mm"), sem("fresh_done"), sem("state_done")
        norm = Norm(nc, ctx, "rn", x_tok, xT_h, xT_l, ident, (ps[:, 6, :], ps[:, 7, :]))
        N_LOADS = 11
        block = ctx.enter_context(nc.Block())

        @block.sync
        def _(sp):
            sp.dma_start(wqk[:], d["r_wqk"].rearrange("(k p) n -> p k n", p=P)).then_inc(loaded, 16)
            sp.dma_start(xT[:], d["xT"].rearrange("(k p) n -> p k n", p=P)).then_inc(loaded, 16)
            sp.dma_start(bqk[:], d["r_bqk"]).then_inc(loaded, 16)
            sp.dma_start(wkv[:], d["r_wkv"].rearrange("(k p) n -> p k n", p=P)).then_inc(loaded, 16)
            sp.dma_start(bkv[:], d["r_bkv"].broadcast_to([P, 2 * D])).then_inc(loaded, 16)
            sp.dma_start(decay[:], d["c_decay"]).then_inc(loaded, 16)
            sp.dma_start(qgain[:], d["c_qgain"]).then_inc(loaded, 16)
            sp.dma_start(kgain[:], d["c_kgain"]).then_inc(loaded, 16)
            sp.dma_start(blockdiag[:], d["c_blockdiag"]).then_inc(loaded, 16)
            sp.dma_start(chunk_gain[:], d["c_chunkgain"]).then_inc(loaded, 16)
            sp.dma_start(ident, d["c_ident"]).then_inc(loaded, 16)
            sp.dma_start(x_tok[:], d["x"].rearrange("(t p) n -> p t n", p=P)).then_inc(x_loaded, 16)

        @block.tensor
        def _(pe):
            pe.wait_ge(loaded, 16 * N_LOADS)
            for n in range(8):
                f, th = n // 2, n % 2
                if n >= 2:
                    pe.wait_ge(qkT_done, n - 1)
                for k in range(KD):
                    last = pe.matmul(ps[:, n % 2, :], wqk[:, k, f * P:(f + 1) * P],
                                     xT[:, k, th * HALF:(th + 1) * HALF], start=(k == 0), stop=(k == KD - 1))
                last.then_inc(qkT_mm, 1)

            def project(c):
                if c >= 2:
                    pe.wait_ge(kv_done, 2 * (c - 1))
                else:
                    pe.wait_ge(qkT_done, 7 + c)
                for k in range(KD):
                    last = pe.matmul(ps[:, c % 2, :], xT[:, k, c * P:(c + 1) * P], wkv[:, k, :],
                                     start=(k == 0), stop=(k == KD - 1))
                last.then_inc(kv_mm, 1)

            def scores(c):
                if c == 0:
                    pe.wait_ge(qkT_done, 8)
                else:
                    pe.wait_ge(aT_done, c)
                for h in range(RH):
                    r = slice(RD * (h % 4), RD * (h % 4) + RD)
                    last = pe.matmul(ps[:, 2 + h % 4, (h // 4) * P:(h // 4 + 1) * P],
                                     qkT[r, 2 + h // 4, c * P:(c + 1) * P], qkT[r, h // 4, c * P:(c + 1) * P],
                                     start=True, stop=True)
                last.then_inc(score_mm, 1)

            project(0)
            project(1)
            scores(0)
            for c in range(NT):
                pe.wait_ge(kg_done, c + 1)
                pe.wait_ge(kv_done, 2 * c + 2)
                if c >= 1:
                    pe.wait_ge(fresh_done, c)
                for g in range(2):
                    last = pe.matmul(ps[:, 7, g * P:(g + 1) * P], kg[:, c % 2, g * P:(g + 1) * P],
                                     kv[:, c % 2, D + g * P:D + (g + 1) * P], start=True, stop=True)
                last.then_inc(state_mm, 1)
                pe.wait_ge(qg_done, c + 1)
                pe.wait_ge(state_done, c + 1)
                pe.wait_ge(aT_done, c + 1)
                if c >= 1:
                    pe.wait_ge(out_done, c)
                for g in range(2):
                    pe.matmul(ps[:, 6, g * P:(g + 1) * P], qgT[:, c % 2, g, :], state[:, g, :],
                              start=(g == 0), stop=False, skip_group_check=True)
                for h in range(RH):
                    last = pe.matmul(ps[:, 6, h * RD:(h + 1) * RD], aT[:, c % 2, h % 4, h // 4, :],
                                     kv[:, c % 2, D + h * RD:D + (h + 1) * RD], start=False,
                                     stop=(h == RH - 1), skip_group_check=True)
                last.then_inc(out_mm, 1)
                if c + 1 < NT:
                    scores(c + 1)
                if c + 2 < NT:
                    project(c + 2)
            pe.wait_ge(out_done, NT)
            norm.tensor(pe)

        @block.scalar
        def _(act):
            act.wait_ge(loaded, 16 * N_LOADS)
            for n in range(8):
                f, th = n // 2, n % 2
                act.wait_ge(qkT_mm, n + 1)
                act.activation(qkT[:, f, th * HALF:(th + 1) * HALF], ps[:, n % 2, :], ACT.Identity,
                               bias=bqk[:, f:f + 1]).then_inc(qkT_done, 1)
            norm.scalar_hi(act)

        @block.gpsimd
        def _(pool):
            pool.memset(state[:], 0.0).then_inc(state_zero, 1)
            norm.pool(pool)

        @block.vector
        def _(dve):
            dve.wait_ge(loaded, 16 * N_LOADS)
            dve.wait_ge(state_zero, 1)
            dve.tensor_copy(state[:], state[:]).then_inc(state_done, 1)

            def keys_values(c):
                dve.wait_ge(kv_mm, c + 1)
                if c >= 2:
                    dve.wait_ge(out_mm, c - 1)
                for j in range(2):
                    dve.tensor_tensor(kv[:, c % 2, j * D:(j + 1) * D], ps[:, c % 2, j * D:(j + 1) * D],
                                      bkv[:, j * D:(j + 1) * D], ALU.add).then_inc(kv_done, 1)
                dve.wait_ge(kv_done, 2 * c + 1)
                dve.tensor_tensor(kg[:, c % 2, :], kv[:, c % 2, 0:D], kgain[:], ALU.mult).then_inc(kg_done, 1)
                if c == 0:
                    dve.wait_ge(qkT_done, 8)
                dve.tensor_tensor(qgT[:, c % 2, :, :], qkT[:, 0:2, c * P:(c + 1) * P], qgain[:], ALU.mult)\
                   .then_inc(qg_done, 1)

            keys_values(0)
            dve.wait_ge(x_loaded, 16)
            for c in range(NT):
                dve.wait_ge(score_mm, c + 1)
                dve.tensor_tensor(aT[:, c % 2, :, :, :].rearrange("p a b q -> p a (b q)"), ps[:, 2:6, 0:2 * P],
                                  decay[:].rearrange("p a b q -> p a (b q)"), ALU.mult).then_inc(aT_done, 1)
                if c + 1 < NT:
                    keys_values(c + 1)
                dve.wait_ge(state_mm, c + 1)
                dve.wait_ge(state_done, c + 1)
                dve.tensor_tensor(fresh[:], ps[:, 7, 0:D], blockdiag[:], ALU.mult).then_inc(fresh_done, 1)
                dve.wait_ge(out_mm, c + 1)
                dve.tensor_tensor(x_tok[:, c, :], ps[:, 6, 0:D], x_tok[:, c, :], ALU.add).then_inc(out_done, 1)
                dve.wait_ge(fresh_done, c + 1)
                for g in range(2):
                    last = dve.scalar_tensor_tensor(out=state[:, g, :], in0=state[:, g, :],
                                                    scalar=chunk_gain[:, g:g + 1],
                                                    in1=fresh[:, g * P:(g + 1) * P], op0=ALU.mult, op1=ALU.add)
                last.then_inc(state_done, 1)
            norm.dve_norm(dve, lambda t: dve.wait_ge(out_done, t + 1))
            norm.dve_lo(dve)


def ffn_stage(nc, ps, x_tok, xT_h, xT_l, ident, masks, d):
    with ExitStack() as ctx:
        sb = lambda n, s, dt=F32: ctx.enter_context(nc.sbuf_tensor(f"f_{n}", s, dt))
        sem = lambda n: ctx.enter_context(nc.semaphore(f"f_{n}"))
        quant = [sb("quant0", [P, KD, FH], I32), sb("quant1", [P, FT, D], I32)]
        scale = [sb("scale0", [P, KD, FH]), sb("scale1", [P, FT, D])]
        w = scale
        w_h = [sb("w0h", [P, KD, FH], F32R), sb("w1h", [P, FT, D], F32R)]
        w_l = [sb("w0l", [P, KD, FH], F32R), sb("w1l", [P, FT, D], F32R)]
        lora_a = [sb("lora_a0", [LORA, D]), sb("lora_a1", [LORA, FH])]
        lora_b = [sb("lora_b0", [LORA, FH]), sb("lora_b1", [LORA, D])]
        b_up = sb("b_up", [P, FT])
        b_down = sb("b_down", [P, D])
        hid = sb("hid", [P, 2, HALF])
        hid_h = sb("hid_h", [P, FT, HALF], F32R)
        hid_l = sb("hid_l", [P, FT, HALF], F32R)

        loaded = sem("loaded")
        lora_mm, w_scaled, w_full, w_hi, w_lo = (sem(n) for n in ("lora_mm", "w_scaled", "w_full", "w_hi", "w_lo"))
        up_mm, relu_done, hid_hi, hid_lo = (sem(n) for n in ("up_mm", "relu_done", "hid_hi", "hid_lo"))
        down_mm, res_done, sum_done = sem("down_mm"), sem("res_done"), sem("sum_done")
        norm = Norm(nc, ctx, "fn", x_tok, xT_h, xT_l, ident, (ps[:, 6, :], ps[:, 7, :]))
        def piece(n, a):
            if n < 4:
                return a[0][:, n // 2, (n % 2) * HALF:(n % 2 + 1) * HALF]
            return a[1][:, 2 * (n - 4):2 * (n - 3), :].rearrange("p a b -> p (a b)")
        N_LOADS = 2 * (1 + 2 + 2) + 2
        block = ctx.enter_context(nc.Block())

        @block.sync
        def _(sp):
            for j, (name, kt) in enumerate((("up", KD), ("down", FT))):
                sp.dma_start(quant[j][:], d[f"f_{name}_q"].rearrange("(k p) n -> p k n", p=P)).then_inc(loaded, 16)
                for b in range(P // QBLOCK):
                    src = d[f"f_{name}_scale"].rearrange("(k b o) n -> b o k n", b=P // QBLOCK, o=1)[b]
                    sp.dma_start(scale[j][QBLOCK * b:QBLOCK * (b + 1), :, :],
                                 src.broadcast_to([QBLOCK, kt, src.shape[2]])).then_inc(loaded, 16)
                sp.dma_start(lora_a[j][:], d[f"f_{name}_a"]).then_inc(loaded, 16)
                sp.dma_start(lora_b[j][:], d[f"f_{name}_b"]).then_inc(loaded, 16)
            sp.dma_start(b_up[:], d["f_b_up"]).then_inc(loaded, 16)
            sp.dma_start(b_down[:], d["f_b_down"].broadcast_to([P, D])).then_inc(loaded, 16)

        @block.tensor
        def _(pe):
            pe.wait_ge(loaded, 16 * N_LOADS)
            for n in range(8):
                if n >= 2:
                    pe.wait_ge(w_full, n - 1)
                if n < 4:
                    last = pe.matmul(ps[:, n % 2, :], lora_a[0][:, (n // 2) * P:(n // 2 + 1) * P],
                                     lora_b[0][:, (n % 2) * HALF:(n % 2 + 1) * HALF], start=True, stop=True)
                else:
                    for j in range(2):
                        row = 2 * (n - 4) + j
                        last = pe.matmul(ps[:, n % 2, j * D:(j + 1) * D], lora_a[1][:, row * P:(row + 1) * P],
                                         lora_b[1][:], start=True, stop=True)
                last.then_inc(lora_mm, 1)
            pe.wait_ge(w_lo, 8)
            for th in range(NHALF):
                for f in range(FT):
                    n = th * FT + f
                    if n >= 2:
                        pe.wait_ge(relu_done, n - 1)
                    for k in range(KD):
                        cols = slice(th * HALF, (th + 1) * HALF)
                        last = split_matmul(pe, ps[:, 2 + n % 2, :], w_h[0][:, k, f * P:(f + 1) * P],
                                            w_l[0][:, k, f * P:(f + 1) * P], xT_h[:, k, cols], xT_l[:, k, cols],
                                            k == 0, k == KD - 1)
                    last.then_inc(up_mm, 1)
                pe.wait_ge(hid_lo, (th + 1) * FT)
                for q in range(HALF // P):
                    n = th * (HALF // P) + q
                    if n >= 2:
                        pe.wait_ge(sum_done, n - 1)
                    for f in range(FT):
                        last = split_matmul(pe, ps[:, 4 + n % 2, 0:D], hid_h[:, f, q * P:(q + 1) * P],
                                            hid_l[:, f, q * P:(q + 1) * P], w_h[1][:, f, :], w_l[1][:, f, :],
                                            f == 0, f == FT - 1)
                    last.then_inc(down_mm, 1)
            norm.tensor(pe)

        @block.scalar
        def _(act):
            for n in range(NHALF * FT):
                act.wait_ge(relu_done, n + 1)
                if n >= FT:
                    act.wait_ge(down_mm, HALF // P)
                act.activation(hid_h[:, n % FT, :], hid[:, n % 2, :], ACT.Copy).then_inc(hid_hi, 1)
            norm.scalar_hi(act)

        @block.gpsimd
        def _(pool):
            for n in range(8):
                pool.wait_ge(w_full, n + 1)
                pool.tensor_scalar(piece(n, w_h), piece(n, w), 1.0, None, ALU.mult).then_inc(w_hi, 1)
            norm.pool(pool)

        @block.vector
        def _(dve):
            dve.wait_ge(loaded, 16 * N_LOADS)

            def low(n):
                dve.wait_ge(w_hi, n + 1)
                dve.tensor_tensor(piece(n, w_l), piece(n, w), piece(n, w_h).bitcast(F32), ALU.subtract)\
                   .then_inc(w_lo, 1)

            for n in range(8):
                dve.scalar_tensor_tensor(out=piece(n, w), in0=piece(n, quant), scalar=-7.5, in1=piece(n, scale),
                                         op0=ALU.add, op1=ALU.mult).then_inc(w_scaled, 1)
                dve.wait_ge(lora_mm, n + 1)
                dve.wait_ge(w_scaled, n + 1)
                dve.tensor_tensor(piece(n, w), ps[:, n % 2, :], piece(n, w), ALU.add).then_inc(w_full, 1)
                if n >= 2:
                    low(n - 2)
            low(6)
            low(7)
            for t in range(NT):
                dve.tensor_tensor(x_tok[:, t, :], x_tok[:, t, :], b_down[:], ALU.add).then_inc(res_done, 1)

            def hidden_low(n):
                dve.wait_ge(hid_hi, n + 1)
                dve.tensor_tensor(hid_l[:, n % FT, :], hid[:, n % 2, :], hid_h[:, n % FT, :].bitcast(F32),
                                  ALU.subtract).then_inc(hid_lo, 1)

            for th in range(NHALF):
                for f in range(FT):
                    n = th * FT + f
                    dve.wait_ge(up_mm, n + 1)
                    if n >= 2:
                        dve.wait_ge(hid_lo, n - 1)
                    dve.tensor_scalar(hid[:, n % 2, :], ps[:, 2 + n % 2, :], b_up[:, f:f + 1], 0.0,
                                      ALU.add, ALU.max).then_inc(relu_done, 1)
                    if f >= 1:
                        hidden_low(n - 1)
                hidden_low(th * FT + FT - 1)
                for q in range(HALF // P):
                    n = th * (HALF // P) + q
                    dve.wait_ge(down_mm, n + 1)
                    dve.wait_ge(res_done, NT)
                    dve.tensor_tensor(x_tok[:, n, :], ps[:, 4 + n % 2, 0:D], x_tok[:, n, :], ALU.add)\
                       .then_inc(sum_done, 1)
            norm.dve_norm(dve, lambda t: dve.wait_ge(sum_done, t + 1))
            norm.dve_lo(dve)


def attention_stage(nc, ps, x_tok, xT_h, xT_l, ident, masks, d):
    ident_r, mask_r = masks
    with ExitStack() as ctx:
        sb = lambda n, s, dt=F32: ctx.enter_context(nc.sbuf_tensor(f"a_{n}", s, dt))
        sem = lambda n: ctx.enter_context(nc.semaphore(f"a_{n}"))
        cosw = sb("cosw", [P, 2, NT, HD])
        sinw = sb("sinw", [P, 2, NT, HD])
        normw = sb("normw", [P, 2, HD])
        wkv = sb("wkv", [P, KD, 2 * HD])
        wkv_h, wkv_l = sb("wkv_h", [P, KD, 2 * HD], F32R), sb("wkv_l", [P, KD, 2 * HD], F32R)
        W = KD * SET * HD
        wset = sb("wset", [P, 2, 2, W])
        wset_h, wset_l = sb("wset_h", [P, 2, 2, W], F32R), sb("wset_l", [P, 2, 2, W], F32R)
        v_h, v_l = sb("v_h", [P, NT, HD], F32R), sb("v_l", [P, NT, HD], F32R)
        kT_h, kT_l = sb("kT_h", [P, S], F32R), sb("kT_l", [P, S], F32R)
        kss, kvar, krs, power = sb("kss", [P, NT]), sb("kvar", [P, NT]), sb("krs", [P, NT]), sb("power", [P, NT])
        square = sb("square", [P, 2, SET, HD])
        qrot = sb("qrot", [P, 2, SET * HD])
        qsum = sb("qsum", [P, SET * HD])
        qss, qvar, qrs = sb("qss", [P, 2, SET]), sb("qvar", [P, 2, SET]), sb("qrs", [P, 2, SET])
        qT_h, qT_l = sb("qT_h", [P, 2, SET * P], F32R), sb("qT_l", [P, 2, SET * P], F32R)
        probs = sb("probs", [P, 2, SET, S])
        peak, nbias = sb("peak", [P, 2, SET]), sb("nbias", [P, 2, SET])
        total, rtotal = sb("total", [P, 2, SET]), sb("rtotal", [P, 2, SET])
        pT_h, pT_l = sb("pT_h", [P, 2, SET * P], F32R), sb("pT_l", [P, 2, SET * P], F32R)
        oT_h, oT_l = sb("oT_h", [P, 2, SET * P], F32R), sb("oT_l", [P, 2, SET * P], F32R)

        const_loaded, table_done, power_set = sem("const_loaded"), sem("table_done"), sem("power_set")
        w_loaded, wkv_hi, wkv_lo = sem("w_loaded"), sem("wkv_hi"), sem("wkv_lo")
        wset_hi, wset_lo = sem("wset_hi"), sem("wset_lo")
        kv_mm, v_hi, v_lo, k_sq, k_cos, k_sin, k_sum = (sem(n) for n in (
            "kv_mm", "v_hi", "v_lo", "k_sq", "k_cos", "k_sin", "k_sum"))
        k_var, k_rs, k_scaled, kT_mm, kT_hi, kT_lo = (sem(n) for n in (
            "k_var", "k_rs", "k_scaled", "kT_mm", "kT_hi", "kT_lo"))
        q_mm, q_sq, q_rope, q_sum, q_var, q_rs, qT_mm, qT_hi, qT_lo = (sem(n) for n in (
            "q_mm", "q_sq", "q_rope", "q_sum", "q_var", "q_rs", "qT_mm", "qT_hi", "qT_lo"))
        score_mm, peak_done, nbias_done, exp_done, rtotal_done, prob_done = (sem(n) for n in (
            "score_mm", "peak_done", "nbias_done", "exp_done", "rtotal_done", "prob_done"))
        pT_mm, pT_hi, pT_lo, pv_mm, oT_hi, oT_lo, wo_mm, y_done = (sem(n) for n in (
            "pT_mm", "pT_hi", "pT_lo", "pv_mm", "oT_hi", "oT_lo", "wo_mm", "y_done"))
        norm = Norm(nc, ctx, "an", x_tok, xT_h, xT_l, ident, (ps[:, 5, :], ps[:, 6, :]))

        krot = probs[:, 0, 0:2, :].rearrange("p a (t n) -> p a t n", t=NT)
        ksum = probs[:, 1, 0, :].rearrange("p (t n) -> p t n", t=NT)
        ksquare = probs[:, 1, 1, :].rearrange("p (t n) -> p t n", t=NT)
        wq_h = wset_h[:, :, 0, :].rearrange("p s (k n) -> p s k n", k=KD)
        wq_l = wset_l[:, :, 0, :].rearrange("p s (k n) -> p s k n", k=KD)
        wo_h = wset_h[:, :, 1, :].rearrange("p s (h n) -> p s h n", h=SET)
        wo_l = wset_l[:, :, 1, :].rearrange("p s (h n) -> p s h n", h=SET)

        def tile_of(s):
            return s % NT

        first_unit = [0]
        for s in range(STEPS):
            first_unit.append(first_unit[-1] + tile_of(s) + 1)
        UNITS = first_unit[STEPS]

        def part(s, j):
            n = tile_of(s) + 1
            return range(n * j // SET, n * (j + 1) // SET)

        def arrivals(s, j):
            n = tile_of(s) + 1
            out = []
            for kt in part(s, j):
                out += ([0] if kt == 0 else []) + ([kt + 1] if kt + 1 < n else [])
            return out

        def swapped(out, in0, table, dve):
            h = HD // 2
            dve.tensor_tensor(out[:, :, 0:h], in0[:, :, h:HD], table[:, :, 0:h], ALU.mult)
            return dve.tensor_tensor(out[:, :, h:HD], in0[:, :, 0:h], table[:, :, h:HD], ALU.mult)

        block = ctx.enter_context(nc.Block())

        @block.sync
        def _(sp):
            for name, dst in (("c_cos", cosw), ("c_sin", sinw)):
                for j in range(2):
                    sp.dma_start(dst[:, j, :, :], d[name].rearrange("(t p) n -> p t n", p=P)).then_inc(const_loaded, 16)
            sp.dma_start(normw[:], d["a_normw"].broadcast_to([P, 2, HD])).then_inc(const_loaded, 16)

            def load(g):
                sp.dma_start(wkv[:], d["a_wkv"][g].rearrange("p (k n) -> p k n", k=KD)).then_inc(w_loaded, 16)
                for s in range(SETS_PER_KV):
                    sp.dma_start(wset[:, s, :, :], d["a_wset"][g, s].rearrange("p (a n) -> p a n", a=2))\
                      .then_inc(w_loaded, 16)

            load(0)
            with sp.Fori(1, NKV) as g:
                sp.wait_ge(wset_lo, 4 * g)
                load(g)

        @block.gpsimd
        def _(pool):
            pool.memset(power[:], -0.5).then_inc(power_set, 1)
            pool.wait_ge(power_set, 1)


            def wait(signal, count):
                count = pool.to_reg(count)
                pool.wait_ge(power_set, 1)
                pool.wait_ge(signal, count)

            with pool.Fori(0, NKV) as g:
                wait(w_loaded, 16 * 3 * g + 48)
                pool.tensor_scalar(wkv_h[:], wkv[:], 1.0, None, ALU.mult).then_inc(wkv_hi, 1)

                def split_set(s):
                    for a in range(2):
                        pool.tensor_scalar(wset_h[:, s, a, :], wset[:, s, a, :], 1.0, None, ALU.mult)\
                            .then_inc(wset_hi, 1)

                split_set(0)
                split_set(1)
                wait(k_sq, g * NT + NT)
                pool.tensor_scalar(kvar[:], kss[:], 1.0 / HD, RMS_EPS, ALU.mult, ALU.add).then_inc(k_var, 1)
                wait(k_var, g + 1)
                pool.tensor_tensor(krs[:], kvar[:], power[:], ALU.pow).then_inc(k_rs, 1)

                def query_scale(s):
                    wait(q_sq, g * STEPS * SET + SET * s + SET)
                    pool.tensor_scalar(qvar[:, s % 2, :], qss[:, s % 2, :], HD * RMS_EPS, None, ALU.add)\
                        .then_inc(q_var, 1)
                    wait(q_rope, g * STEPS + s + 1)
                    pool.tensor_tensor(qsum[:], qrot[:, 0, :], qrot[:, 1, :], ALU.add).then_inc(q_sum, 1)
                    wait(q_var, g * STEPS + s + 1)
                    pool.tensor_tensor(qrs[:, s % 2, :], qvar[:, s % 2, :], power[:, 0:SET], ALU.pow)\
                        .then_inc(q_rs, 1)

                query_scale(0)
                for s in range(STEPS):
                    if s + 1 < STEPS:
                        wait(qT_mm, g * STEPS + s + 1)
                        query_scale(s + 1)
                    L = (tile_of(s) + 1) * P
                    for h in range(SET):
                        wait(rtotal_done, g * STEPS * SET + SET * s + h + 1)
                        pool.tensor_scalar(probs[:, s % 2, h, 0:L], probs[:, s % 2, h, 0:L],
                                           rtotal[:, s % 2, h:h + 1], None, ALU.mult).then_inc(prob_done, 1)
                wait(y_done, g * STEPS + STEPS)
            norm.pool(pool)

        @block.scalar
        def _(act):
            with act.Fori(0, NKV) as g:
                for p in range(NT // 2):
                    act.wait_ge(kv_mm, g * (NT // 2) + p + 1)
                    pair = ps[:, 5 + p % 2, :].rearrange("p (t n) -> p t n", t=2)
                    for j in range(2):
                        act.activation(ksquare[:, 2 * p + j, :], pair[:, j, 0:HD], ACT.Square,
                                       accum_out=kss[:, 2 * p + j:2 * p + j + 1]).then_inc(k_sq, 1)
                    act.activation(v_h[:, 2 * p:2 * p + 2, :], pair[:, :, HD:2 * HD], ACT.Copy).then_inc(v_hi, 1)

                def squares(s):
                    act.wait_ge(q_mm, g * STEPS + s + 1)
                    if s >= 2:
                        act.wait_ge(q_var, g * STEPS + s - 1)
                    for h in range(SET):
                        act.activation(square[:, s % 2, h, :], ps[:, 4, h * HD:(h + 1) * HD], ACT.Square,
                                       accum_out=qss[:, s % 2, h:h + 1]).then_inc(q_sq, 1)

                def query_high(s):
                    act.wait_ge(qT_mm, g * STEPS + s + 1)
                    if s >= 2:
                        act.wait_ge(score_mm, g * STEPS * SET + SET * (s - 1))
                    act.activation(qT_h[:, s % 2, :], ps[:, 4, :], ACT.Copy).then_inc(qT_hi, 1)

                def exp(s, h):
                    L = (tile_of(s) + 1) * P
                    act.wait_ge(nbias_done, g * STEPS * SET + SET * s + h + 1)
                    if s >= 2 and h == 0:
                        act.wait_ge(pT_mm, g * UNITS + first_unit[s - 1])
                    if L <= HALF:
                        src = ps[:, 2 * (h % 2), 0:L]
                    else:
                        src = ps[:, 2 * (h % 2):2 * (h % 2) + 2, :].rearrange("p a n -> p (a n)")[:, 0:L]
                    act.activation(probs[:, s % 2, h, 0:L], src, ACT.Exp, bias=nbias[:, s % 2, h:h + 1],
                                   scale=qrs[:, s % 2, h:h + 1], accum_out=total[:, s % 2, h:h + 1])\
                       .then_inc(exp_done, 1)

                def prob_high(s, j):
                    for kt in arrivals(s, j):
                        u = first_unit[s] + kt
                        act.wait_ge(pT_mm, g * UNITS + u + 1)
                        if u >= 2:
                            act.wait_ge(pv_mm, g * UNITS + u - 1)
                        act.activation(pT_h[:, u % 2, :], ps[:, 5 + u % 2, :], ACT.Copy).then_inc(pT_hi, 1)

                squares(0)
                for m in range(2):
                    act.wait_ge(kT_mm, 2 * g + m + 1)
                    act.activation(kT_h[:, m * HALF:(m + 1) * HALF], ps[:, 5 + m, :], ACT.Copy).then_inc(kT_hi, 1)
                query_high(0)
                for s in range(STEPS + 1):
                    for h in range(SET):
                        if s < STEPS:
                            exp(s, h)
                        if s >= 1:
                            prob_high(s - 1, h)
                        if h == 0 and s + 1 < STEPS:
                            squares(s + 1)
                        if h == 2 and s + 1 < STEPS:
                            query_high(s + 1)
                    if s >= 1:
                        act.wait_ge(pv_mm, g * UNITS + first_unit[s])
                        if s >= 3:
                            act.wait_ge(wo_mm, g * STEPS + s - 2)
                        act.activation(oT_h[:, (s - 1) % 2, :], ps[:, 7, :], ACT.Copy).then_inc(oT_hi, 1)
                act.wait_ge(y_done, g * STEPS + STEPS)
            norm.scalar_hi(act)

        @block.vector
        def _(dve):
            dve.wait_ge(const_loaded, 16 * 5)
            h = HD // 2
            for j in range(2):
                for t in range(NT):
                    dve.tensor_tensor(cosw[:, j, t, :], cosw[:, j, t, :], normw[:, j, :], ALU.mult)\
                       .then_inc(table_done, 1)
                    dve.tensor_tensor(sinw[:, j, t, 0:h], sinw[:, j, t, 0:h], normw[:, j, h:HD], ALU.mult)
                    dve.tensor_tensor(sinw[:, j, t, h:HD], sinw[:, j, t, h:HD], normw[:, j, 0:h], ALU.mult)\
                       .then_inc(table_done, 1)
            dve.wait_ge(table_done, 4 * NT)
            with dve.Fori(0, NKV) as g:
                dve.wait_ge(wkv_hi, g + 1)
                dve.tensor_tensor(wkv_l[:], wkv[:], wkv_h[:].bitcast(F32), ALU.subtract).then_inc(wkv_lo, 1)

                def split_set(s):
                    for a in range(2):
                        dve.wait_ge(wset_hi, 4 * g + 2 * s + a + 1)
                        dve.tensor_tensor(wset_l[:, s, a, :], wset[:, s, a, :], wset_h[:, s, a, :].bitcast(F32),
                                          ALU.subtract).then_inc(wset_lo, 1)

                for p in range(NT // 2):
                    dve.wait_ge(v_hi, g * (NT // 2) + p + 1)
                    pair = ps[:, 5 + p % 2, :].rearrange("p (t n) -> p t n", t=2)
                    two = slice(2 * p, 2 * p + 2)
                    dve.tensor_tensor(krot[:, 0, two, :], pair[:, :, 0:HD], cosw[:, 1, two, :], ALU.mult)\
                       .then_inc(k_cos, 1)
                    swapped(krot[:, 1, two, :], pair[:, :, 0:HD], sinw[:, 1, two, :], dve).then_inc(k_sin, 1)
                    dve.tensor_tensor(v_l[:, two, :], pair[:, :, HD:2 * HD], v_h[:, two, :].bitcast(F32),
                                      ALU.subtract).then_inc(v_lo, 1)
                dve.wait_ge(k_sin, g * (NT // 2) + NT // 2)
                dve.wait_ge(k_cos, g * (NT // 2) + NT // 2)
                dve.tensor_tensor(ksum, krot[:, 0, :, :], krot[:, 1, :, :], ALU.add).then_inc(k_sum, 1)
                split_set(0)
                dve.wait_ge(k_sum, g + 1)
                dve.wait_ge(k_rs, g + 1)
                for t in range(NT):
                    dve.tensor_scalar(ksum[:, t, :], ksum[:, t, :], krs[:, t:t + 1], None, ALU.mult)\
                       .then_inc(k_scaled, 1)

                def rope(s):
                    dve.wait_ge(q_sq, g * STEPS * SET + SET * s + SET)
                    if s >= 1:
                        dve.wait_ge(q_sum, g * STEPS + s)
                    q = ps[:, 4, :].rearrange("p (h n) -> p h n", h=SET)
                    t = tile_of(s)
                    out = qrot[:].rearrange("p a (h n) -> p a h n", h=SET)
                    dve.tensor_tensor(out[:, 0, :, :], q,
                                      cosw[:, 0, t:t + 1, :].broadcast_to([P, SET, HD]), ALU.mult)
                    swapped(out[:, 1, :, :], q, sinw[:, 0, t:t + 1, :].broadcast_to([P, SET, HD]), dve)\
                        .then_inc(q_rope, 1)

                def query_low(s):
                    dve.wait_ge(qT_hi, g * STEPS + s + 1)
                    dve.tensor_tensor(qT_l[:, s % 2, :], ps[:, 4, :], qT_h[:, s % 2, :].bitcast(F32),
                                      ALU.subtract).then_inc(qT_lo, 1)

                def row_max(s, hh):
                    L = (tile_of(s) + 1) * P
                    n = g * STEPS * SET + SET * s + hh
                    dve.wait_ge(score_mm, n + 1)
                    if L <= HALF:
                        src = ps[:, 2 * (hh % 2), 0:L]
                    else:
                        src = ps[:, 2 * (hh % 2):2 * (hh % 2) + 2, :].rearrange("p a n -> p (a n)")[:, 0:L]
                    dve.tensor_reduce(peak[:, s % 2, hh:hh + 1], src, AX.X, ALU.max).then_inc(peak_done, 1)
                    if hh == 0:
                        dve.wait_ge(q_rs, g * STEPS + s + 1)
                    dve.wait_ge(peak_done, n + 1)
                    dve.tensor_scalar(nbias[:, s % 2, hh:hh + 1], peak[:, s % 2, hh:hh + 1],
                                      qrs[:, s % 2, hh:hh + 1], -1.0, ALU.mult, ALU.mult).then_inc(nbias_done, 1)

                def row_total(s, hh):
                    dve.wait_ge(exp_done, g * STEPS * SET + SET * s + hh + 1)
                    dve.reciprocal(rtotal[:, s % 2, hh:hh + 1], total[:, s % 2, hh:hh + 1]).then_inc(rtotal_done, 1)

                def prob_low(s, j):
                    for kt in arrivals(s, j):
                        u = first_unit[s] + kt
                        dve.wait_ge(pT_hi, g * UNITS + u + 1)
                        dve.tensor_tensor(pT_l[:, u % 2, :], ps[:, 5 + u % 2, :], pT_h[:, u % 2, :].bitcast(F32),
                                          ALU.subtract).then_inc(pT_lo, 1)

                def add_output(s):
                    dve.wait_ge(wo_mm, g * STEPS + s + 1)
                    t = tile_of(s)
                    dve.tensor_tensor(x_tok[:, t, :], ps[:, 4, 0:D], x_tok[:, t, :], ALU.add).then_inc(y_done, 1)

                rope(0)
                for m in range(2):
                    dve.wait_ge(kT_hi, 2 * g + m + 1)
                    dve.tensor_tensor(kT_l[:, m * HALF:(m + 1) * HALF], ps[:, 5 + m, :],
                                      kT_h[:, m * HALF:(m + 1) * HALF].bitcast(F32), ALU.subtract).then_inc(kT_lo, 1)
                query_low(0)
                split_set(1)
                for s in range(STEPS + 2):
                    for hh in range(SET):
                        if s < STEPS:
                            row_max(s, hh)
                            if hh >= 1:
                                row_total(s, hh - 1)
                        if hh == 0 and s >= 2:
                            add_output(s - 2)
                        if 1 <= s <= STEPS:
                            prob_low(s - 1, hh)
                        if hh == 0 and s + 1 < STEPS:
                            rope(s + 1)
                        if hh == 2 and s + 1 < STEPS:
                            query_low(s + 1)
                    if s < STEPS:
                        row_total(s, SET - 1)
                    if 1 <= s <= STEPS:
                        dve.wait_ge(oT_hi, g * STEPS + s)
                        dve.tensor_tensor(oT_l[:, (s - 1) % 2, :], ps[:, 7, :],
                                          oT_h[:, (s - 1) % 2, :].bitcast(F32), ALU.subtract).then_inc(oT_lo, 1)
                dve.wait_ge(y_done, g * STEPS + STEPS)
            norm.dve_norm(dve, lambda t: None)
            norm.dve_lo(dve)

        @block.tensor
        def _(pe):
            with pe.Fori(0, NKV) as g:
                pe.wait_ge(wkv_lo, g + 1)
                for p in range(NT // 2):
                    if p >= 2:
                        pe.wait_ge(v_lo, g * (NT // 2) + p - 1)
                        pe.wait_ge(k_sq, g * NT + 2 * (p - 1))
                    for j in range(2):
                        t = 2 * p + j
                        for k in range(KD):
                            last = split_matmul(pe, ps[:, 5 + p % 2, j * 2 * HD:(j + 1) * 2 * HD],
                                                xT_h[:, k, t * P:(t + 1) * P], xT_l[:, k, t * P:(t + 1) * P],
                                                wkv_h[:, k, :], wkv_l[:, k, :], k == 0, k == KD - 1)
                    last.then_inc(kv_mm, 1)

                def project(s):
                    st, t = s // NT, tile_of(s)
                    if s % NT == 0:
                        pe.wait_ge(wset_lo, 4 * g + 2 * st + 2)
                    for k in range(KD):
                        last = split_matmul(pe, ps[:, 4, :], xT_h[:, k, t * P:(t + 1) * P],
                                            xT_l[:, k, t * P:(t + 1) * P], wq_h[:, st, k, :], wq_l[:, st, k, :],
                                            k == 0, k == KD - 1)
                    last.then_inc(q_mm, 1)

                def transpose_queries(s):
                    pe.wait_ge(q_sum, g * STEPS + s + 1)
                    pe.wait_ge(q_sq, g * STEPS * SET + SET * s + SET)
                    for h in range(SET):
                        last = pe.transpose(ps[:, 4, h * P:(h + 1) * P], qsum[:, h * HD:(h + 1) * HD], ident)
                    last.then_inc(qT_mm, 1)

                def scores(s, h):
                    n = SET * s + h
                    if n >= 2:
                        pe.wait_ge(exp_done, g * STEPS * SET + n - 1)
                    if h == 0:
                        pe.wait_ge(qT_lo, g * STEPS + s + 1)
                    L = (tile_of(s) + 1) * P
                    qh, ql = qT_h[:, s % 2, h * P:(h + 1) * P], qT_l[:, s % 2, h * P:(h + 1) * P]
                    for b in range((L + HALF - 1) // HALF):
                        w = min(HALF, L - b * HALF)
                        cols = slice(b * HALF, b * HALF + w)
                        out = ps[:, 2 * (h % 2) + b, 0:w]
                        diag = b * HALF + w == L
                        last = split_matmul(pe, out, qh, ql, kT_h[:, cols], kT_l[:, cols], True, True)
                        if diag:
                            last = pe.matmul(out[:, w - P:w], ident_r, mask_r, start=False, stop=True,
                                             skip_group_check=True)
                    last.then_inc(score_mm, 1)

                def transpose_probs(s, kt):
                    u = first_unit[s] + kt
                    if u >= 2:
                        pe.wait_ge(pT_lo, g * UNITS + u - 1)
                    if kt == 0:
                        pe.wait_ge(prob_done, g * STEPS * SET + SET * s + SET)
                    for h in range(SET):
                        last = pe.transpose(ps[:, 5 + u % 2, h * P:(h + 1) * P],
                                            probs[:, s % 2, h, kt * P:(kt + 1) * P], ident)
                    last.then_inc(pT_mm, 1)

                def values(s, j):
                    n = tile_of(s) + 1
                    for kt in part(s, j):
                        if kt == 0:
                            transpose_probs(s, 0)
                        if kt + 1 < n:
                            transpose_probs(s, kt + 1)
                        u = first_unit[s] + kt
                        pe.wait_ge(pT_lo, g * UNITS + u + 1)
                        if kt == 0 and s >= 1:
                            pe.wait_ge(oT_lo, g * STEPS + s)
                        split_matmul(pe, ps[:, 7, :], v_h[:, kt, :], v_l[:, kt, :], pT_h[:, u % 2, :],
                                     pT_l[:, u % 2, :], kt == 0, kt == n - 1).then_inc(pv_mm, 1)

                def output(s):
                    st = s // NT
                    pe.wait_ge(oT_lo, g * STEPS + s + 1)
                    for h in range(SET):
                        last = split_matmul(pe, ps[:, 4, 0:D], oT_h[:, s % 2, h * P:(h + 1) * P],
                                            oT_l[:, s % 2, h * P:(h + 1) * P], wo_h[:, st, h, :], wo_l[:, st, h, :],
                                            h == 0, h == SET - 1)
                    last.then_inc(wo_mm, 1)

                project(0)
                transpose_queries(0)
                for m in range(2):
                    pe.wait_ge(k_scaled, g * NT + 4 * m + 4)
                    pe.wait_ge(v_lo, g * (NT // 2) + NT // 2)
                    for j in range(4):
                        last = pe.transpose(ps[:, 5 + m, j * P:(j + 1) * P], ksum[:, 4 * m + j, :], ident)
                    last.then_inc(kT_mm, 1)
                pe.wait_ge(kT_lo, 2 * g + 2)
                for s in range(STEPS + 2):
                    for h in range(SET):
                        if s < STEPS:
                            scores(s, h)
                        if h == 0 and s >= 2:
                            if s < STEPS:
                                pe.wait_ge(qT_lo, g * STEPS + s + 1)
                            else:
                                pe.wait_ge(y_done, g * STEPS + s - 2)
                            output(s - 2)
                        if 1 <= s <= STEPS:
                            values(s - 1, h)
                        if h == 0 and s + 1 < STEPS:
                            if s >= 2:
                                pe.wait_ge(y_done, g * STEPS + s - 1)
                            project(s + 1)
                        if h == 2 and s + 1 < STEPS:
                            transpose_queries(s + 1)
                pe.wait_ge(y_done, g * STEPS + STEPS)
            norm.tensor(pe)


def moe_stage(nc, ps, x_tok, xT_h, xT_l, ident, masks, d, out):
    with ExitStack() as ctx:
        sb = lambda n, s, dt=F32: ctx.enter_context(nc.sbuf_tensor(f"m_{n}", s, dt))
        sem = lambda n: ctx.enter_context(nc.semaphore(f"m_{n}"))
        gate_w = sb("gate_w", [P, KD, NE])
        gate_b = sb("gate_b", [P, NE])
        xT = sb("xT", [P, KD, S])
        logit = sb("logit", [P, NT, NE + 4])
        best = sb("best", [P, NT, 8])
        marked = sb("marked", [P, NT, NE + 4])
        nbest = sb("nbest", [P, NT])
        coef = sb("coef", [P, NT, NE])
        esum, rsum = sb("esum", [P, NT]), sb("rsum", [P, NT])
        coefT = sb("coefT", [NE, S])
        b_down = sb("b_down", [NE, D])
        W = 3 * D
        raw = sb("raw", [P, 2, W + 2])
        b_gu = sb("b_gu", [P, 2, 2])
        w_h, w_l = sb("w_h", [P, 2, W], F32R), sb("w_l", [P, 2, W], F32R)
        gate = sb("gate", [P, 2, HALF])
        glu = sb("glu", [P, 2, HALF])
        up = sb("up", [P, 2, HALF])
        act_f = sb("act_f", [P, 2, HALF])
        act_h, act_l = sb("act_h", [P, 2, HALF], F32R), sb("act_l", [P, 2, HALF], F32R)

        loaded, w_loaded = sem("loaded"), [sem("w_loaded0"), sem("w_loaded1")]
        x_joined, logit_mm, logit_done, absent_set, best_done, slots_set = (sem(n) for n in (
            "x_joined", "logit_mm", "logit_done", "absent_set", "best_done", "slots_set"))
        marked_done, nbest_done, exp_done, sel_done, masked_done, esum_done, rsum_done, coef_done = (sem(n) for n in (
            "marked_done", "nbest_done", "exp_done", "sel_done", "masked_done", "esum_done", "rsum_done", "coef_done"))
        coefT_mm, coefT_done, bias_mm, bias_done = (sem(n) for n in ("coefT_mm", "coefT_done", "bias_mm", "bias_done"))
        w_hi, w_lo = sem("w_hi"), sem("w_lo")
        gu_mm, gate_done, glu_done, up_done, act_done, act_hi, act_lo = (sem(n) for n in (
            "gu_mm", "gate_done", "glu_done", "up_done", "act_done", "act_hi", "act_lo"))
        clip_done = sem("clip_done")
        down_mm, y_done, stored = sem("down_mm"), sem("y_done"), sem("stored")
        norm = Norm(nc, ctx, "mn", x_tok, None, None, ident, (None, None))
        TPH = HALF // P
        PER = 2 * NHALF
        block = ctx.enter_context(nc.Block())

        @block.sync
        def _(sp):
            sp.dma_start(gate_w[:], d["m_gate_w"].rearrange("(k p) n -> p k n", p=P)).then_inc(loaded, 16)
            sp.dma_start(gate_b[:], d["m_gate_b"].broadcast_to([P, NE])).then_inc(loaded, 16)
            sp.dma_start(b_down[:], d["m_b_down"]).then_inc(loaded, 16)
            for e in range(2):
                sp.dma_start(raw[:, e, :], d["m_w"][e]).then_inc(w_loaded[e], 16)
            with sp.Fori(1, NE // 2) as i:
                for j in range(2):
                    sp.wait_ge(w_lo, 2 * i + j - 1)
                    sp.dma_start(raw[:, j, :], d["m_w"][2 * i + j]).then_inc(w_loaded[j], 16)
            for t in range(NT):
                sp.wait_ge(norm.s_x, t + 1)
                sp.dma_start(out[t * P:(t + 1) * P, :], x_tok[:, t, :]).then_inc(stored, 16)
            sp.wait_ge(stored, 16 * NT)

        @block.gpsimd
        def _(pool):
            def wait(signal, count):
                count = pool.to_reg(count)
                pool.wait_ge(loaded, 16 * 3)
                pool.wait_ge(signal, count)

            def pair(i, first):
                for j in range(2):
                    wait(w_loaded[j], 16 * i + 16)
                    if not first:
                        wait(down_mm, PER * i + NHALF * j - NHALF)
                    pool.tensor_scalar(w_h[:, j, :], raw[:, j, 0:W], 1.0, None, ALU.mult).then_inc(w_hi, 1)
                    pool.tensor_scalar(b_gu[:, j, :], raw[:, j, W:W + 2], 1.0, None, ALU.mult)
                    wait(w_hi, 2 * i + j + 1)
                    pool.tensor_tensor(w_l[:, j, :], raw[:, j, 0:W], w_h[:, j, :].bitcast(F32), ALU.subtract)\
                        .then_inc(w_lo, 1)

            pair(0, True)
            with pool.Fori(1, NE // 2) as i:
                pair(i, False)
            norm.pool(pool)

        @block.scalar
        def _(act):
            for t in range(NT):
                act.wait_ge(nbest_done, 1)
                act.wait_ge(logit_done, NT)
                act.activation(coef[:, t, :], logit[:, t, 0:NE], ACT.Exp, bias=nbest[:, t:t + 1]).then_inc(exp_done, 1)
            for th in range(NHALF):
                act.wait_ge(coefT_mm, th + 1)
                act.activation(coefT[:, th * HALF:(th + 1) * HALF], ps[0:NE, 2 + th, :], ACT.Copy)\
                   .then_inc(coefT_done, 1)

            def units(i, first):
                for m in range(PER):
                    n = PER * i + m
                    act.wait_ge(gate_done, n + 1)
                    act.wait_ge(gu_mm, n + 1)
                    if not first or m >= 2:
                        act.wait_ge(act_done, n - 1)
                    act.activation(up[:, m % 2, :], ps[:, 2 * (m % 2) + 1, :], ACT.Identity,
                                   bias=b_gu[:, m // NHALF, 1:2])\
                       .then_inc(up_done, 1)
                    act.activation(glu[:, m % 2, :], gate[:, m % 2, :], ACT.Gelu_apprx_sigmoid).then_inc(glu_done, 1)
                    act.wait_ge(act_done, n + 1)
                    if not first or m >= 2:
                        act.wait_ge(down_mm, n - 1)
                    act.activation(act_h[:, m % 2, :], act_f[:, m % 2, :], ACT.Copy).then_inc(act_hi, 1)

            units(0, True)
            with act.Fori(1, NE // 2) as i:
                units(i, False)

        @block.vector
        def _(dve):
            dve.wait_ge(loaded, 16 * 3)
            dve.tensor_tensor(xT[:], xT_h[:].bitcast(F32), xT_l[:].bitcast(F32), ALU.add).then_inc(x_joined, 1)
            dve.memset(logit[:, :, NE:NE + 4], ABSENT).then_inc(absent_set, 1)
            for t in range(NT):
                dve.wait_ge(logit_mm, t + 1)
                dve.tensor_tensor(logit[:, t, 0:NE], ps[:, t % 2, 0:NE], gate_b[:], ALU.add).then_inc(logit_done, 1)
            dve.wait_ge(absent_set, 1)
            for t in range(NT):
                dve.wait_ge(logit_done, t + 1)
                dve.max(best[:, t, :], logit[:, t, 0:NE]).then_inc(best_done, 1)
            dve.wait_ge(best_done, NT)
            dve.memset(best[:, :, TOPK:8], ABSENT).then_inc(slots_set, 1)
            dve.tensor_scalar(nbest[:], best[:, :, 0], -1.0, None, ALU.mult).then_inc(nbest_done, 1)
            dve.wait_ge(slots_set, 1)
            for t in range(NT):
                dve.match_replace(marked[:, t, :], best[:, t, :], logit[:, t, :], -ABSENT).then_inc(marked_done, 1)
            dve.wait_ge(marked_done, NT)
            dve.tensor_tensor(marked[:, :, 0:NE], marked[:, :, 0:NE], logit[:, :, 0:NE], ALU.not_equal)\
               .then_inc(sel_done, 1)
            dve.wait_ge(sel_done, 1)
            dve.wait_ge(exp_done, NT)
            dve.tensor_tensor(coef[:], coef[:], marked[:, :, 0:NE], ALU.mult).then_inc(masked_done, 1)
            dve.wait_ge(masked_done, 1)
            dve.tensor_reduce(esum[:], coef[:], AX.X, ALU.add).then_inc(esum_done, 1)
            dve.wait_ge(esum_done, 1)
            dve.reciprocal(rsum[:], esum[:]).then_inc(rsum_done, 1)
            dve.wait_ge(rsum_done, 1)
            for t in range(NT):
                dve.tensor_scalar(coef[:, t, :], coef[:, t, :], rsum[:, t:t + 1], None, ALU.mult)\
                   .then_inc(coef_done, 1)
            for t in range(NT):
                dve.wait_ge(bias_mm, t + 1)
                dve.tensor_tensor(x_tok[:, t, :], ps[:, 4 + t % 2, 0:D], x_tok[:, t, :], ALU.add)\
                   .then_inc(bias_done, 1)
            dve.wait_ge(bias_done, NT)

            def add_half(n, m, i, j):
                dve.wait_ge(down_mm, n + 1)
                th = m % 2
                for q in range(TPH):
                    t = th * TPH + q
                    e = 2 * i + j
                    c = coef[:, t, bass.ds(e, 1)] if not isinstance(e, int) else coef[:, t, e:e + 1]
                    last = dve.scalar_tensor_tensor(
                        out=x_tok[:, t, :], in0=ps[:, 4 + 2 * th + q // 2, (q % 2) * D:(q % 2 + 1) * D],
                        scalar=c, in1=x_tok[:, t, :], op0=ALU.mult, op1=ALU.add)
                last.then_inc(y_done, 1)

            def units(i, first):
                for m in range(PER):
                    n = PER * i + m
                    dve.wait_ge(gu_mm, n + 1)
                    if not first or m >= 2:
                        dve.wait_ge(glu_done, n - 1)
                    dve.tensor_scalar(gate[:, m % 2, :], ps[:, 2 * (m % 2), :], b_gu[:, m // NHALF, 0:1], LIMIT, ALU.add, ALU.min)\
                       .then_inc(gate_done, 1)
                    dve.wait_ge(up_done, n + 1)
                    dve.tensor_scalar(up[:, m % 2, :], up[:, m % 2, :], LIMIT, -LIMIT, ALU.min, ALU.max)\
                       .then_inc(clip_done, 1)
                    dve.wait_ge(clip_done, n + 1)
                    dve.wait_ge(glu_done, n + 1)
                    if not first or m >= 2:
                        dve.wait_ge(act_lo, n - 1)
                    dve.scalar_tensor_tensor(out=act_f[:, m % 2, :], in0=up[:, m % 2, :], scalar=1.0,
                                             in1=glu[:, m % 2, :], op0=ALU.add, op1=ALU.mult).then_inc(act_done, 1)
                    if not first or m >= 1:
                        pm = (m - 1) % PER
                        add_half(n - 1, pm, i if m >= 1 else i - 1, pm // NHALF)
                    dve.wait_ge(act_hi, n + 1)
                    dve.tensor_tensor(act_l[:, m % 2, :], act_f[:, m % 2, :], act_h[:, m % 2, :].bitcast(F32),
                                      ALU.subtract).then_inc(act_lo, 1)

            units(0, True)
            with dve.Fori(1, NE // 2) as i:
                units(i, False)
            add_half(NE * NHALF - 1, PER - 1, NE // 2 - 1, 1)
            dve.wait_ge(y_done, NE * NHALF)
            norm.dve_norm(dve, lambda t: None)

        @block.tensor
        def _(pe):
            pe.wait_ge(loaded, 16 * 3)
            pe.wait_ge(x_joined, 1)
            for t in range(NT):
                if t >= 2:
                    pe.wait_ge(logit_done, t - 1)
                for k in range(KD):
                    last = pe.matmul(ps[:, t % 2, 0:NE], xT[:, k, t * P:(t + 1) * P], gate_w[:, k, :],
                                     start=(k == 0), stop=(k == KD - 1))
                last.then_inc(logit_mm, 1)
            for th in range(NHALF):
                pe.wait_ge(coef_done, TPH * (th + 1))
                for q in range(TPH):
                    t = th * TPH + q
                    last = pe.transpose(ps[0:NE, 2 + th, q * P:(q + 1) * P], coef[:, t, :], ident)
                last.then_inc(coefT_mm, 1)
            pe.wait_ge(coefT_done, NHALF)
            for t in range(NT):
                if t >= 2:
                    pe.wait_ge(bias_done, t - 1)
                pe.matmul(ps[:, 4 + t % 2, 0:D], coefT[:, t * P:(t + 1) * P], b_down[:], start=True, stop=True)\
                  .then_inc(bias_mm, 1)
            pe.wait_ge(bias_done, NT)

            def gate_up(i, m, first):
                n = PER * i + m
                j, th = m // NHALF, m % NHALF
                if th == 0:
                    pe.wait_ge(w_lo, 2 * i + j + 1)
                if not first or m >= 2:
                    pe.wait_ge(up_done, n - 1)
                cols = slice(th * HALF, (th + 1) * HALF)
                for a in range(2):
                    for k in range(KD):
                        w = slice(a * D + k * NI, a * D + (k + 1) * NI)
                        last = split_matmul(pe, ps[:, 2 * (m % 2) + a, :], w_h[:, j, w], w_l[:, j, w],
                                            xT_h[:, k, cols], xT_l[:, k, cols], k == 0, k == KD - 1)
                last.then_inc(gu_mm, 1)

            def down(n, m, first):
                j, th = m // NHALF, m % NHALF
                pe.wait_ge(act_lo, n + 1)
                if not first:
                    pe.wait_ge(y_done, n - 1)
                for q in range(TPH):
                    last = split_matmul(pe, ps[:, 4 + 2 * th + q // 2, (q % 2) * D:(q % 2 + 1) * D],
                                        act_h[:, m % 2, q * P:(q + 1) * P], act_l[:, m % 2, q * P:(q + 1) * P],
                                        w_h[:, j, 2 * D:3 * D], w_l[:, j, 2 * D:3 * D], True, True)
                last.then_inc(down_mm, 1)

            def units(i, first):
                for m in range(PER):
                    gate_up(i, m, first)
                    if not first or m >= 1:
                        down(PER * i + m - 1, (m - 1) % PER, first and m < 3)

            units(0, True)
            with pe.Fori(1, NE // 2) as i:
                units(i, False)
            down(NE * NHALF - 1, PER - 1, False)


LAST_STAGE = 4


def build(nc, d, out):
    with ExitStack() as ctx:
        sb = lambda n, s, dt=F32: ctx.enter_context(nc.sbuf_tensor(n, s, dt))
        sem = lambda n: ctx.enter_context(nc.semaphore(n))
        ps = ctx.enter_context(nc.psum_tensor("ps", [P, 8, HALF], F32))
        x_tok = sb("x_tok", [P, NT, D])
        xT_h, xT_l = sb("xT_h", [P, KD, S], F32R), sb("xT_l", [P, KD, S], F32R)
        ident = sb("ident", [P, P])
        mask = sb("mask", [P, P])
        ident_r, mask_r = sb("ident_r", [P, P], F32R), sb("mask_r", [P, P], F32R)
        retention_stage(nc, ps, x_tok, xT_h, xT_l, ident[:], None, d)
        if LAST_STAGE >= 2:
            ffn_stage(nc, ps, x_tok, xT_h, xT_l, ident[:], None, d)
        mask_loaded, masks_set = sem("mask_loaded"), sem("masks_set")
        with nc.Block() as block:
            @block.sync
            def _(sp):
                sp.dma_start(mask[:], d["c_mask"]).then_inc(mask_loaded, 16)

            @block.vector
            def _(dve):
                dve.tensor_copy(ident_r[:], ident[:]).then_inc(masks_set, 1)
                dve.wait_ge(mask_loaded, 16)
                dve.tensor_copy(mask_r[:], mask[:]).then_inc(masks_set, 1)
                dve.wait_ge(masks_set, 2)
        if LAST_STAGE >= 3:
            attention_stage(nc, ps, x_tok, xT_h, xT_l, ident[:], (ident_r[:], mask_r[:]), d)
        if LAST_STAGE >= 4:
            moe_stage(nc, ps, x_tok, xT_h, xT_l, ident[:], None, d, out)
        else:
            stored = sem("stored")
            with nc.Block() as block:
                @block.sync
                def _(sp):
                    sp.dma_start(out.rearrange("(t p) n -> p t n", p=P), x_tok[:]).then_inc(stored, 16)
                    sp.wait_ge(stored, 16)


def constants():
    import numpy as np
    f = np.float32
    gamma = (1.0 - np.exp2(np.linspace(np.log2(1.0 / 32.0), np.log2(1.0 / 512.0), RH).astype(f))).astype(f)
    gamma = gamma.astype(np.float64)
    i = np.arange(P)
    decay = np.where(i[None, :] >= i[:, None], gamma[:, None, None] ** np.maximum(i[None, :] - i[:, None], 0), 0.0)
    head_of = np.arange(D) // RD
    c = {
        "c_decay": decay.reshape(2, 4, P, P).transpose(2, 1, 0, 3).astype(f),
        "c_qgain": (gamma[head_of][:, None] ** (i[None, :] + 1)).reshape(2, P, P).transpose(1, 0, 2).astype(f),
        "c_kgain": (gamma[head_of][None, :] ** (P - 1 - i[:, None])).astype(f),
        "c_blockdiag": np.tile((i[:, None] // RD == i[None, :] // RD).astype(f), (1, 2)),
        "c_chunkgain": (gamma[head_of] ** P).reshape(2, P).T.astype(f),
        "c_ident": np.eye(P, dtype=f),
        "c_mask": np.where(i[None, :] <= i[:, None], 0.0, MASKED).astype(f),
    }
    inv = (1.0 / (f(1000000.0) ** (np.arange(0, HD, 2).astype(f) / f(HD)))).astype(f)
    ang = (np.arange(S).astype(f)[:, None] * inv[None, :]).astype(f).astype(np.float64)
    c["c_cos"] = np.concatenate([np.cos(ang), np.cos(ang)], 1).astype(f)
    c["c_sin"] = np.concatenate([-np.sin(ang), np.sin(ang)], 1).astype(f)
    return {k: np.ascontiguousarray(v) for k, v in c.items()}


def kernel(**inputs):
    import numpy as np
    import concourse.bacc as bacc
    from concourse.bass_utils import run_bass_kernel_spmd

    a = {k: np.asarray(v) for k, v in inputs.items()}
    x = a["L0_attn_x"].reshape(S, D)
    bqk = np.concatenate([a["L0_attn_bq"], a["L0_attn_bk"]]).reshape(4, P).T
    wq = a["L1_attn_Wq"].reshape(KD, P, NKV, SETS_PER_KV, SET * HD).transpose(2, 3, 1, 0, 4)
    wo = a["L1_attn_Wo"].reshape(NKV, SETS_PER_KV, SET, HD, D).transpose(0, 1, 3, 2, 4)
    per_kv = lambda w: w.reshape(KD, P, NKV, HD).transpose(2, 1, 0, 3)
    per_expert = lambda w: w.reshape(NE, KD, P, NI).transpose(0, 2, 1, 3).reshape(NE, P, D)
    arrays = {
        "x": x, "xT": x.T,
        "r_wqk": np.concatenate([a["L0_attn_Wq"], a["L0_attn_Wk"]], 1),
        "r_wkv": np.concatenate([a["L0_attn_Wk"], a["L0_attn_Wv"]], 1),
        "r_bqk": bqk,
        "r_bkv": np.concatenate([a["L0_attn_bk"], a["L0_attn_bv"]]).reshape(1, 2 * D),
        "f_up_q": a["L0_ffn_w_up_q"].T, "f_up_scale": a["L0_ffn_w_up_scale"].T,
        "f_up_a": a["L0_ffn_w_up_lora_a"].T, "f_up_b": a["L0_ffn_w_up_lora_b"],
        "f_down_q": a["L0_ffn_w_down_q"].T, "f_down_scale": a["L0_ffn_w_down_scale"].T,
        "f_down_a": a["L0_ffn_w_down_lora_a"].T, "f_down_b": a["L0_ffn_w_down_lora_b"],
        "f_b_up": a["L0_ffn_b_up"].reshape(FT, P).T, "f_b_down": a["L0_ffn_b_down"].reshape(1, D),
        "a_wkv": np.concatenate([per_kv(a["L1_attn_Wk"]), per_kv(a["L1_attn_Wv"])], 3).reshape(NKV, P, KD * 2 * HD),
        "a_wset": np.concatenate([wq.reshape(NKV, SETS_PER_KV, P, -1), wo.reshape(NKV, SETS_PER_KV, P, -1)], 3),
        "a_normw": np.stack([a["L1_attn_q_norm_w"], a["L1_attn_k_norm_w"]]).reshape(1, 2, HD),
        "m_gate_w": a["L1_ffn_gate_w"].T, "m_gate_b": a["L1_ffn_gate_b"].reshape(1, NE),
        "m_w": np.concatenate([per_expert(a["L1_ffn_w_gate"]), per_expert(a["L1_ffn_w_up"]), a["L1_ffn_w_down"],
                               a["L1_ffn_b_gate"][:, :, None], a["L1_ffn_b_up"][:, :, None]], 2),
        "m_b_down": a["L1_ffn_b_down"],
        **constants(),
    }
    arrays = {f"in_{k}": np.ascontiguousarray(v) for k, v in arrays.items()}
    nc = bacc.Bacc("TRN2", target_bir_lowering=False, num_devices=1)
    d = {k[3:]: nc.dram_tensor(k, v.shape, mybir.dt.from_np(v.dtype), kind="ExternalInput").ap()
         for k, v in arrays.items()}
    out = nc.dram_tensor("out_x", (S, D), F32, kind="ExternalOutput").ap()
    build(nc, d, out)
    r = run_bass_kernel_spmd(nc, [arrays], core_ids=[0])
    return r.results[0]["out_x"].reshape(a["L0_attn_x"].shape)
```

```python
from contextlib import ExitStack

import concourse.bass as bass
from concourse import mybir

F32 = mybir.dt.float32
F32R = mybir.dt.float32r
I32 = mybir.dt.int32
ALU = mybir.AluOpType
ACT = mybir.ActivationFunctionType
AX = mybir.AxisListType

P = 128
S, D = 1024, 256
NT = S // P
KD = D // P
LN_EPS = 1e-5
RH, RD = 8, 32
FH = 1024
FT = FH // P
LORA = 16
QBLOCK = 64
NH, NKV, HD = 32, 4, 128
SET = 4
SETS_PER_KV = NH // NKV // SET
STEPS = SETS_PER_KV * NT
RMS_EPS = 1e-6
MASKED = -1e30
NE, NI = 32, 128
TOPK = 4
HALF = 512
NHALF = S // HALF
ALPHA, LIMIT = 1.702, 7.0
ABSENT = -3e38


def split_matmul(pe, out, w_h, w_l, x_h, x_l, start, stop, shared=False):
    pe.matmul(out, w_h, x_h, start=start, stop=False, skip_group_check=shared)
    pe.matmul(out, w_h, x_l, start=False, stop=False, skip_group_check=shared)
    return pe.matmul(out, w_l, x_h, start=False, stop=stop, skip_group_check=shared)


class Norm:

    def __init__(self, nc, ctx, tag, x_tok, xT_h, xT_l, ident, banks):
        sb = lambda n, s: ctx.enter_context(nc.sbuf_tensor(f"{tag}_{n}", s, F32))
        sem = lambda n: ctx.enter_context(nc.semaphore(f"{tag}_{n}"))
        self.stats, self.mv = sb("stats", [P, NT, 6]), sb("mv", [P, NT, 2])
        self.var, self.power, self.rstd = sb("var", [P, NT]), sb("power", [P, NT]), sb("rstd", [P, NT])
        self.x, self.xT_h, self.xT_l, self.ident, self.banks = x_tok, xT_h, xT_l, ident, banks
        self.s_stats, self.s_mv, self.s_rstd = sem("stats_done"), sem("mv_done"), sem("rstd_done")
        self.s_x, self.s_tr, self.s_hi, self.s_lo = sem("x_done"), sem("tr_done"), sem("hi_done"), sem("lo_done")

    def dve_norm(self, dve, ready):
        for t in range(NT):
            ready(t)
            dve.bn_stats(self.stats[:, t, :], self.x[:, t, :]).then_inc(self.s_stats, 1)
        for t in range(NT):
            dve.wait_ge(self.s_stats, t + 1)
            dve.bn_aggr(self.mv[:, t, :], self.stats[:, t, :]).then_inc(self.s_mv, 1)
        dve.wait_ge(self.s_rstd, 3)
        for t in range(NT):
            dve.tensor_scalar(self.x[:, t, :], self.x[:, t, :], self.mv[:, t, 0:1], self.rstd[:, t:t + 1],
                              ALU.subtract, ALU.mult).then_inc(self.s_x, 1)

    def pool(self, pool):
        pool.memset(self.power[:], -0.5).then_inc(self.s_rstd, 1)
        pool.wait_ge(self.s_mv, NT)
        pool.tensor_scalar(self.var[:], self.mv[:, :, 1], LN_EPS, None, ALU.add).then_inc(self.s_rstd, 1)
        pool.wait_ge(self.s_rstd, 2)
        pool.tensor_tensor(self.rstd[:], self.var[:], self.power[:], ALU.pow).then_inc(self.s_rstd, 1)

    def tensor(self, pe):
        for t in range(NT):
            pe.wait_ge(self.s_x, t + 1)
            if t >= 2:
                pe.wait_ge(self.s_lo, t - 1)
            for k in range(KD):
                last = pe.transpose(self.banks[t % 2][:, k * P:(k + 1) * P],
                                    self.x[:, t, k * P:(k + 1) * P], self.ident)
            last.then_inc(self.s_tr, 1)

    def bank(self, t):
        return self.banks[t % 2][:, 0:D].rearrange("p (k q) -> p k q", k=KD)

    def scalar_hi(self, act):
        for t in range(NT):
            act.wait_ge(self.s_tr, t + 1)
            act.activation(self.xT_h[:, :, t * P:(t + 1) * P], self.bank(t), ACT.Copy).then_inc(self.s_hi, 1)

    def dve_lo(self, dve):
        for t in range(NT):
            dve.wait_ge(self.s_hi, t + 1)
            dve.tensor_tensor(self.xT_l[:, :, t * P:(t + 1) * P], self.bank(t),
                              self.xT_h[:, :, t * P:(t + 1) * P].bitcast(F32), ALU.subtract).then_inc(self.s_lo, 1)


def retention_stage(nc, ps, x_tok, xT_h, xT_l, ident, masks, d):
    with ExitStack() as ctx:
        sb = lambda n, s, dt=F32: ctx.enter_context(nc.sbuf_tensor(f"r_{n}", s, dt))
        sem = lambda n: ctx.enter_context(nc.semaphore(f"r_{n}"))
        xT = sb("xT", [P, KD, S])
        wqk = sb("wqk", [P, KD, 2 * D])
        wkv = sb("wkv", [P, KD, 2 * D])
        bqk = sb("bqk", [P, 4])
        bkv = sb("bkv", [P, 2 * D])
        decay = sb("decay", [P, 4, 2, P])
        qgain = sb("qgain", [P, 2, P])
        kgain = sb("kgain", [P, D])
        blockdiag = sb("blockdiag", [P, D])
        chunk_gain = sb("chunk_gain", [P, 2])
        qkT = sb("qkT", [P, 4, S])
        qgT = sb("qgT", [P, 2, 2, P])
        kv = sb("kv", [P, 2, 2 * D])
        kg = sb("kg", [P, 2, D])
        aT = sb("aT", [P, 2, 4, 2, P])
        state = sb("state", [P, 2, P])
        fresh = sb("fresh", [P, D])

        loaded = sem("loaded")
        x_loaded = sem("x_loaded")
        qkT_mm, qkT_done = sem("qkT_mm"), sem("qkT_done")
        kv_mm, kv_done, kg_done = sem("kv_mm"), sem("kv_done"), sem("kg_done")
        qg_done, state_zero = sem("qg_done"), sem("state_zero")
        score_mm, aT_done = sem("score_mm"), sem("aT_done")
        out_mm, out_done = sem("out_mm"), sem("out_done")
        state_mm, fresh_done, state_done = sem("state_mm"), sem("fresh_done"), sem("state_done")
        norm = Norm(nc, ctx, "rn", x_tok, xT_h, xT_l, ident, (ps[:, 6, :], ps[:, 7, :]))
        N_LOADS = 11
        block = ctx.enter_context(nc.Block())

        @block.sync
        def _(sp):
            sp.dma_start(wqk[:], d["r_wqk"].rearrange("(k p) n -> p k n", p=P)).then_inc(loaded, 16)
            sp.dma_start(xT[:], d["xT"].rearrange("(k p) n -> p k n", p=P)).then_inc(loaded, 16)
            sp.dma_start(bqk[:], d["r_bqk"]).then_inc(loaded, 16)
            sp.dma_start(wkv[:], d["r_wkv"].rearrange("(k p) n -> p k n", p=P)).then_inc(loaded, 16)
            sp.dma_start(bkv[:], d["r_bkv"].broadcast_to([P, 2 * D])).then_inc(loaded, 16)
            sp.dma_start(decay[:], d["c_decay"]).then_inc(loaded, 16)
            sp.dma_start(qgain[:], d["c_qgain"]).then_inc(loaded, 16)
            sp.dma_start(kgain[:], d["c_kgain"]).then_inc(loaded, 16)
            sp.dma_start(blockdiag[:], d["c_blockdiag"]).then_inc(loaded, 16)
            sp.dma_start(chunk_gain[:], d["c_chunkgain"]).then_inc(loaded, 16)
            sp.dma_start(ident, d["c_ident"]).then_inc(loaded, 16)
            sp.dma_start(x_tok[:], d["x"].rearrange("(t p) n -> p t n", p=P)).then_inc(x_loaded, 16)

        @block.tensor
        def _(pe):
            pe.wait_ge(loaded, 16 * N_LOADS)
            for n in range(8):
                f, th = n // 2, n % 2
                if n >= 2:
                    pe.wait_ge(qkT_done, n - 1)
                for k in range(KD):
                    last = pe.matmul(ps[:, n % 2, :], wqk[:, k, f * P:(f + 1) * P],
                                     xT[:, k, th * HALF:(th + 1) * HALF], start=(k == 0), stop=(k == KD - 1))
                last.then_inc(qkT_mm, 1)

            def project(c):
                if c >= 2:
                    pe.wait_ge(kv_done, 2 * (c - 1))
                else:
                    pe.wait_ge(qkT_done, 7 + c)
                for k in range(KD):
                    last = pe.matmul(ps[:, c % 2, :], xT[:, k, c * P:(c + 1) * P], wkv[:, k, :],
                                     start=(k == 0), stop=(k == KD - 1))
                last.then_inc(kv_mm, 1)

            def scores(c):
                if c == 0:
                    pe.wait_ge(qkT_done, 8)
                else:
                    pe.wait_ge(aT_done, c)
                for h in range(RH):
                    r = slice(RD * (h % 4), RD * (h % 4) + RD)
                    last = pe.matmul(ps[:, 2 + h % 4, (h // 4) * P:(h // 4 + 1) * P],
                                     qkT[r, 2 + h // 4, c * P:(c + 1) * P], qkT[r, h // 4, c * P:(c + 1) * P],
                                     start=True, stop=True)
                last.then_inc(score_mm, 1)

            project(0)
            project(1)
            scores(0)
            for c in range(NT):
                pe.wait_ge(kg_done, c + 1)
                pe.wait_ge(kv_done, 2 * c + 2)
                if c >= 1:
                    pe.wait_ge(fresh_done, c)
                for g in range(2):
                    last = pe.matmul(ps[:, 7, g * P:(g + 1) * P], kg[:, c % 2, g * P:(g + 1) * P],
                                     kv[:, c % 2, D + g * P:D + (g + 1) * P], start=True, stop=True)
                last.then_inc(state_mm, 1)
                pe.wait_ge(qg_done, c + 1)
                pe.wait_ge(state_done, c + 1)
                pe.wait_ge(aT_done, c + 1)
                if c >= 1:
                    pe.wait_ge(out_done, c)
                for g in range(2):
                    pe.matmul(ps[:, 6, g * P:(g + 1) * P], qgT[:, c % 2, g, :], state[:, g, :],
                              start=(g == 0), stop=False, skip_group_check=True)
                for h in range(RH):
                    last = pe.matmul(ps[:, 6, h * RD:(h + 1) * RD], aT[:, c % 2, h % 4, h // 4, :],
                                     kv[:, c % 2, D + h * RD:D + (h + 1) * RD], start=False,
                                     stop=(h == RH - 1), skip_group_check=True)
                last.then_inc(out_mm, 1)
                if c + 1 < NT:
                    scores(c + 1)
                if c + 2 < NT:
                    project(c + 2)
            pe.wait_ge(out_done, NT)
            norm.tensor(pe)

        @block.scalar
        def _(act):
            act.wait_ge(loaded, 16 * N_LOADS)
            for n in range(8):
                f, th = n // 2, n % 2
                act.wait_ge(qkT_mm, n + 1)
                act.activation(qkT[:, f, th * HALF:(th + 1) * HALF], ps[:, n % 2, :], ACT.Identity,
                               bias=bqk[:, f:f + 1]).then_inc(qkT_done, 1)
            norm.scalar_hi(act)

        @block.gpsimd
        def _(pool):
            pool.memset(state[:], 0.0).then_inc(state_zero, 1)
            norm.pool(pool)

        @block.vector
        def _(dve):
            dve.wait_ge(loaded, 16 * N_LOADS)
            dve.wait_ge(state_zero, 1)
            dve.tensor_copy(state[:], state[:]).then_inc(state_done, 1)

            def keys_values(c):
                dve.wait_ge(kv_mm, c + 1)
                if c >= 2:
                    dve.wait_ge(out_mm, c - 1)
                for j in range(2):
                    dve.tensor_tensor(kv[:, c % 2, j * D:(j + 1) * D], ps[:, c % 2, j * D:(j + 1) * D],
                                      bkv[:, j * D:(j + 1) * D], ALU.add).then_inc(kv_done, 1)
                dve.wait_ge(kv_done, 2 * c + 1)
                dve.tensor_tensor(kg[:, c % 2, :], kv[:, c % 2, 0:D], kgain[:], ALU.mult).then_inc(kg_done, 1)
                if c == 0:
                    dve.wait_ge(qkT_done, 8)
                dve.tensor_tensor(qgT[:, c % 2, :, :], qkT[:, 0:2, c * P:(c + 1) * P], qgain[:], ALU.mult)\
                   .then_inc(qg_done, 1)

            keys_values(0)
            dve.wait_ge(x_loaded, 16)
            for c in range(NT):
                dve.wait_ge(score_mm, c + 1)
                dve.tensor_tensor(aT[:, c % 2, :, :, :].rearrange("p a b q -> p a (b q)"), ps[:, 2:6, 0:2 * P],
                                  decay[:].rearrange("p a b q -> p a (b q)"), ALU.mult).then_inc(aT_done, 1)
                if c + 1 < NT:
                    keys_values(c + 1)
                dve.wait_ge(state_mm, c + 1)
                dve.wait_ge(state_done, c + 1)
                dve.tensor_tensor(fresh[:], ps[:, 7, 0:D], blockdiag[:], ALU.mult).then_inc(fresh_done, 1)
                dve.wait_ge(out_mm, c + 1)
                dve.tensor_tensor(x_tok[:, c, :], ps[:, 6, 0:D], x_tok[:, c, :], ALU.add).then_inc(out_done, 1)
                dve.wait_ge(fresh_done, c + 1)
                for g in range(2):
                    last = dve.scalar_tensor_tensor(out=state[:, g, :], in0=state[:, g, :],
                                                    scalar=chunk_gain[:, g:g + 1],
                                                    in1=fresh[:, g * P:(g + 1) * P], op0=ALU.mult, op1=ALU.add)
                last.then_inc(state_done, 1)
            norm.dve_norm(dve, lambda t: dve.wait_ge(out_done, t + 1))
            norm.dve_lo(dve)


def ffn_stage(nc, ps, x_tok, xT_h, xT_l, ident, masks, d):
    with ExitStack() as ctx:
        sb = lambda n, s, dt=F32: ctx.enter_context(nc.sbuf_tensor(f"f_{n}", s, dt))
        sem = lambda n: ctx.enter_context(nc.semaphore(f"f_{n}"))
        quant = [sb("quant0", [P, KD, FH], I32), sb("quant1", [P, FT, D], I32)]
        scale = [sb("scale0", [P, KD, FH]), sb("scale1", [P, FT, D])]
        w = scale
        w_h = [sb("w0h", [P, KD, FH], F32R), sb("w1h", [P, FT, D], F32R)]
        w_l = [sb("w0l", [P, KD, FH], F32R), sb("w1l", [P, FT, D], F32R)]
        lora_a = [sb("lora_a0", [LORA, D]), sb("lora_a1", [LORA, FH])]
        lora_b = [sb("lora_b0", [LORA, FH]), sb("lora_b1", [LORA, D])]
        b_up = sb("b_up", [P, FT])
        b_down = sb("b_down", [P, D])
        hid = sb("hid", [P, 2, HALF])
        hid_h = sb("hid_h", [P, FT, HALF], F32R)
        hid_l = sb("hid_l", [P, FT, HALF], F32R)

        loaded = sem("loaded")
        lora_mm, w_scaled, w_full, w_hi, w_lo = (sem(n) for n in ("lora_mm", "w_scaled", "w_full", "w_hi", "w_lo"))
        up_mm, relu_done, hid_hi, hid_lo = (sem(n) for n in ("up_mm", "relu_done", "hid_hi", "hid_lo"))
        down_mm, res_done, sum_done = sem("down_mm"), sem("res_done"), sem("sum_done")
        norm = Norm(nc, ctx, "fn", x_tok, xT_h, xT_l, ident, (ps[:, 6, :], ps[:, 7, :]))
        def piece(n, a):
            if n < 4:
                return a[0][:, n // 2, (n % 2) * HALF:(n % 2 + 1) * HALF]
            return a[1][:, 2 * (n - 4):2 * (n - 3), :].rearrange("p a b -> p (a b)")
        N_LOADS = 2 * (1 + 2 + 2) + 2
        block = ctx.enter_context(nc.Block())

        @block.sync
        def _(sp):
            for j, (name, kt) in enumerate((("up", KD), ("down", FT))):
                sp.dma_start(quant[j][:], d[f"f_{name}_q"].rearrange("(k p) n -> p k n", p=P)).then_inc(loaded, 16)
                for b in range(P // QBLOCK):
                    src = d[f"f_{name}_scale"].rearrange("(k b o) n -> b o k n", b=P // QBLOCK, o=1)[b]
                    sp.dma_start(scale[j][QBLOCK * b:QBLOCK * (b + 1), :, :],
                                 src.broadcast_to([QBLOCK, kt, src.shape[2]])).then_inc(loaded, 16)
                sp.dma_start(lora_a[j][:], d[f"f_{name}_a"]).then_inc(loaded, 16)
                sp.dma_start(lora_b[j][:], d[f"f_{name}_b"]).then_inc(loaded, 16)
            sp.dma_start(b_up[:], d["f_b_up"]).then_inc(loaded, 16)
            sp.dma_start(b_down[:], d["f_b_down"].broadcast_to([P, D])).then_inc(loaded, 16)

        @block.tensor
        def _(pe):
            pe.wait_ge(loaded, 16 * N_LOADS)
            for n in range(8):
                if n >= 2:
                    pe.wait_ge(w_full, n - 1)
                if n < 4:
                    last = pe.matmul(ps[:, n % 2, :], lora_a[0][:, (n // 2) * P:(n // 2 + 1) * P],
                                     lora_b[0][:, (n % 2) * HALF:(n % 2 + 1) * HALF], start=True, stop=True)
                else:
                    for j in range(2):
                        row = 2 * (n - 4) + j
                        last = pe.matmul(ps[:, n % 2, j * D:(j + 1) * D], lora_a[1][:, row * P:(row + 1) * P],
                                         lora_b[1][:], start=True, stop=True)
                last.then_inc(lora_mm, 1)
            pe.wait_ge(w_lo, 8)
            for th in range(NHALF):
                for f in range(FT):
                    n = th * FT + f
                    if n >= 2:
                        pe.wait_ge(relu_done, n - 1)
                    for k in range(KD):
                        cols = slice(th * HALF, (th + 1) * HALF)
                        last = split_matmul(pe, ps[:, 2 + n % 2, :], w_h[0][:, k, f * P:(f + 1) * P],
                                            w_l[0][:, k, f * P:(f + 1) * P], xT_h[:, k, cols], xT_l[:, k, cols],
                                            k == 0, k == KD - 1)
                    last.then_inc(up_mm, 1)
                pe.wait_ge(hid_lo, (th + 1) * FT)
                for q in range(HALF // P):
                    n = th * (HALF // P) + q
                    if n >= 2:
                        pe.wait_ge(sum_done, n - 1)
                    for f in range(FT):
                        last = split_matmul(pe, ps[:, 4 + n % 2, 0:D], hid_h[:, f, q * P:(q + 1) * P],
                                            hid_l[:, f, q * P:(q + 1) * P], w_h[1][:, f, :], w_l[1][:, f, :],
                                            f == 0, f == FT - 1)
                    last.then_inc(down_mm, 1)
            norm.tensor(pe)

        @block.scalar
        def _(act):
            for n in range(NHALF * FT):
                act.wait_ge(relu_done, n + 1)
                if n >= FT:
                    act.wait_ge(down_mm, HALF // P)
                act.activation(hid_h[:, n % FT, :], hid[:, n % 2, :], ACT.Copy).then_inc(hid_hi, 1)
            norm.scalar_hi(act)

        @block.gpsimd
        def _(pool):
            for n in range(8):
                pool.wait_ge(w_full, n + 1)
                pool.tensor_copy(piece(n, w_h), piece(n, w)).then_inc(w_hi, 1)
            norm.pool(pool)

        @block.vector
        def _(dve):
            dve.wait_ge(loaded, 16 * N_LOADS)

            def low(n):
                dve.wait_ge(w_hi, n + 1)
                dve.tensor_tensor(piece(n, w_l), piece(n, w), piece(n, w_h).bitcast(F32), ALU.subtract)\
                   .then_inc(w_lo, 1)

            for n in range(8):
                dve.scalar_tensor_tensor(out=piece(n, w), in0=piece(n, quant), scalar=-7.5, in1=piece(n, scale),
                                         op0=ALU.add, op1=ALU.mult).then_inc(w_scaled, 1)
                dve.wait_ge(lora_mm, n + 1)
                dve.wait_ge(w_scaled, n + 1)
                dve.tensor_tensor(piece(n, w), ps[:, n % 2, :], piece(n, w), ALU.add).then_inc(w_full, 1)
                if n >= 2:
                    low(n - 2)
            low(6)
            low(7)
            for t in range(NT):
                dve.tensor_tensor(x_tok[:, t, :], x_tok[:, t, :], b_down[:], ALU.add).then_inc(res_done, 1)

            def hidden_low(n):
                dve.wait_ge(hid_hi, n + 1)
                dve.tensor_tensor(hid_l[:, n % FT, :], hid[:, n % 2, :], hid_h[:, n % FT, :].bitcast(F32),
                                  ALU.subtract).then_inc(hid_lo, 1)

            for th in range(NHALF):
                for f in range(FT):
                    n = th * FT + f
                    dve.wait_ge(up_mm, n + 1)
                    if n >= 2:
                        dve.wait_ge(hid_lo, n - 1)
                    dve.tensor_scalar(hid[:, n % 2, :], ps[:, 2 + n % 2, :], b_up[:, f:f + 1], 0.0,
                                      ALU.add, ALU.max).then_inc(relu_done, 1)
                    if f >= 1:
                        hidden_low(n - 1)
                hidden_low(th * FT + FT - 1)
                for q in range(HALF // P):
                    n = th * (HALF // P) + q
                    dve.wait_ge(down_mm, n + 1)
                    dve.wait_ge(res_done, NT)
                    dve.tensor_tensor(x_tok[:, n, :], ps[:, 4 + n % 2, 0:D], x_tok[:, n, :], ALU.add)\
                       .then_inc(sum_done, 1)
            norm.dve_norm(dve, lambda t: dve.wait_ge(sum_done, t + 1))
            norm.dve_lo(dve)


def attention_stage(nc, ps, x_tok, xT_h, xT_l, ident, masks, d):
    ident_r, mask_r = masks
    with ExitStack() as ctx:
        sb = lambda n, s, dt=F32: ctx.enter_context(nc.sbuf_tensor(f"a_{n}", s, dt))
        sem = lambda n: ctx.enter_context(nc.semaphore(f"a_{n}"))
        cosw = sb("cosw", [P, 2, NT, HD])
        sinw = sb("sinw", [P, 2, NT, HD])
        normw = sb("normw", [P, 2, HD])
        wkv = sb("wkv", [P, KD, 2 * HD])
        wkv_h, wkv_l = sb("wkv_h", [P, KD, 2 * HD], F32R), sb("wkv_l", [P, KD, 2 * HD], F32R)
        W = KD * SET * HD
        wset = sb("wset", [P, 2, 2, W])
        wset_h, wset_l = sb("wset_h", [P, 2, 2, W], F32R), sb("wset_l", [P, 2, 2, W], F32R)
        v_h, v_l = sb("v_h", [P, NT, HD], F32R), sb("v_l", [P, NT, HD], F32R)
        kT_h, kT_l = sb("kT_h", [P, S], F32R), sb("kT_l", [P, S], F32R)
        kss, kvar, krs, power = sb("kss", [P, NT]), sb("kvar", [P, NT]), sb("krs", [P, NT]), sb("power", [P, NT])
        square = sb("square", [P, 2, SET, HD])
        qrot = sb("qrot", [P, 2, SET * HD])
        qsum = sb("qsum", [P, SET * HD])
        qss, qvar, nqrs = sb("qss", [P, 2, SET]), sb("qvar", [P, 2, SET]), sb("nqrs", [P, 2, SET])
        qpow = sb("qpow", [P, SET])
        qT_h, qT_l = sb("qT_h", [P, 2, SET * P], F32R), sb("qT_l", [P, 2, SET * P], F32R)
        probs = sb("probs", [P, 2, SET, S])
        nbias = sb("nbias", [P, 2, SET])
        total, rtotal = sb("total", [P, 2, SET]), sb("rtotal", [P, 2, SET])
        pT = sb("pT", [P, 4, SET * P])
        pT_h, pT_l = sb("pT_h", [P, 4, SET * P], F32R), sb("pT_l", [P, 4, SET * P], F32R)
        recip = sb("recip", [P, SET * P])
        oT = sb("oT", [P, SET * P])
        oT_h, oT_l = sb("oT_h", [P, 2, SET * P], F32R), sb("oT_l", [P, 2, SET * P], F32R)

        const_loaded, table_done, power_set = sem("const_loaded"), sem("table_done"), sem("power_set")
        wkv_loaded, wkv_hi, wkv_lo = sem("wkv_loaded"), sem("wkv_hi"), sem("wkv_lo")
        wset_loaded, wset_hi, wset_lo = ([sem(f"wset{s}_{n}") for s in range(SETS_PER_KV)]
                                         for n in ("loaded", "hi", "lo"))
        kv_mm, v_hi, v_lo, k_sq, k_cos, k_sin, k_sum = (sem(n) for n in (
            "kv_mm", "v_hi", "v_lo", "k_sq", "k_cos", "k_sin", "k_sum"))
        k_var, k_rs, k_scaled, kT_mm, kT_hi, kT_lo = (sem(n) for n in (
            "k_var", "k_rs", "k_scaled", "kT_mm", "kT_hi", "kT_lo"))
        q_mm, q_sq, q_rope, q_sum, q_var, q_rs, qT_mm, qT_hi, qT_lo = (sem(n) for n in (
            "q_mm", "q_sq", "q_rope", "q_sum", "q_var", "q_rs", "qT_mm", "qT_hi", "qT_lo"))
        q_pow, pT_raw = sem("q_pow"), sem("pT_raw")
        score_mm, nbias_done, exp_done, rtotal_done = (sem(n) for n in (
            "score_mm", "nbias_done", "exp_done", "rtotal_done"))
        pT_mm, pT_hi, pT_lo, pv_mm, oT_hi, oT_lo, wo_mm, y_done = (sem(n) for n in (
            "pT_mm", "pT_hi", "pT_lo", "pv_mm", "oT_hi", "oT_lo", "wo_mm", "y_done"))
        recip_mm, recip_done, oT_raw, oT_done = (sem(n) for n in ("recip_mm", "recip_done", "oT_raw", "oT_done"))
        norm = Norm(nc, ctx, "an", x_tok, xT_h, xT_l, ident, (ps[:, 5, :], ps[:, 6, :]))

        krot = probs[:, 0, 0:2, :].rearrange("p a (t n) -> p a t n", t=NT)
        ksum = probs[:, 1, 0, :].rearrange("p (t n) -> p t n", t=NT)
        ksquare = probs[:, 1, 1, :].rearrange("p (t n) -> p t n", t=NT)
        wq_h = wset_h[:, :, 0, :].rearrange("p s (k n) -> p s k n", k=KD)
        wq_l = wset_l[:, :, 0, :].rearrange("p s (k n) -> p s k n", k=KD)
        wo_h = wset_h[:, :, 1, :].rearrange("p s (h n) -> p s h n", h=SET)
        wo_l = wset_l[:, :, 1, :].rearrange("p s (h n) -> p s h n", h=SET)

        ORDER = [t for pair in zip(range(NT // 2), range(NT - 1, NT // 2 - 1, -1)) for t in pair]
        AHEAD = 3
        FBUF = AHEAD + 1

        def tile_of(s):
            return ORDER[s % NT]

        first_unit = [0]
        for s in range(STEPS):
            first_unit.append(first_unit[-1] + tile_of(s) + 1)
        UNITS = first_unit[STEPS]

        def part(s, j):
            n = tile_of(s) + 1
            return range(n * j // SET, n * (j + 1) // SET)

        def arrivals(s, j):
            n = tile_of(s) + 1
            first = list(range(min(AHEAD, n))) if j == 0 else []
            return first + [kt + AHEAD for kt in part(s, j) if kt + AHEAD < n]

        turns = [("q", 0)]
        for slot in range(STEPS + 1):
            for j in range(SET):
                if j == SET - 1 and slot + 1 < STEPS:
                    turns.append(("q", slot + 1))
                if slot >= 1:
                    turns += [("p", slot - 1, kt) for kt in arrivals(slot - 1, j)]
            if slot >= 1:
                turns.append(("r", slot - 1))
        turn = {key: n for n, key in enumerate(turns)}

        def turn_bank(key):
            return ps[:, 5 + turn[key] % 2, :]

        def score_bank(s, h):
            L = (tile_of(s) + 1) * P
            if L <= HALF:
                return ps[:, 2 * (h % 2), 0:L]
            return ps[:, 2 * (h % 2):2 * (h % 2) + 2, :].rearrange("p a n -> p (a n)")[:, 0:L]

        def swapped(out, in0, table, dve):
            h = HD // 2
            dve.tensor_tensor(out[:, :, 0:h], in0[:, :, h:HD], table[:, :, 0:h], ALU.mult)
            return dve.tensor_tensor(out[:, :, h:HD], in0[:, :, 0:h], table[:, :, h:HD], ALU.mult)

        block = ctx.enter_context(nc.Block())


        @block.sync
        def _(sp):
            for name, dst in (("c_cos", cosw), ("c_sin", sinw)):
                for j in range(2):
                    sp.dma_start(dst[:, j, :, :], d[name].rearrange("(t p) n -> p t n", p=P)).then_inc(const_loaded, 16)
            sp.dma_start(normw[:], d["a_normw"].broadcast_to([P, 2, HD])).then_inc(const_loaded, 16)

            def load_kv(g):
                sp.dma_start(wkv[:], d["a_wkv"][g].rearrange("p (k n) -> p k n", k=KD)).then_inc(wkv_loaded, 16)

            def load_set(g, s):
                sp.dma_start(wset[:, s, :, :], d["a_wset"][g, s].rearrange("p (a n) -> p a n", a=2))\
                  .then_inc(wset_loaded[s], 16)

            load_kv(0)
            load_set(0, 0)
            load_set(0, 1)
            with sp.Fori(1, NKV) as g:
                sp.wait_ge(wkv_lo, g)
                load_kv(g)
                sp.wait_ge(wset_lo[0], 4 * g)
                load_set(g, 0)
                sp.wait_ge(wset_lo[1], 4 * g)
                load_set(g, 1)
            sp.wait_ge(wkv_lo, NKV)
            load_kv(0)
            sp.wait_ge(wset_lo[0], 4 * NKV)
            load_set(0, 0)

        @block.gpsimd
        def _(pool):
            pool.memset(power[:], -0.5).then_inc(power_set, 1)
            pool.wait_ge(power_set, 1)

            def wait(signal, count):
                count = pool.to_reg(count)
                pool.wait_ge(power_set, 1)
                pool.wait_ge(signal, count)

            def split_kv(g):
                wait(wkv_loaded, 16 * g + 16)
                pool.tensor_copy(wkv_h[:], wkv[:]).then_inc(wkv_hi, 1)
                wait(wkv_hi, g + 1)
                pool.tensor_tensor(wkv_l[:], wkv[:], wkv_h[:].bitcast(F32), ALU.subtract).then_inc(wkv_lo, 1)

            def split_set(g, s, n):
                at = (slice(None), s, n // 2, slice(n % 2 * W // 2, (n % 2 + 1) * W // 2))
                wait(wset_loaded[s], 16 * g + 16)
                pool.tensor_copy(wset_h[at], wset[at]).then_inc(wset_hi[s], 1)
                wait(wset_hi[s], 4 * g + n + 1)
                pool.tensor_tensor(wset_l[at], wset[at], wset_h[at].bitcast(F32), ALU.subtract)\
                    .then_inc(wset_lo[s], 1)

            split_kv(0)
            for n in range(4):
                split_set(0, 0, n)
            with pool.Fori(0, NKV) as g:
                wait(k_sq, g * NT + NT)
                pool.tensor_scalar(kvar[:], kss[:], 1.0 / HD, RMS_EPS, ALU.mult, ALU.add).then_inc(k_var, 1)
                wait(k_var, g + 1)
                pool.tensor_tensor(krs[:], kvar[:], power[:], ALU.pow).then_inc(k_rs, 1)

                def queries(s):
                    wait(q_sq, g * STEPS * SET + SET * s + SET)
                    pool.tensor_scalar(qvar[:, s % 2, :], qss[:, s % 2, :], HD * RMS_EPS, None, ALU.add)\
                        .then_inc(q_var, 1)
                    if s >= 1:
                        wait(qT_mm, g * STEPS + s)
                    wait(q_rope, g * STEPS + s + 1)
                    pool.tensor_tensor(qsum[:], qrot[:, 0, :], qrot[:, 1, :], ALU.add).then_inc(q_sum, 1)
                    wait(q_var, g * STEPS + s + 1)
                    pool.tensor_tensor(qpow[:], qvar[:, s % 2, :], power[:, 0:SET], ALU.pow).then_inc(q_pow, 1)
                    wait(q_pow, g * STEPS + s + 1)
                    pool.tensor_scalar(nqrs[:, s % 2, :], qpow[:], -1.0, None, ALU.mult).then_inc(q_rs, 1)

                def divide(s):
                    wait(oT_raw, g * STEPS + s + 1)
                    pool.tensor_tensor(oT[:], oT[:], recip[:], ALU.mult).then_inc(oT_done, 1)

                def output_high(s):
                    if s >= 2:
                        wait(wo_mm, g * STEPS + s - 1)
                    wait(oT_done, g * STEPS + s + 1)
                    pool.tensor_copy(oT_h[:, s % 2, :], oT[:]).then_inc(oT_hi, 1)

                def output_low(s):
                    wait(oT_hi, g * STEPS + s + 1)
                    pool.tensor_tensor(oT_l[:, s % 2, :], oT[:], oT_h[:, s % 2, :].bitcast(F32), ALU.subtract)\
                        .then_inc(oT_lo, 1)

                queries(0)
                for s in range(STEPS + 2):
                    divided = s >= 2
                    if divided:
                        divide(s - 2)
                    if s + 1 < STEPS:
                        queries(s + 1)
                    if divided:
                        output_high(s - 2)
                        output_low(s - 2)
                    if s < 4:
                        split_set(g, 1, s)
                    if s == NT + 3:
                        split_kv(g + 1)
                    if s >= NT + 4 and s < NT + 8:
                        wait(wo_mm, g * STEPS + NT)
                        split_set(g + 1, 0, s - NT - 4)
                wait(y_done, g * STEPS + STEPS)
            norm.pool(pool)

        @block.scalar
        def _(act):
            with act.Fori(0, NKV) as g:
                for p in range(NT // 2):
                    act.wait_ge(kv_mm, g * (NT // 2) + p + 1)
                    pair = ps[:, p, :].rearrange("p (t n) -> p t n", t=2)
                    for j in range(2):
                        act.activation(ksquare[:, 2 * p + j, :], pair[:, j, 0:HD], ACT.Square,
                                       accum_out=kss[:, 2 * p + j:2 * p + j + 1]).then_inc(k_sq, 1)
                    act.activation(v_h[:, 2 * p:2 * p + 2, :], pair[:, :, HD:2 * HD], ACT.Copy).then_inc(v_hi, 1)

                def squares(s):
                    act.wait_ge(q_mm, g * STEPS + s + 1)
                    if s >= 2:
                        act.wait_ge(q_var, g * STEPS + s - 1)
                    for h in range(SET):
                        act.activation(square[:, s % 2, h, :], ps[:, 4, h * HD:(h + 1) * HD], ACT.Square,
                                       accum_out=qss[:, s % 2, h:h + 1]).then_inc(q_sq, 1)

                def query_high(s):
                    act.wait_ge(qT_mm, g * STEPS + s + 1)
                    if s >= 2:
                        act.wait_ge(score_mm, g * STEPS * SET + SET * (s - 1))
                    act.activation(qT_h[:, s % 2, :], turn_bank(("q", s)), ACT.Copy).then_inc(qT_hi, 1)

                def exp(s, h):
                    L = (tile_of(s) + 1) * P
                    act.wait_ge(nbias_done, g * STEPS * SET + SET * s + h + 1)
                    if s >= 2 and h == 0:
                        act.wait_ge(pT_mm, g * UNITS + first_unit[s - 1])
                    act.activation(probs[:, s % 2, h, 0:L], score_bank(s, h), ACT.Exp, scale=-1.0,
                                   bias=nbias[:, s % 2, h:h + 1], accum_out=total[:, s % 2, h:h + 1])\
                       .then_inc(exp_done, 1)

                def prob_raw(s, j):
                    for kt in arrivals(s, j):
                        u = first_unit[s] + kt
                        act.wait_ge(pT_mm, g * UNITS + u + 1)
                        if u >= FBUF:
                            act.wait_ge(pv_mm, g * UNITS + u - FBUF + 1)
                        act.activation(pT_h[:, u % FBUF, :], turn_bank(("p", s, kt)), ACT.Copy)
                        act.activation(pT[:, u % FBUF, :], turn_bank(("p", s, kt)), ACT.Copy).then_inc(pT_raw, 1)

                squares(0)
                for m in range(2):
                    act.wait_ge(kT_mm, 2 * g + m + 1)
                    act.activation(kT_h[:, m * HALF:(m + 1) * HALF], ps[:, 6 + m, :], ACT.Copy).then_inc(kT_hi, 1)
                query_high(0)
                for s in range(STEPS + 1):
                    scored, values = s < STEPS, s >= 1
                    if scored:
                        exp(s, 0)
                    if values:
                        prob_raw(s - 1, 0)
                    if scored:
                        exp(s, 1)
                    if s + 1 < STEPS:
                        squares(s + 1)
                    if scored:
                        exp(s, 2)
                    if values:
                        prob_raw(s - 1, 1)
                    if scored:
                        exp(s, 3)
                    if values:
                        prob_raw(s - 1, 2)
                    if s + 1 < STEPS:
                        query_high(s + 1)
                    if values:
                        prob_raw(s - 1, 3)
                        act.wait_ge(recip_mm, g * STEPS + s)
                        if s >= 2:
                            act.wait_ge(oT_lo, g * STEPS + s - 1)
                        act.activation(recip[:], turn_bank(("r", s - 1)), ACT.Copy).then_inc(recip_done, 1)
                        act.wait_ge(pv_mm, g * UNITS + first_unit[s])
                        act.activation(oT[:], ps[:, 7, :], ACT.Copy).then_inc(oT_raw, 1)
                act.wait_ge(y_done, g * STEPS + STEPS)
            norm.scalar_hi(act)

        @block.vector
        def _(dve):
            dve.wait_ge(const_loaded, 16 * 5)
            h = HD // 2
            for j in range(2):
                for t in range(NT):
                    dve.tensor_tensor(cosw[:, j, t, :], cosw[:, j, t, :], normw[:, j, :], ALU.mult)\
                       .then_inc(table_done, 1)
                    dve.tensor_tensor(sinw[:, j, t, 0:h], sinw[:, j, t, 0:h], normw[:, j, h:HD], ALU.mult)
                    dve.tensor_tensor(sinw[:, j, t, h:HD], sinw[:, j, t, h:HD], normw[:, j, 0:h], ALU.mult)\
                       .then_inc(table_done, 1)

            dve.wait_ge(table_done, 4 * NT)
            with dve.Fori(0, NKV) as g:
                for p in range(NT // 2):
                    dve.wait_ge(v_hi, g * (NT // 2) + p + 1)
                    pair = ps[:, p, :].rearrange("p (t n) -> p t n", t=2)
                    two = slice(2 * p, 2 * p + 2)
                    dve.tensor_tensor(krot[:, 0, two, :], pair[:, :, 0:HD], cosw[:, 1, two, :], ALU.mult)\
                       .then_inc(k_cos, 1)
                    swapped(krot[:, 1, two, :], pair[:, :, 0:HD], sinw[:, 1, two, :], dve).then_inc(k_sin, 1)
                    dve.tensor_tensor(v_l[:, two, :], pair[:, :, HD:2 * HD], v_h[:, two, :].bitcast(F32),
                                      ALU.subtract).then_inc(v_lo, 1)
                dve.wait_ge(k_sin, g * (NT // 2) + NT // 2)
                dve.wait_ge(k_cos, g * (NT // 2) + NT // 2)
                dve.tensor_tensor(ksum, krot[:, 0, :, :], krot[:, 1, :, :], ALU.add).then_inc(k_sum, 1)
                dve.wait_ge(k_sum, g + 1)
                dve.wait_ge(k_rs, g + 1)
                for t in range(NT):
                    dve.tensor_scalar(ksum[:, t, :], ksum[:, t, :], krs[:, t:t + 1], None, ALU.mult)\
                       .then_inc(k_scaled, 1)

                def rope(s):
                    dve.wait_ge(q_sq, g * STEPS * SET + SET * s + SET)
                    if s >= 1:
                        dve.wait_ge(q_sum, g * STEPS + s)
                    q = ps[:, 4, :].rearrange("p (h n) -> p h n", h=SET)
                    t = tile_of(s)
                    out = qrot[:].rearrange("p a (h n) -> p a h n", h=SET)
                    dve.tensor_tensor(out[:, 0, :, :], q,
                                      cosw[:, 0, t:t + 1, :].broadcast_to([P, SET, HD]), ALU.mult)
                    swapped(out[:, 1, :, :], q, sinw[:, 0, t:t + 1, :].broadcast_to([P, SET, HD]), dve)\
                        .then_inc(q_rope, 1)

                def query_low(s):
                    dve.wait_ge(qT_hi, g * STEPS + s + 1)
                    dve.tensor_tensor(qT_l[:, s % 2, :], turn_bank(("q", s)), qT_h[:, s % 2, :].bitcast(F32),
                                      ALU.subtract).then_inc(qT_lo, 1)

                def scale_scores(s, hh):
                    dve.wait_ge(score_mm, g * STEPS * SET + SET * s + hh + 1)
                    if hh == 0:
                        dve.wait_ge(q_rs, g * STEPS + s + 1)
                    dve.tensor_scalar(score_bank(s, hh), score_bank(s, hh), nqrs[:, s % 2, hh:hh + 1], None,
                                      ALU.mult, ALU.min, accum_out=nbias[:, s % 2, hh:hh + 1]).then_inc(nbias_done, 1)

                def row_totals(s):
                    dve.wait_ge(exp_done, g * STEPS * SET + SET * s + SET)
                    dve.reciprocal(rtotal[:, s % 2, :], total[:, s % 2, :]).then_inc(rtotal_done, 1)

                def prob_low(s, j):
                    for kt in arrivals(s, j):
                        u = first_unit[s] + kt
                        dve.wait_ge(pT_raw, g * UNITS + u + 1)
                        dve.tensor_tensor(pT_l[:, u % FBUF, :], pT[:, u % FBUF, :],
                                          pT_h[:, u % FBUF, :].bitcast(F32), ALU.subtract).then_inc(pT_lo, 1)

                def add_output(s):
                    dve.wait_ge(wo_mm, g * STEPS + s + 1)
                    t = tile_of(s)
                    dve.tensor_tensor(x_tok[:, t, :], ps[:, 4, 0:D], x_tok[:, t, :], ALU.add).then_inc(y_done, 1)

                rope(0)
                for m in range(2):
                    dve.wait_ge(kT_hi, 2 * g + m + 1)
                    dve.tensor_tensor(kT_l[:, m * HALF:(m + 1) * HALF], ps[:, 6 + m, :],
                                      kT_h[:, m * HALF:(m + 1) * HALF].bitcast(F32), ALU.subtract).then_inc(kT_lo, 1)
                query_low(0)
                for s in range(STEPS + 3):
                    scored, values = s < STEPS, 1 <= s <= STEPS
                    if scored:
                        scale_scores(s, 0)
                        scale_scores(s, 1)
                    if values:
                        row_totals(s - 1)
                        prob_low(s - 1, 0)
                    if s + 1 < STEPS:
                        rope(s + 1)
                    if scored:
                        scale_scores(s, 2)
                    if values:
                        prob_low(s - 1, 1)
                    if scored:
                        scale_scores(s, 3)
                    if values:
                        prob_low(s - 1, 2)
                    if s >= 3:
                        add_output(s - 3)
                    if s + 1 < STEPS:
                        query_low(s + 1)
                    if values:
                        prob_low(s - 1, 3)
                dve.wait_ge(y_done, g * STEPS + STEPS)
            norm.dve_norm(dve, lambda t: None)
            norm.dve_lo(dve)

        @block.tensor
        def _(pe):
            with pe.Fori(0, NKV) as g:
                pe.wait_ge(wkv_lo, g + 1)
                for p in range(NT // 2):
                    for j in range(2):
                        t = 2 * p + j
                        for k in range(KD):
                            last = split_matmul(pe, ps[:, p, j * 2 * HD:(j + 1) * 2 * HD],
                                                xT_h[:, k, t * P:(t + 1) * P], xT_l[:, k, t * P:(t + 1) * P],
                                                wkv_h[:, k, :], wkv_l[:, k, :], k == 0, k == KD - 1)
                    last.then_inc(kv_mm, 1)

                def project(s):
                    st, t = s // NT, tile_of(s)
                    if s % NT == 0:
                        pe.wait_ge(wset_lo[st], 4 * g + 2)
                    if s >= 5:
                        pe.wait_ge(y_done, g * STEPS + s - 4)
                    elif s >= 1:
                        pe.wait_ge(q_rope, g * STEPS + s)
                    for k in range(KD):
                        last = split_matmul(pe, ps[:, 4, :], xT_h[:, k, t * P:(t + 1) * P],
                                            xT_l[:, k, t * P:(t + 1) * P], wq_h[:, st, k, :], wq_l[:, st, k, :],
                                            k == 0, k == KD - 1)
                    last.then_inc(q_mm, 1)

                def take_turn(key):
                    n = turn[key]
                    if n < 2:
                        return
                    before = turns[n - 2]
                    if before[0] == "q":
                        pe.wait_ge(qT_lo, g * STEPS + before[1] + 1)
                    elif before[0] == "p":
                        pe.wait_ge(pT_raw, g * UNITS + first_unit[before[1]] + before[2] + 1)
                    else:
                        pe.wait_ge(recip_done, g * STEPS + before[1] + 1)

                def transpose_queries(s):
                    take_turn(("q", s))
                    pe.wait_ge(q_sum, g * STEPS + s + 1)
                    for h in range(SET):
                        last = pe.transpose(turn_bank(("q", s))[:, h * P:(h + 1) * P], qsum[:, h * HD:(h + 1) * HD], ident)
                    last.then_inc(qT_mm, 1)

                def scores(s, h):
                    n = SET * s + h
                    if n >= 2:
                        pe.wait_ge(exp_done, g * STEPS * SET + n - 1)
                    if h == 0:
                        pe.wait_ge(qT_lo, g * STEPS + s + 1)
                    L = (tile_of(s) + 1) * P
                    qh, ql = qT_h[:, s % 2, h * P:(h + 1) * P], qT_l[:, s % 2, h * P:(h + 1) * P]
                    for b in range((L + HALF - 1) // HALF):
                        w = min(HALF, L - b * HALF)
                        cols = slice(b * HALF, b * HALF + w)
                        out = ps[:, 2 * (h % 2) + b, 0:w]
                        last = split_matmul(pe, out, qh, ql, kT_h[:, cols], kT_l[:, cols], True, True)
                        if b * HALF + w == L:
                            last = pe.matmul(out[:, w - P:w], ident_r, mask_r, start=False, stop=True,
                                             skip_group_check=True)
                    last.then_inc(score_mm, 1)

                def transpose_probs(s, kt):
                    take_turn(("p", s, kt))
                    if kt == 0:
                        pe.wait_ge(exp_done, g * STEPS * SET + SET * s + SET)
                    for h in range(SET):
                        last = pe.transpose(turn_bank(("p", s, kt))[:, h * P:(h + 1) * P],
                                            probs[:, s % 2, h, kt * P:(kt + 1) * P], ident)
                    last.then_inc(pT_mm, 1)

                def weigh_values(s, j):
                    n = tile_of(s) + 1
                    if j == 0:
                        for kt in range(min(AHEAD, n)):
                            transpose_probs(s, kt)
                    for kt in part(s, j):
                        if kt + AHEAD < n:
                            transpose_probs(s, kt + AHEAD)
                        u = first_unit[s] + kt
                        pe.wait_ge(pT_lo, g * UNITS + u + 1)
                        if kt == 0 and s >= 1:
                            pe.wait_ge(oT_raw, g * STEPS + s)
                        split_matmul(pe, ps[:, 7, :], v_h[:, kt, :], v_l[:, kt, :], pT_h[:, u % FBUF, :],
                                     pT_l[:, u % FBUF, :], kt == 0, kt == n - 1).then_inc(pv_mm, 1)

                def spread_recip(s):
                    take_turn(("r", s))
                    pe.wait_ge(rtotal_done, g * STEPS + s + 1)
                    for h in range(SET):
                        last = pe.transpose(turn_bank(("r", s))[:, h * P:(h + 1) * P],
                                            rtotal[:, s % 2, h:h + 1].broadcast_to([P, P]), ident)
                    last.then_inc(recip_mm, 1)

                def output(s):
                    st = s // NT
                    if s + 4 < STEPS:
                        pe.wait_ge(q_rope, g * STEPS + s + 5)
                    elif s >= 1:
                        pe.wait_ge(y_done, g * STEPS + s)
                    pe.wait_ge(wset_lo[st], 4 * g + 4)
                    pe.wait_ge(oT_lo, g * STEPS + s + 1)
                    for h in range(SET):
                        last = split_matmul(pe, ps[:, 4, 0:D], oT_h[:, s % 2, h * P:(h + 1) * P],
                                            oT_l[:, s % 2, h * P:(h + 1) * P], wo_h[:, st, h, :], wo_l[:, st, h, :],
                                            h == 0, h == SET - 1)
                    last.then_inc(wo_mm, 1)

                project(0)
                for m in range(2):
                    pe.wait_ge(k_scaled, g * NT + 4 * m + 4)
                    for j in range(4):
                        last = pe.transpose(ps[:, 6 + m, j * P:(j + 1) * P], ksum[:, 4 * m + j, :], ident)
                    last.then_inc(kT_mm, 1)
                transpose_queries(0)
                pe.wait_ge(v_lo, g * (NT // 2) + NT // 2)
                pe.wait_ge(kT_lo, 2 * g + 2)
                for s in range(STEPS + 3):
                    scored, values = s < STEPS, 1 <= s <= STEPS
                    if scored:
                        scores(s, 0)
                        scores(s, 1)
                    if s + 1 < STEPS:
                        project(s + 1)
                    if values:
                        weigh_values(s - 1, 0)
                    if scored:
                        scores(s, 2)
                    if values:
                        weigh_values(s - 1, 1)
                    if scored:
                        scores(s, 3)
                    if values:
                        weigh_values(s - 1, 2)
                    if s >= 3:
                        output(s - 3)
                    if s + 1 < STEPS:
                        transpose_queries(s + 1)
                    if values:
                        weigh_values(s - 1, 3)
                        spread_recip(s - 1)
                pe.wait_ge(y_done, g * STEPS + STEPS)
            norm.tensor(pe)


def moe_stage(nc, ps, x_tok, xT_h, xT_l, ident, masks, d, out):
    with ExitStack() as ctx:
        sb = lambda n, s, dt=F32: ctx.enter_context(nc.sbuf_tensor(f"m_{n}", s, dt))
        sem = lambda n: ctx.enter_context(nc.semaphore(f"m_{n}"))
        gate_w = sb("gate_w", [P, KD, NE])
        gate_b = sb("gate_b", [P, NE])
        xT = sb("xT", [P, KD, S])
        logit = sb("logit", [P, NT, NE + 4])
        best = sb("best", [P, NT, 8])
        marked = sb("marked", [P, NT, NE + 4])
        nbest = sb("nbest", [P, NT])
        coef = sb("coef", [P, NT, NE])
        esum, rsum = sb("esum", [P, NT]), sb("rsum", [P, NT])
        coefT = sb("coefT", [NE, S])
        b_down = sb("b_down", [NE, D])
        W = 3 * D
        raw = sb("raw", [P, 2, W + 2])
        b_gu = sb("b_gu", [P, 2, 2])
        w_h, w_l = sb("w_h", [P, 2, W], F32R), sb("w_l", [P, 2, W], F32R)
        gate = sb("gate", [P, 2, HALF])
        glu = sb("glu", [P, 2, HALF])
        up = sb("up", [P, 2, HALF])
        act_f = sb("act_f", [P, 2, HALF])
        act_h, act_l = sb("act_h", [P, 2, HALF], F32R), sb("act_l", [P, 2, HALF], F32R)

        loaded, w_loaded = sem("loaded"), [sem("w_loaded0"), sem("w_loaded1")]
        x_joined, logit_mm, logit_done, absent_set, best_done, slots_set = (sem(n) for n in (
            "x_joined", "logit_mm", "logit_done", "absent_set", "best_done", "slots_set"))
        marked_done, nbest_done, exp_done, sel_done, masked_done, esum_done, rsum_done, coef_done = (sem(n) for n in (
            "marked_done", "nbest_done", "exp_done", "sel_done", "masked_done", "esum_done", "rsum_done", "coef_done"))
        coefT_mm, coefT_done, bias_mm, bias_done = (sem(n) for n in ("coefT_mm", "coefT_done", "bias_mm", "bias_done"))
        w_hi, w_lo = sem("w_hi"), sem("w_lo")
        gu_mm, gate_done, glu_done, up_done, act_done, act_hi, act_lo = (sem(n) for n in (
            "gu_mm", "gate_done", "glu_done", "up_done", "act_done", "act_hi", "act_lo"))
        clip_done = sem("clip_done")
        down_mm, y_done, stored = sem("down_mm"), sem("y_done"), sem("stored")
        norm = Norm(nc, ctx, "mn", x_tok, None, None, ident, (None, None))
        TPH = HALF // P
        PER = 2 * NHALF
        block = ctx.enter_context(nc.Block())

        @block.sync
        def _(sp):
            sp.dma_start(gate_w[:], d["m_gate_w"].rearrange("(k p) n -> p k n", p=P)).then_inc(loaded, 16)
            sp.dma_start(gate_b[:], d["m_gate_b"].broadcast_to([P, NE])).then_inc(loaded, 16)
            sp.dma_start(b_down[:], d["m_b_down"]).then_inc(loaded, 16)
            for e in range(2):
                sp.dma_start(raw[:, e, :], d["m_w"][e]).then_inc(w_loaded[e], 16)
            with sp.Fori(1, NE // 2) as i:
                for j in range(2):
                    sp.wait_ge(w_lo, 2 * i + j - 1)
                    sp.dma_start(raw[:, j, :], d["m_w"][2 * i + j]).then_inc(w_loaded[j], 16)
            for t in range(NT):
                sp.wait_ge(norm.s_x, t + 1)
                sp.dma_start(out[t * P:(t + 1) * P, :], x_tok[:, t, :]).then_inc(stored, 16)
            sp.wait_ge(stored, 16 * NT)

        @block.gpsimd
        def _(pool):
            def wait(signal, count):
                count = pool.to_reg(count)
                pool.wait_ge(loaded, 16 * 3)
                pool.wait_ge(signal, count)

            def pair(i, first):
                for j in range(2):
                    wait(w_loaded[j], 16 * i + 16)
                    if not first:
                        wait(down_mm, PER * i + NHALF * j - NHALF)
                    pool.tensor_copy(w_h[:, j, :], raw[:, j, 0:W]).then_inc(w_hi, 1)
                    pool.tensor_copy(b_gu[:, j, :], raw[:, j, W:W + 2])
                    wait(w_hi, 2 * i + j + 1)
                    pool.tensor_tensor(w_l[:, j, :], raw[:, j, 0:W], w_h[:, j, :].bitcast(F32), ALU.subtract)\
                        .then_inc(w_lo, 1)

            pair(0, True)
            with pool.Fori(1, NE // 2) as i:
                pair(i, False)
            norm.pool(pool)

        @block.scalar
        def _(act):
            for t in range(NT):
                act.wait_ge(nbest_done, 1)
                act.wait_ge(logit_done, NT)
                act.activation(coef[:, t, :], logit[:, t, 0:NE], ACT.Exp, bias=nbest[:, t:t + 1]).then_inc(exp_done, 1)
            for th in range(NHALF):
                act.wait_ge(coefT_mm, th + 1)
                act.activation(coefT[:, th * HALF:(th + 1) * HALF], ps[0:NE, 2 + th, :], ACT.Copy)\
                   .then_inc(coefT_done, 1)

            def units(i, first):
                for m in range(PER):
                    n = PER * i + m
                    act.wait_ge(gate_done, n + 1)
                    act.wait_ge(gu_mm, n + 1)
                    if not first or m >= 2:
                        act.wait_ge(act_done, n - 1)
                    act.activation(up[:, m % 2, :], ps[:, 2 * (m % 2) + 1, :], ACT.Identity,
                                   bias=b_gu[:, m // NHALF, 1:2])\
                       .then_inc(up_done, 1)
                    act.activation(glu[:, m % 2, :], gate[:, m % 2, :], ACT.Gelu_apprx_sigmoid).then_inc(glu_done, 1)
                    act.wait_ge(act_done, n + 1)
                    if not first or m >= 2:
                        act.wait_ge(down_mm, n - 1)
                    act.activation(act_h[:, m % 2, :], act_f[:, m % 2, :], ACT.Copy).then_inc(act_hi, 1)

            units(0, True)
            with act.Fori(1, NE // 2) as i:
                units(i, False)

        @block.vector
        def _(dve):
            dve.wait_ge(loaded, 16 * 3)
            dve.tensor_tensor(xT[:], xT_h[:].bitcast(F32), xT_l[:].bitcast(F32), ALU.add).then_inc(x_joined, 1)
            dve.memset(logit[:, :, NE:NE + 4], ABSENT).then_inc(absent_set, 1)
            for t in range(NT):
                dve.wait_ge(logit_mm, t + 1)
                dve.tensor_tensor(logit[:, t, 0:NE], ps[:, t % 2, 0:NE], gate_b[:], ALU.add).then_inc(logit_done, 1)
            dve.wait_ge(absent_set, 1)
            for t in range(NT):
                dve.wait_ge(logit_done, t + 1)
                dve.max(best[:, t, :], logit[:, t, 0:NE]).then_inc(best_done, 1)
            dve.wait_ge(best_done, NT)
            dve.memset(best[:, :, TOPK:8], ABSENT).then_inc(slots_set, 1)
            dve.tensor_scalar(nbest[:], best[:, :, 0], -1.0, None, ALU.mult).then_inc(nbest_done, 1)
            dve.wait_ge(slots_set, 1)
            for t in range(NT):
                dve.match_replace(marked[:, t, :], best[:, t, :], logit[:, t, :], -ABSENT).then_inc(marked_done, 1)
            dve.wait_ge(marked_done, NT)
            dve.tensor_tensor(marked[:, :, 0:NE], marked[:, :, 0:NE], logit[:, :, 0:NE], ALU.not_equal)\
               .then_inc(sel_done, 1)
            dve.wait_ge(sel_done, 1)
            dve.wait_ge(exp_done, NT)
            dve.tensor_tensor(coef[:], coef[:], marked[:, :, 0:NE], ALU.mult).then_inc(masked_done, 1)
            dve.wait_ge(masked_done, 1)
            dve.tensor_reduce(esum[:], coef[:], AX.X, ALU.add).then_inc(esum_done, 1)
            dve.wait_ge(esum_done, 1)
            dve.reciprocal(rsum[:], esum[:]).then_inc(rsum_done, 1)
            dve.wait_ge(rsum_done, 1)
            for t in range(NT):
                dve.tensor_scalar(coef[:, t, :], coef[:, t, :], rsum[:, t:t + 1], None, ALU.mult)\
                   .then_inc(coef_done, 1)
            for t in range(NT):
                dve.wait_ge(bias_mm, t + 1)
                dve.tensor_tensor(x_tok[:, t, :], ps[:, 4 + t % 2, 0:D], x_tok[:, t, :], ALU.add)\
                   .then_inc(bias_done, 1)
            dve.wait_ge(bias_done, NT)

            def add_half(n, m, i, j):
                dve.wait_ge(down_mm, n + 1)
                th = m % 2
                for q in range(TPH):
                    t = th * TPH + q
                    e = 2 * i + j
                    c = coef[:, t, bass.ds(e, 1)] if not isinstance(e, int) else coef[:, t, e:e + 1]
                    last = dve.scalar_tensor_tensor(
                        out=x_tok[:, t, :], in0=ps[:, 4 + 2 * th + q // 2, (q % 2) * D:(q % 2 + 1) * D],
                        scalar=c, in1=x_tok[:, t, :], op0=ALU.mult, op1=ALU.add)
                last.then_inc(y_done, 1)

            def units(i, first):
                for m in range(PER):
                    n = PER * i + m
                    dve.wait_ge(gu_mm, n + 1)
                    if not first or m >= 2:
                        dve.wait_ge(glu_done, n - 1)
                    dve.tensor_scalar(gate[:, m % 2, :], ps[:, 2 * (m % 2), :], b_gu[:, m // NHALF, 0:1], LIMIT, ALU.add, ALU.min)\
                       .then_inc(gate_done, 1)
                    dve.wait_ge(up_done, n + 1)
                    dve.tensor_scalar(up[:, m % 2, :], up[:, m % 2, :], LIMIT, -LIMIT, ALU.min, ALU.max)\
                       .then_inc(clip_done, 1)
                    dve.wait_ge(clip_done, n + 1)
                    dve.wait_ge(glu_done, n + 1)
                    if not first or m >= 2:
                        dve.wait_ge(act_lo, n - 1)
                    dve.scalar_tensor_tensor(out=act_f[:, m % 2, :], in0=up[:, m % 2, :], scalar=1.0,
                                             in1=glu[:, m % 2, :], op0=ALU.add, op1=ALU.mult).then_inc(act_done, 1)
                    if not first or m >= 1:
                        pm = (m - 1) % PER
                        add_half(n - 1, pm, i if m >= 1 else i - 1, pm // NHALF)
                    dve.wait_ge(act_hi, n + 1)
                    dve.tensor_tensor(act_l[:, m % 2, :], act_f[:, m % 2, :], act_h[:, m % 2, :].bitcast(F32),
                                      ALU.subtract).then_inc(act_lo, 1)

            units(0, True)
            with dve.Fori(1, NE // 2) as i:
                units(i, False)
            add_half(NE * NHALF - 1, PER - 1, NE // 2 - 1, 1)
            dve.wait_ge(y_done, NE * NHALF)
            norm.dve_norm(dve, lambda t: None)

        @block.tensor
        def _(pe):
            pe.wait_ge(loaded, 16 * 3)
            pe.wait_ge(x_joined, 1)
            for t in range(NT):
                if t >= 2:
                    pe.wait_ge(logit_done, t - 1)
                for k in range(KD):
                    last = pe.matmul(ps[:, t % 2, 0:NE], xT[:, k, t * P:(t + 1) * P], gate_w[:, k, :],
                                     start=(k == 0), stop=(k == KD - 1))
                last.then_inc(logit_mm, 1)
            for th in range(NHALF):
                pe.wait_ge(coef_done, TPH * (th + 1))
                for q in range(TPH):
                    t = th * TPH + q
                    last = pe.transpose(ps[0:NE, 2 + th, q * P:(q + 1) * P], coef[:, t, :], ident)
                last.then_inc(coefT_mm, 1)
            pe.wait_ge(coefT_done, NHALF)
            for t in range(NT):
                if t >= 2:
                    pe.wait_ge(bias_done, t - 1)
                pe.matmul(ps[:, 4 + t % 2, 0:D], coefT[:, t * P:(t + 1) * P], b_down[:], start=True, stop=True)\
                  .then_inc(bias_mm, 1)
            pe.wait_ge(bias_done, NT)

            def gate_up(i, m, first):
                n = PER * i + m
                j, th = m // NHALF, m % NHALF
                if th == 0:
                    pe.wait_ge(w_lo, 2 * i + j + 1)
                if not first or m >= 2:
                    pe.wait_ge(up_done, n - 1)
                cols = slice(th * HALF, (th + 1) * HALF)
                for a in range(2):
                    for k in range(KD):
                        w = slice(a * D + k * NI, a * D + (k + 1) * NI)
                        last = split_matmul(pe, ps[:, 2 * (m % 2) + a, :], w_h[:, j, w], w_l[:, j, w],
                                            xT_h[:, k, cols], xT_l[:, k, cols], k == 0, k == KD - 1)
                last.then_inc(gu_mm, 1)

            def down(n, m, first):
                j, th = m // NHALF, m % NHALF
                pe.wait_ge(act_lo, n + 1)
                if not first:
                    pe.wait_ge(y_done, n - 1)
                for q in range(TPH):
                    last = split_matmul(pe, ps[:, 4 + 2 * th + q // 2, (q % 2) * D:(q % 2 + 1) * D],
                                        act_h[:, m % 2, q * P:(q + 1) * P], act_l[:, m % 2, q * P:(q + 1) * P],
                                        w_h[:, j, 2 * D:3 * D], w_l[:, j, 2 * D:3 * D], True, True)
                last.then_inc(down_mm, 1)

            def units(i, first):
                for m in range(PER):
                    gate_up(i, m, first)
                    if not first or m >= 1:
                        down(PER * i + m - 1, (m - 1) % PER, first and m < 3)

            units(0, True)
            with pe.Fori(1, NE // 2) as i:
                units(i, False)
            down(NE * NHALF - 1, PER - 1, False)


LAST_STAGE = 4


def build(nc, d, out):
    with ExitStack() as ctx:
        sb = lambda n, s, dt=F32: ctx.enter_context(nc.sbuf_tensor(n, s, dt))
        sem = lambda n: ctx.enter_context(nc.semaphore(n))
        ps = ctx.enter_context(nc.psum_tensor("ps", [P, 8, HALF], F32))
        x_tok = sb("x_tok", [P, NT, D])
        xT_h, xT_l = sb("xT_h", [P, KD, S], F32R), sb("xT_l", [P, KD, S], F32R)
        ident = sb("ident", [P, P])
        mask = sb("mask", [P, P])
        ident_r, mask_r = sb("ident_r", [P, P], F32R), sb("mask_r", [P, P], F32R)
        retention_stage(nc, ps, x_tok, xT_h, xT_l, ident[:], None, d)
        if LAST_STAGE >= 2:
            ffn_stage(nc, ps, x_tok, xT_h, xT_l, ident[:], None, d)
        mask_loaded, masks_set = sem("mask_loaded"), sem("masks_set")
        with nc.Block() as block:
            @block.sync
            def _(sp):
                sp.dma_start(mask[:], d["c_mask"]).then_inc(mask_loaded, 16)

            @block.vector
            def _(dve):
                dve.tensor_copy(ident_r[:], ident[:]).then_inc(masks_set, 1)
                dve.wait_ge(mask_loaded, 16)
                dve.tensor_copy(mask_r[:], mask[:]).then_inc(masks_set, 1)
                dve.wait_ge(masks_set, 2)
        if LAST_STAGE >= 3:
            attention_stage(nc, ps, x_tok, xT_h, xT_l, ident[:], (ident_r[:], mask_r[:]), d)
        if LAST_STAGE >= 4:
            moe_stage(nc, ps, x_tok, xT_h, xT_l, ident[:], None, d, out)
        else:
            stored = sem("stored")
            with nc.Block() as block:
                @block.sync
                def _(sp):
                    sp.dma_start(out.rearrange("(t p) n -> p t n", p=P), x_tok[:]).then_inc(stored, 16)
                    sp.wait_ge(stored, 16)


def constants():
    import numpy as np
    f = np.float32
    gamma = (1.0 - np.exp2(np.linspace(np.log2(1.0 / 32.0), np.log2(1.0 / 512.0), RH).astype(f))).astype(f)
    gamma = gamma.astype(np.float64)
    i = np.arange(P)
    decay = np.where(i[None, :] >= i[:, None], gamma[:, None, None] ** np.maximum(i[None, :] - i[:, None], 0), 0.0)
    head_of = np.arange(D) // RD
    c = {
        "c_decay": decay.reshape(2, 4, P, P).transpose(2, 1, 0, 3).astype(f),
        "c_qgain": (gamma[head_of][:, None] ** (i[None, :] + 1)).reshape(2, P, P).transpose(1, 0, 2).astype(f),
        "c_kgain": (gamma[head_of][None, :] ** (P - 1 - i[:, None])).astype(f),
        "c_blockdiag": np.tile((i[:, None] // RD == i[None, :] // RD).astype(f), (1, 2)),
        "c_chunkgain": (gamma[head_of] ** P).reshape(2, P).T.astype(f),
        "c_ident": np.eye(P, dtype=f),
        "c_mask": np.where(i[None, :] <= i[:, None], 0.0, MASKED).astype(f),
    }
    inv = (1.0 / (f(1000000.0) ** (np.arange(0, HD, 2).astype(f) / f(HD)))).astype(f)
    ang = (np.arange(S).astype(f)[:, None] * inv[None, :]).astype(f).astype(np.float64)
    c["c_cos"] = np.concatenate([np.cos(ang), np.cos(ang)], 1).astype(f)
    c["c_sin"] = np.concatenate([-np.sin(ang), np.sin(ang)], 1).astype(f)
    return {k: np.ascontiguousarray(v) for k, v in c.items()}


def kernel(**inputs):
    import numpy as np
    import concourse.bacc as bacc
    from concourse.bass_utils import run_bass_kernel_spmd

    a = {k: np.asarray(v) for k, v in inputs.items()}
    x = a["L0_attn_x"].reshape(S, D)
    bqk = np.concatenate([a["L0_attn_bq"], a["L0_attn_bk"]]).reshape(4, P).T
    wq = a["L1_attn_Wq"].reshape(KD, P, NKV, SETS_PER_KV, SET * HD).transpose(2, 3, 1, 0, 4)
    wo = a["L1_attn_Wo"].reshape(NKV, SETS_PER_KV, SET, HD, D).transpose(0, 1, 3, 2, 4)
    per_kv = lambda w: w.reshape(KD, P, NKV, HD).transpose(2, 1, 0, 3)
    per_expert = lambda w: w.reshape(NE, KD, P, NI).transpose(0, 2, 1, 3).reshape(NE, P, D)
    arrays = {
        "x": x, "xT": x.T,
        "r_wqk": np.concatenate([a["L0_attn_Wq"], a["L0_attn_Wk"]], 1),
        "r_wkv": np.concatenate([a["L0_attn_Wk"], a["L0_attn_Wv"]], 1),
        "r_bqk": bqk,
        "r_bkv": np.concatenate([a["L0_attn_bk"], a["L0_attn_bv"]]).reshape(1, 2 * D),
        "f_up_q": a["L0_ffn_w_up_q"].T, "f_up_scale": a["L0_ffn_w_up_scale"].T,
        "f_up_a": a["L0_ffn_w_up_lora_a"].T, "f_up_b": a["L0_ffn_w_up_lora_b"],
        "f_down_q": a["L0_ffn_w_down_q"].T, "f_down_scale": a["L0_ffn_w_down_scale"].T,
        "f_down_a": a["L0_ffn_w_down_lora_a"].T, "f_down_b": a["L0_ffn_w_down_lora_b"],
        "f_b_up": a["L0_ffn_b_up"].reshape(FT, P).T, "f_b_down": a["L0_ffn_b_down"].reshape(1, D),
        "a_wkv": np.concatenate([per_kv(a["L1_attn_Wk"]), per_kv(a["L1_attn_Wv"])], 3).reshape(NKV, P, KD * 2 * HD),
        "a_wset": np.concatenate([wq.reshape(NKV, SETS_PER_KV, P, -1), wo.reshape(NKV, SETS_PER_KV, P, -1)], 3),
        "a_normw": np.stack([a["L1_attn_q_norm_w"], a["L1_attn_k_norm_w"]]).reshape(1, 2, HD),
        "m_gate_w": a["L1_ffn_gate_w"].T, "m_gate_b": a["L1_ffn_gate_b"].reshape(1, NE),
        "m_w": np.concatenate([per_expert(a["L1_ffn_w_gate"]), per_expert(a["L1_ffn_w_up"]), a["L1_ffn_w_down"],
                               a["L1_ffn_b_gate"][:, :, None], a["L1_ffn_b_up"][:, :, None]], 2),
        "m_b_down": a["L1_ffn_b_down"],
        **constants(),
    }
    arrays = {f"in_{k}": np.ascontiguousarray(v) for k, v in arrays.items()}
    nc = bacc.Bacc("TRN2", target_bir_lowering=False, num_devices=1)
    d = {k[3:]: nc.dram_tensor(k, v.shape, mybir.dt.from_np(v.dtype), kind="ExternalInput").ap()
         for k, v in arrays.items()}
    out = nc.dram_tensor("out_x", (S, D), F32, kind="ExternalOutput").ap()
    build(nc, d, out)
    r = run_bass_kernel_spmd(nc, [arrays], core_ids=[0])
    return r.results[0]["out_x"].reshape(a["L0_attn_x"].shape)
```

```python
from contextlib import ExitStack

import concourse.bass as bass
from concourse import mybir

F32 = mybir.dt.float32
F32R = mybir.dt.float32r
I32 = mybir.dt.int32
ALU = mybir.AluOpType
ACT = mybir.ActivationFunctionType
AX = mybir.AxisListType

P = 128
S, D = 1024, 256
NT = S // P
KD = D // P
LN_EPS = 1e-5
RH, RD = 8, 32
FH = 1024
FT = FH // P
LORA = 16
QBLOCK = 64
NH, NKV, HD = 32, 4, 128
SET = 4
SETS_PER_KV = NH // NKV // SET
STEPS = SETS_PER_KV * NT
RMS_EPS = 1e-6
MASKED = -1e30
NE, NI = 32, 128
TOPK = 4
HALF = 512
NHALF = S // HALF
LIMIT = 7.0
ABSENT = -3e38


def split_matmul(pe, out, w_h, w_l, x_h, x_l, start, stop):
    pe.matmul(out, w_h, x_h, start=start, stop=False)
    pe.matmul(out, w_h, x_l, start=False, stop=False)
    return pe.matmul(out, w_l, x_h, start=False, stop=stop)


class Norm:

    def __init__(self, nc, ctx, tag, x_tok, xT_h, xT_l, ident, banks):
        sb = lambda n, s: ctx.enter_context(nc.sbuf_tensor(f"{tag}_{n}", s, F32))
        sem = lambda n: ctx.enter_context(nc.semaphore(f"{tag}_{n}"))
        self.stats, self.mv = sb("stats", [P, NT, 6]), sb("mv", [P, NT, 2])
        self.var, self.power, self.rstd = sb("var", [P, NT]), sb("power", [P, NT]), sb("rstd", [P, NT])
        self.x, self.xT_h, self.xT_l, self.ident, self.banks = x_tok, xT_h, xT_l, ident, banks
        self.s_stats, self.s_mv, self.s_rstd = sem("stats_done"), sem("mv_done"), sem("rstd_done")
        self.s_x, self.s_tr, self.s_hi, self.s_lo = sem("x_done"), sem("tr_done"), sem("hi_done"), sem("lo_done")

    def dve_stats(self, dve, t):
        dve.bn_stats(self.stats[:, t, :], self.x[:, t, :]).then_inc(self.s_stats, 1)

    def dve_moments(self, dve):
        dve.wait_ge(self.s_stats, NT)
        for t in range(NT):
            dve.bn_aggr(self.mv[:, t, :], self.stats[:, t, :]).then_inc(self.s_mv, 1)

    def dve_scale(self, dve):
        dve.wait_ge(self.s_rstd, 3)
        for t in range(NT):
            dve.tensor_scalar(self.x[:, t, :], self.x[:, t, :], self.mv[:, t, 0:1], self.rstd[:, t:t + 1],
                              ALU.subtract, ALU.mult).then_inc(self.s_x, 1)

    def pool(self, pool):
        pool.memset(self.power[:], -0.5).then_inc(self.s_rstd, 1)
        pool.wait_ge(self.s_mv, NT)
        pool.tensor_scalar(self.var[:], self.mv[:, :, 1], LN_EPS, None, ALU.add).then_inc(self.s_rstd, 1)
        pool.wait_ge(self.s_rstd, 2)
        pool.tensor_tensor(self.rstd[:], self.var[:], self.power[:], ALU.pow).then_inc(self.s_rstd, 1)

    def tensor(self, pe):
        for t in range(NT):
            pe.wait_ge(self.s_x, t + 1)
            banks = len(self.banks)
            if t >= banks:
                pe.wait_ge(self.s_lo, t - banks + 1)
            for k in range(KD):
                last = pe.transpose(self.banks[t % banks][:, k * P:(k + 1) * P],
                                    self.x[:, t, k * P:(k + 1) * P], self.ident)
            last.then_inc(self.s_tr, 1)

    def bank(self, t):
        return self.banks[t % len(self.banks)][:, 0:D].rearrange("p (k q) -> p k q", k=KD)

    def scalar_hi(self, act):
        for t in range(NT):
            act.wait_ge(self.s_tr, t + 1)
            act.activation(self.xT_h[:, :, t * P:(t + 1) * P], self.bank(t), ACT.Copy).then_inc(self.s_hi, 1)

    def dve_lo(self, dve):
        for t in range(NT):
            dve.wait_ge(self.s_hi, t + 1)
            dve.tensor_tensor(self.xT_l[:, :, t * P:(t + 1) * P], self.bank(t),
                              self.xT_h[:, :, t * P:(t + 1) * P].bitcast(F32), ALU.subtract).then_inc(self.s_lo, 1)


class AttentionOperands:

    def __init__(self, nc, ctx):
        sb = lambda n, s, dt=F32: ctx.enter_context(nc.sbuf_tensor(f"a_{n}", s, dt))
        sem = lambda n: ctx.enter_context(nc.semaphore(f"a_{n}"))
        self.cosw = sb("cosw", [P, 2, NT, HD])
        self.sinw = sb("sinw", [P, 2, NT, HD])
        self.normw = sb("normw", [P, 2, HD])
        self.mask = sb("mask", [P, P])
        self.ident_r, self.mask_r = sb("ident_r", [P, P], F32R), sb("mask_r", [P, P], F32R)
        self.wkv = sb("wkv", [P, KD, 2 * HD])
        self.wkv_h, self.wkv_l = sb("wkv_h", [P, KD, 2 * HD], F32R), sb("wkv_l", [P, KD, 2 * HD], F32R)
        self.W = W = KD * SET * HD
        self.wset = sb("wset", [P, 2, W])
        self.wset_h, self.wset_l = sb("wset_h", [P, 2, 2, W], F32R), sb("wset_l", [P, 2, 2, W], F32R)
        self.const_loaded, self.table_done, self.masks_set = sem("const_loaded"), sem("table_done"), sem("masks_set")
        self.wkv_loaded, self.wkv_hi, self.wkv_lo = sem("wkv_loaded"), sem("wkv_hi"), sem("wkv_lo")
        self.wset_loaded = sem("wset_loaded")
        self.wset_hi, self.wset_lo = ([sem(f"wset{s}_{n}") for s in range(SETS_PER_KV)] for n in ("hi", "lo"))

    def load_kv(self, sp, d, g):
        sp.dma_start(self.wkv[:], d["a_wkv"][g].rearrange("p (k n) -> p k n", k=KD)).then_inc(self.wkv_loaded, 16)

    def load_set(self, sp, d, g, s):
        sp.dma_start(self.wset[:], d["a_wset"][g, s].rearrange("p (a n) -> p a n", a=2))\
          .then_inc(self.wset_loaded, 16)

    def load_first(self, sp, d):
        for name, dst in (("c_cos", self.cosw), ("c_sin", self.sinw)):
            for j in range(2):
                sp.dma_start(dst[:, j, :, :], d[name].rearrange("(t p) n -> p t n", p=P))\
                  .then_inc(self.const_loaded, 16)
        sp.dma_start(self.normw[:], d["a_normw"].broadcast_to([P, 2, HD])).then_inc(self.const_loaded, 16)
        sp.dma_start(self.mask[:], d["c_mask"]).then_inc(self.const_loaded, 16)
        self.load_kv(sp, d, 0)
        self.load_set(sp, d, 0, 0)

    def set_piece(self, s, n):
        cols = slice(n % 2 * self.W // 2, (n % 2 + 1) * self.W // 2)
        return self.wset[:, n // 2, cols], self.wset_h[:, s, n // 2, cols], self.wset_l[:, s, n // 2, cols]

    def prepare_first(self, pool, ident):
        h = HD // 2
        pool.wait_ge(self.const_loaded, 16 * 6)
        pool.tensor_copy(self.ident_r[:], ident).then_inc(self.masks_set, 1)
        pool.tensor_copy(self.mask_r[:], self.mask[:]).then_inc(self.masks_set, 1)
        for j in range(2):
            for table, out, weight in ((self.cosw, slice(0, HD), slice(0, HD)),
                                       (self.sinw, slice(0, h), slice(h, HD)), (self.sinw, slice(h, HD), slice(0, h))):
                w = self.normw[:, j:j + 1, weight].broadcast_to([P, NT, weight.stop - weight.start])
                pool.tensor_tensor(table[:, j, :, out], table[:, j, :, out], w, ALU.mult).then_inc(self.table_done, 1)
        pool.wait_ge(self.wkv_loaded, 16)
        pool.tensor_copy(self.wkv_h[:], self.wkv[:]).then_inc(self.wkv_hi, 1)
        pool.wait_ge(self.wkv_hi, 1)
        pool.tensor_tensor(self.wkv_l[:], self.wkv[:], self.wkv_h[:].bitcast(F32), ALU.subtract)\
            .then_inc(self.wkv_lo, 1)
        pool.wait_ge(self.wset_loaded, 16)
        for n in range(4):
            raw, high, low = self.set_piece(0, n)
            pool.tensor_copy(high, raw).then_inc(self.wset_hi[0], 1)
            pool.wait_ge(self.wset_hi[0], n + 1)
            pool.tensor_tensor(low, raw, high.bitcast(F32), ALU.subtract).then_inc(self.wset_lo[0], 1)


class FfnOperands:

    N_LOADS = 2 * (1 + 2 + 2) + 2

    def __init__(self, nc, ctx):
        sb = lambda n, s, dt=F32: ctx.enter_context(nc.sbuf_tensor(f"f_{n}", s, dt))
        self.quant = [sb("quant0", [P, KD, FH], I32), sb("quant1", [P, FT, D], I32)]
        self.scale = [sb("scale0", [P, KD, FH]), sb("scale1", [P, FT, D])]
        self.lora_a = [sb("lora_a0", [LORA, D]), sb("lora_a1", [LORA, FH])]
        self.lora_b = [sb("lora_b0", [LORA, FH]), sb("lora_b1", [LORA, D])]
        self.b_up = sb("b_up", [P, FT])
        self.b_down = sb("b_down", [P, D])
        self.loaded = ctx.enter_context(nc.semaphore("f_loaded"))
        self.w_scaled = ctx.enter_context(nc.semaphore("f_w_scaled"))
        self.lora_mm = ctx.enter_context(nc.semaphore("f_lora_mm"))

    @staticmethod
    def piece(n, a):
        if n < 4:
            return a[0][:, n // 2, (n % 2) * HALF:(n % 2 + 1) * HALF]
        return a[1][:, 2 * (n - 4):2 * (n - 3), :].rearrange("p a b -> p (a b)")

    def load(self, sp, d):
        for j, (name, kt) in enumerate((("up", KD), ("down", FT))):
            sp.dma_start(self.quant[j][:], d[f"f_{name}_q"].rearrange("(k p) n -> p k n", p=P))\
              .then_inc(self.loaded, 16)
            for b in range(P // QBLOCK):
                src = d[f"f_{name}_scale"].rearrange("(k b o) n -> b o k n", b=P // QBLOCK, o=1)[b]
                sp.dma_start(self.scale[j][QBLOCK * b:QBLOCK * (b + 1), :, :],
                             src.broadcast_to([QBLOCK, kt, src.shape[2]])).then_inc(self.loaded, 16)
            sp.dma_start(self.lora_a[j][:], d[f"f_{name}_a"]).then_inc(self.loaded, 16)
            sp.dma_start(self.lora_b[j][:], d[f"f_{name}_b"]).then_inc(self.loaded, 16)
        sp.dma_start(self.b_up[:], d["f_b_up"]).then_inc(self.loaded, 16)
        sp.dma_start(self.b_down[:], d["f_b_down"].broadcast_to([P, D])).then_inc(self.loaded, 16)

    def lora(self, pe, ps, n):
        if n < 4:
            last = pe.matmul(ps[:, n, :], self.lora_a[0][:, (n // 2) * P:(n // 2 + 1) * P],
                             self.lora_b[0][:, (n % 2) * HALF:(n % 2 + 1) * HALF], start=True, stop=True)
        else:
            for j in range(2):
                row = 2 * (n - 4) + j
                last = pe.matmul(ps[:, n, j * D:(j + 1) * D], self.lora_a[1][:, row * P:(row + 1) * P],
                                 self.lora_b[1][:], start=True, stop=True)
        last.then_inc(self.lora_mm, 1)

    def dequantise(self, dve, n):
        if n == 0:
            dve.wait_ge(self.loaded, 16 * self.N_LOADS)
        dve.scalar_tensor_tensor(out=self.piece(n, self.scale), in0=self.piece(n, self.quant), scalar=-7.5,
                                 in1=self.piece(n, self.scale), op0=ALU.add, op1=ALU.mult).then_inc(self.w_scaled, 1)


def retention_stage(nc, ps, x_tok, xT_h, xT_l, ident, ffn, operands, d):
    with ExitStack() as ctx:
        sb = lambda n, s, dt=F32: ctx.enter_context(nc.sbuf_tensor(f"r_{n}", s, dt))
        sem = lambda n: ctx.enter_context(nc.semaphore(f"r_{n}"))
        xT = sb("xT", [P, KD, S])
        wqk = sb("wqk", [P, KD, 2 * D])
        wkv = sb("wkv", [P, KD, 2 * D])
        wqk_h, wqk_l = sb("wqk_h", [P, KD, 2 * D], F32R), sb("wqk_l", [P, KD, 2 * D], F32R)
        wkv_h, wkv_l = sb("wkv_h", [P, KD, 2 * D], F32R), sb("wkv_l", [P, KD, 2 * D], F32R)
        bqk = sb("bqk", [P, 4])
        bkv = sb("bkv", [P, 2 * D])
        decay = sb("decay", [P, 4, 2, P])
        qgain = sb("qgain", [P, 2, P])
        kgain = sb("kgain", [P, D])
        blockdiag = sb("blockdiag", [P, D])
        chunk_gain = sb("chunk_gain", [P, 2])
        qkT = sb("qkT", [P, 4, S])
        qgT = sb("qgT", [P, 2, 2, P])
        kv = sb("kv", [P, 2, 2 * D])
        kg = sb("kg", [P, 2, D])
        aT = sb("aT", [P, 2, 4, 2, P])
        state = sb("state", [P, 2, P])
        fresh = sb("fresh", [P, D])

        qk_loaded, loaded = sem("qk_loaded"), sem("loaded")
        x_loaded = sem("x_loaded")
        wqk_hi, wqk_lo, xT_hi, xT_lo, wkv_hi, wkv_lo = (sem(n) for n in (
            "wqk_hi", "wqk_lo", "xT_hi", "xT_lo", "wkv_hi", "wkv_lo"))
        qkT_mm, qkT_done = sem("qkT_mm"), sem("qkT_done")
        kv_mm, kv_done, kg_done = sem("kv_mm"), sem("kv_done"), sem("kg_done")
        qg_done, state_zero = sem("qg_done"), sem("state_zero")
        score_mm, aT_done = sem("score_mm"), sem("aT_done")
        out_mm, out_done = sem("out_mm"), sem("out_done")
        state_mm, fresh_done, state_done = sem("state_mm"), sem("fresh_done"), sem("state_done")
        norm = Norm(nc, ctx, "rn", x_tok, xT_h, xT_l, ident, (ps[:, 6, :], ps[:, 7, :]))
        N_LOADS = 8
        block = ctx.enter_context(nc.Block())

        @block.sync
        def _(sp):
            sp.dma_start(wqk[:], d["r_wqk"].rearrange("(k p) n -> p k n", p=P)).then_inc(qk_loaded, 16)
            sp.dma_start(xT[:], d["xT"].rearrange("(k p) n -> p k n", p=P)).then_inc(qk_loaded, 16)
            sp.dma_start(bqk[:], d["r_bqk"]).then_inc(qk_loaded, 16)
            sp.dma_start(wkv[:], d["r_wkv"].rearrange("(k p) n -> p k n", p=P)).then_inc(loaded, 16)
            sp.dma_start(bkv[:], d["r_bkv"].broadcast_to([P, 2 * D])).then_inc(loaded, 16)
            sp.dma_start(decay[:], d["c_decay"]).then_inc(loaded, 16)
            sp.dma_start(qgain[:], d["c_qgain"]).then_inc(loaded, 16)
            sp.dma_start(kgain[:], d["c_kgain"]).then_inc(loaded, 16)
            sp.dma_start(blockdiag[:], d["c_blockdiag"]).then_inc(loaded, 16)
            sp.dma_start(chunk_gain[:], d["c_chunkgain"]).then_inc(loaded, 16)
            sp.dma_start(ident, d["c_ident"]).then_inc(loaded, 16)
            sp.dma_start(x_tok[:], d["x"].rearrange("(t p) n -> p t n", p=P)).then_inc(x_loaded, 16)
            ffn.load(sp, d)
            operands.load_first(sp, d)

        @block.tensor
        def _(pe):
            pe.wait_ge(wqk_lo, 1)
            for n in range(8):
                th, f = n // 4, n % 4
                if f == 0:
                    pe.wait_ge(xT_lo, th + 1)
                if n >= 2:
                    pe.wait_ge(qkT_done, n - 1)
                cols, rows = slice(th * HALF, (th + 1) * HALF), slice(f * P, (f + 1) * P)
                for k in range(KD):
                    last = split_matmul(pe, ps[:, n % 2, :], wqk_h[:, k, rows], wqk_l[:, k, rows],
                                        xT_h[:, k, cols], xT_l[:, k, cols], k == 0, k == KD - 1)
                last.then_inc(qkT_mm, 1)

            def project(c):
                if c >= 2:
                    pe.wait_ge(kv_done, 2 * (c - 1))
                else:
                    pe.wait_ge(qkT_done, 7 + c)
                for k in range(KD):
                    last = split_matmul(pe, ps[:, c % 2, :], xT_h[:, k, c * P:(c + 1) * P],
                                        xT_l[:, k, c * P:(c + 1) * P], wkv_h[:, k, :], wkv_l[:, k, :],
                                        k == 0, k == KD - 1)
                last.then_inc(kv_mm, 1)

            def scores(c):
                if c == 0:
                    pe.wait_ge(qkT_done, 8)
                else:
                    pe.wait_ge(aT_done, c)
                for h in range(RH):
                    r = slice(RD * (h % 4), RD * (h % 4) + RD)
                    last = pe.matmul(ps[:, 2 + h % 4, (h // 4) * P:(h // 4 + 1) * P],
                                     qkT[r, 2 + h // 4, c * P:(c + 1) * P], qkT[r, h // 4, c * P:(c + 1) * P],
                                     start=True, stop=True)
                last.then_inc(score_mm, 1)

            pe.wait_ge(wkv_lo, 1)
            project(0)
            project(1)
            scores(0)
            for c in range(NT):
                pe.wait_ge(kg_done, c + 1)
                pe.wait_ge(kv_done, 2 * c + 2)
                if c >= 1:
                    pe.wait_ge(fresh_done, c)
                for g in range(2):
                    last = pe.matmul(ps[:, 7, g * P:(g + 1) * P], kg[:, c % 2, g * P:(g + 1) * P],
                                     kv[:, c % 2, D + g * P:D + (g + 1) * P], start=True, stop=True)
                last.then_inc(state_mm, 1)
                pe.wait_ge(qg_done, c + 1)
                pe.wait_ge(state_done, c + 1)
                pe.wait_ge(aT_done, c + 1)
                if c >= 1:
                    pe.wait_ge(out_done, c)
                for g in range(2):
                    pe.matmul(ps[:, 6, g * P:(g + 1) * P], qgT[:, c % 2, g, :], state[:, g, :],
                              start=(g == 0), stop=False, skip_group_check=True)
                for h in range(RH):
                    last = pe.matmul(ps[:, 6, h * RD:(h + 1) * RD], aT[:, c % 2, h % 4, h // 4, :],
                                     kv[:, c % 2, D + h * RD:D + (h + 1) * RD], start=False,
                                     stop=(h == RH - 1), skip_group_check=True)
                last.then_inc(out_mm, 1)
                if c + 1 < NT:
                    scores(c + 1)
                if c + 2 < NT:
                    project(c + 2)
            pe.wait_ge(ffn.loaded, 16 * ffn.N_LOADS)
            pe.wait_ge(aT_done, NT)
            for n in range(6):
                ffn.lora(pe, ps, n)
            pe.wait_ge(out_done, NT)
            norm.tensor(pe)

        @block.scalar
        def _(act):
            act.wait_ge(qk_loaded, 16 * 3)
            act.activation(wqk_h[:], wqk[:], ACT.Copy).then_inc(wqk_hi, 1)
            for th in range(NHALF):
                cols = slice(th * HALF, (th + 1) * HALF)
                act.activation(xT_h[:, :, cols], xT[:, :, cols], ACT.Copy).then_inc(xT_hi, 1)
            act.wait_ge(loaded, 16 * N_LOADS)
            act.activation(wkv_h[:], wkv[:], ACT.Copy).then_inc(wkv_hi, 1)
            for n in range(8):
                th, f = n // 4, n % 4
                act.wait_ge(qkT_mm, n + 1)
                act.activation(qkT[:, f, th * HALF:(th + 1) * HALF], ps[:, n % 2, :], ACT.Identity,
                               bias=bqk[:, f:f + 1]).then_inc(qkT_done, 1)
            norm.scalar_hi(act)

        @block.gpsimd
        def _(pool):
            pool.memset(state[:], 0.0).then_inc(state_zero, 1)
            pool.wait_ge(loaded, 16 * N_LOADS)
            operands.prepare_first(pool, ident)
            norm.pool(pool)

        @block.vector
        def _(dve):
            dve.wait_ge(wqk_hi, 1)
            dve.tensor_tensor(wqk_l[:], wqk[:], wqk_h[:].bitcast(F32), ALU.subtract).then_inc(wqk_lo, 1)
            for th in range(NHALF):
                cols = slice(th * HALF, (th + 1) * HALF)
                dve.wait_ge(xT_hi, th + 1)
                dve.tensor_tensor(xT_l[:, :, cols], xT[:, :, cols], xT_h[:, :, cols].bitcast(F32), ALU.subtract)\
                   .then_inc(xT_lo, 1)
            dve.wait_ge(wkv_hi, 1)
            dve.tensor_tensor(wkv_l[:], wkv[:], wkv_h[:].bitcast(F32), ALU.subtract).then_inc(wkv_lo, 1)
            dve.wait_ge(loaded, 16 * N_LOADS)
            dve.wait_ge(state_zero, 1)
            dve.tensor_copy(state[:], state[:]).then_inc(state_done, 1)

            def keys_values(c):
                dve.wait_ge(kv_mm, c + 1)
                if c >= 2:
                    dve.wait_ge(out_mm, c - 1)
                for j in range(2):
                    dve.tensor_tensor(kv[:, c % 2, j * D:(j + 1) * D], ps[:, c % 2, j * D:(j + 1) * D],
                                      bkv[:, j * D:(j + 1) * D], ALU.add).then_inc(kv_done, 1)
                dve.wait_ge(kv_done, 2 * c + 1)
                dve.tensor_tensor(kg[:, c % 2, :], kv[:, c % 2, 0:D], kgain[:], ALU.mult).then_inc(kg_done, 1)
                if c == 0:
                    dve.wait_ge(qkT_done, 8)
                dve.tensor_tensor(qgT[:, c % 2, :, :], qkT[:, 0:2, c * P:(c + 1) * P], qgain[:], ALU.mult)\
                   .then_inc(qg_done, 1)

            keys_values(0)
            dve.wait_ge(x_loaded, 16)
            for c in range(NT):
                dve.wait_ge(score_mm, c + 1)
                dve.tensor_tensor(aT[:, c % 2, :, :, :].rearrange("p a b q -> p a (b q)"), ps[:, 2:6, 0:2 * P],
                                  decay[:].rearrange("p a b q -> p a (b q)"), ALU.mult).then_inc(aT_done, 1)
                if c + 1 < NT:
                    keys_values(c + 1)
                dve.wait_ge(state_mm, c + 1)
                dve.wait_ge(state_done, c + 1)
                dve.tensor_tensor(fresh[:], ps[:, 7, 0:D], blockdiag[:], ALU.mult).then_inc(fresh_done, 1)
                dve.wait_ge(out_mm, c + 1)
                dve.tensor_tensor(x_tok[:, c, :], ps[:, 6, 0:D], x_tok[:, c, :], ALU.add).then_inc(out_done, 1)
                dve.wait_ge(fresh_done, c + 1)
                for g in range(2):
                    last = dve.scalar_tensor_tensor(out=state[:, g, :], in0=state[:, g, :],
                                                    scalar=chunk_gain[:, g:g + 1],
                                                    in1=fresh[:, g * P:(g + 1) * P], op0=ALU.mult, op1=ALU.add)
                last.then_inc(state_done, 1)
                dve.wait_ge(out_done, c + 1)
                norm.dve_stats(dve, c)
                ffn.dequantise(dve, c)
            norm.dve_moments(dve)
            norm.dve_scale(dve)
            norm.dve_lo(dve)


def ffn_stage(nc, ps, x_tok, xT_h, xT_l, ident, ffn, d):
    with ExitStack() as ctx:
        sb = lambda n, s, dt=F32: ctx.enter_context(nc.sbuf_tensor(f"f_{n}", s, dt))
        sem = lambda n: ctx.enter_context(nc.semaphore(f"f_{n}"))
        w, b_up, b_down, piece = ffn.scale, ffn.b_up, ffn.b_down, ffn.piece
        w_h = [sb("w0h", [P, KD, FH], F32R), sb("w1h", [P, FT, D], F32R)]
        w_l = [sb("w0l", [P, KD, FH], F32R), sb("w1l", [P, FT, D], F32R)]
        hid = sb("hid", [P, 2, HALF])
        hid_h = sb("hid_h", [P, FT, HALF], F32R)
        hid_l = sb("hid_l", [P, FT, HALF], F32R)

        lora_mm = ffn.lora_mm
        w_full, w_hi, w_lo = sem("w_full"), sem("w_hi"), sem("w_lo")
        up_mm, relu_done, hid_hi, hid_lo = (sem(n) for n in ("up_mm", "relu_done", "hid_hi", "hid_lo"))
        down_mm, res_done, sum_done = sem("down_mm"), sem("res_done"), sem("sum_done")
        norm = Norm(nc, ctx, "fn", x_tok, xT_h, xT_l, ident, [ps[:, b, :] for b in (0, 1, 6, 7)])
        block = ctx.enter_context(nc.Block())

        @block.tensor
        def _(pe):
            for n in (6, 7):
                ffn.lora(pe, ps, n)
            pe.wait_ge(w_lo, 4)
            for th in range(NHALF):
                for f in range(FT):
                    n = th * FT + f
                    if n >= 2:
                        pe.wait_ge(relu_done, n - 1)
                    for k in range(KD):
                        cols = slice(th * HALF, (th + 1) * HALF)
                        last = split_matmul(pe, ps[:, 2 + n % 2, :], w_h[0][:, k, f * P:(f + 1) * P],
                                            w_l[0][:, k, f * P:(f + 1) * P], xT_h[:, k, cols], xT_l[:, k, cols],
                                            k == 0, k == KD - 1)
                    last.then_inc(up_mm, 1)
                pe.wait_ge(w_lo, 8)
                for q in range(HALF // P):
                    n = th * (HALF // P) + q
                    if n >= 2:
                        pe.wait_ge(sum_done, n - 1)
                    for f in range(FT):
                        if q == 0:
                            pe.wait_ge(hid_lo, th * FT + f + 1)
                        last = split_matmul(pe, ps[:, 4 + n % 2, 0:D], hid_h[:, f, q * P:(q + 1) * P],
                                            hid_l[:, f, q * P:(q + 1) * P], w_h[1][:, f, :], w_l[1][:, f, :],
                                            f == 0, f == FT - 1)
                    last.then_inc(down_mm, 1)
            norm.tensor(pe)

        @block.scalar
        def _(act):
            for n in range(8):
                act.wait_ge(w_full, n + 1)
                act.activation(piece(n, w_h), piece(n, w), ACT.Copy).then_inc(w_hi, 1)
            for n in range(NHALF * FT):
                act.wait_ge(relu_done, n + 1)
                if n >= FT:
                    act.wait_ge(down_mm, HALF // P)
                act.activation(hid_h[:, n % FT, :], hid[:, n % 2, :], ACT.Copy).then_inc(hid_hi, 1)
            norm.scalar_hi(act)

        @block.gpsimd
        def _(pool):
            norm.pool(pool)

        @block.vector
        def _(dve):
            def low(n):
                dve.wait_ge(w_hi, n + 1)
                dve.tensor_tensor(piece(n, w_l), piece(n, w), piece(n, w_h).bitcast(F32), ALU.subtract)\
                   .then_inc(w_lo, 1)

            for n in range(8):
                dve.wait_ge(lora_mm, n + 1)
                dve.wait_ge(ffn.w_scaled, n + 1)
                dve.tensor_tensor(piece(n, w), ps[:, n, :], piece(n, w), ALU.add).then_inc(w_full, 1)
                if n >= 2:
                    low(n - 2)
            low(6)
            low(7)

            def hidden_low(n):
                dve.wait_ge(hid_hi, n + 1)
                dve.tensor_tensor(hid_l[:, n % FT, :], hid[:, n % 2, :], hid_h[:, n % FT, :].bitcast(F32),
                                  ALU.subtract).then_inc(hid_lo, 1)

            for th in range(NHALF):
                for f in range(FT):
                    n = th * FT + f
                    dve.wait_ge(up_mm, n + 1)
                    if n >= 2:
                        dve.wait_ge(hid_lo, n - 1)
                    dve.tensor_scalar(hid[:, n % 2, :], ps[:, 2 + n % 2, :], b_up[:, f:f + 1], 0.0,
                                      ALU.add, ALU.max).then_inc(relu_done, 1)
                    if f >= 1:
                        hidden_low(n - 1)
                hidden_low(th * FT + FT - 1)
                for q in range(HALF // P):
                    n = th * (HALF // P) + q
                    dve.tensor_tensor(x_tok[:, n, :], x_tok[:, n, :], b_down[:], ALU.add).then_inc(res_done, 1)
                    dve.wait_ge(down_mm, n + 1)
                    dve.wait_ge(res_done, n + 1)
                    dve.tensor_tensor(x_tok[:, n, :], ps[:, 4 + n % 2, 0:D], x_tok[:, n, :], ALU.add)\
                       .then_inc(sum_done, 1)
                    dve.wait_ge(sum_done, n + 1)
                    norm.dve_stats(dve, n)
            norm.dve_moments(dve)
            norm.dve_scale(dve)
            norm.dve_lo(dve)


def attention_stage(nc, ps, x_tok, xT_h, xT_l, ident, operands, d):
    with ExitStack() as ctx:
        sb = lambda n, s, dt=F32: ctx.enter_context(nc.sbuf_tensor(f"a_{n}", s, dt))
        sem = lambda n: ctx.enter_context(nc.semaphore(f"a_{n}"))
        cosw, sinw, ident_r, mask_r = operands.cosw, operands.sinw, operands.ident_r[:], operands.mask_r[:]
        wkv, wkv_h, wkv_l = operands.wkv, operands.wkv_h, operands.wkv_l
        wset_h, wset_l = operands.wset_h, operands.wset_l
        wkv_loaded, wkv_hi, wkv_lo = operands.wkv_loaded, operands.wkv_hi, operands.wkv_lo
        wset_loaded, wset_hi, wset_lo = operands.wset_loaded, operands.wset_hi, operands.wset_lo
        v_h, v_l = sb("v_h", [P, NT, HD], F32R), sb("v_l", [P, NT, HD], F32R)
        kT_h, kT_l = sb("kT_h", [P, S], F32R), sb("kT_l", [P, S], F32R)
        krot = sb("krot", [P, 2, 2, 2, HD])
        ksum, vraw = sb("ksum", [P, NT, HD]), sb("vraw", [P, NT, HD])
        ksquare = sb("ksquare", [P, 4, HD])
        kss, kvar, krs, power = sb("kss", [P, NT]), sb("kvar", [P, NT]), sb("krs", [P, NT]), sb("power", [P, NT])
        square = sb("square", [P, 2, SET, HD])
        qrot = sb("qrot", [P, 2, SET * HD])
        qsum = sb("qsum", [P, SET * HD])
        qss, qvar, nqrs = sb("qss", [P, 2, SET]), sb("qvar", [P, 2, SET]), sb("nqrs", [P, 2, SET])
        qpow = sb("qpow", [P, SET])
        qT_h, qT_l = sb("qT_h", [P, 2, SET * P], F32R), sb("qT_l", [P, 2, SET * P], F32R)
        probs = sb("probs", [P, 2, SET, S])
        nbias = sb("nbias", [P, 2, SET])
        total, rtotal = sb("total", [P, 2, SET]), sb("rtotal", [P, 2, SET])
        FBUF = 6
        pT_h, pT_l = sb("pT_h", [P, FBUF, SET * P], F32R), sb("pT_l", [P, FBUF, SET * P], F32R)
        recip = sb("recip", [P, SET * P])
        oT = sb("oT", [P, SET * P])
        oT_h, oT_l = sb("oT_h", [P, 2, SET * P], F32R), sb("oT_l", [P, 2, SET * P], F32R)

        power_set = sem("power_set")
        kv_mm, k_sq, kv_read, k_sum, k_var, k_rs, k_scaled = (sem(n) for n in (
            "kv_mm", "k_sq", "kv_read", "k_sum", "k_var", "k_rs", "k_scaled"))
        v_raw, v_hi, v_lo, kT_mm, kT_hi, kT_lo = (sem(n) for n in ("v_raw", "v_hi", "v_lo", "kT_mm", "kT_hi", "kT_lo"))
        q_mm, q_sq, q_rope, q_sum, q_var, q_rs, qT_mm, qT_hi, qT_lo = (sem(n) for n in (
            "q_mm", "q_sq", "q_rope", "q_sum", "q_var", "q_rs", "qT_mm", "qT_hi", "qT_lo"))
        q_pow = sem("q_pow")
        score_mm, nbias_done, exp_done, rtotal_done = (sem(n) for n in (
            "score_mm", "nbias_done", "exp_done", "rtotal_done"))
        pT_mm, pT_hi, pT_lo, pv_mm, oT_hi, oT_lo, wo_mm, y_done = (sem(n) for n in (
            "pT_mm", "pT_hi", "pT_lo", "pv_mm", "oT_hi", "oT_lo", "wo_mm", "y_done"))
        recip_mm, recip_done, oT_raw, oT_done = (sem(n) for n in ("recip_mm", "recip_done", "oT_raw", "oT_done"))
        norm = Norm(nc, ctx, "an", x_tok, xT_h, xT_l, ident, [ps[:, b, :] for b in (0, 1, 2, 3, 5, 6)])

        wq_h = wset_h[:, :, 0, :].rearrange("p s (k n) -> p s k n", k=KD)
        wq_l = wset_l[:, :, 0, :].rearrange("p s (k n) -> p s k n", k=KD)
        wo_h = wset_h[:, :, 1, :].rearrange("p s (h n) -> p s h n", h=SET)
        wo_l = wset_l[:, :, 1, :].rearrange("p s (h n) -> p s h n", h=SET)

        ORDER = [t for pair in zip(range(NT // 2), range(NT - 1, NT // 2 - 1, -1)) for t in pair]
        AHEAD = 4

        def tile_of(s):
            return ORDER[s % NT]

        first_unit = [0]
        for s in range(2 * STEPS):
            first_unit.append(first_unit[-1] + tile_of(s) + 1)
        UNITS = first_unit[STEPS]

        def part(s, j):
            n = tile_of(s) + 1
            return range(n * j // SET, n * (j + 1) // SET)

        def early(s):
            return list(range(min(4 if tile_of(s) >= NT // 2 else 2, tile_of(s) + 1)))

        def arrivals(s, j):
            n = tile_of(s) + 1
            first = list(range(len(early(s)), min(AHEAD, n))) if j == 0 else []
            return first + [kt + AHEAD for kt in part(s, j) if kt + AHEAD < n]

        turns = [("q", 0)]
        for slot in range(2 * STEPS):
            if slot >= 1:
                turns += [("p", slot - 1, kt) for kt in early(slot - 1)]
            for j in range(SET):
                if j == (2 if tile_of(slot) >= NT // 2 else SET - 1):
                    turns.append(("q", slot + 1))
                if slot >= 1:
                    turns += [("p", slot - 1, kt) for kt in arrivals(slot - 1, j)]
            if slot >= 1:
                turns.append(("r", slot - 1))

        def bank_of(key):
            if key[0] == "p":
                banks = (1, 3, 5, 6) if tile_of(key[1]) >= NT // 2 else (5, 6)
                return banks[key[2] % len(banks)]
            return 5 if key[0] == "q" else 6

        def turn_bank(key):
            return ps[:, bank_of(key), :]

        def turn_before(key, last):
            for before in reversed(turns[:turns.index(key)]):
                if bank_of(before) == bank_of(key) and exists(before[1], last):
                    return None if bank_of(key) < 4 and before[1] != key[1] else before

        def score_bank(s, h):
            L = (tile_of(s) + 1) * P
            if L <= HALF:
                return ps[:, 2 * (h % 2), 0:L]
            return ps[:, 2 * (h % 2):2 * (h % 2) + 2, :].rearrange("p a n -> p (a n)")[:, 0:L]

        def swapped(out, in0, table, dve):
            h = HD // 2
            dve.tensor_tensor(out[:, :, 0:h], in0[:, :, h:HD], table[:, :, 0:h], ALU.mult)
            return dve.tensor_tensor(out[:, :, h:HD], in0[:, :, 0:h], table[:, :, h:HD], ALU.mult)

        block = ctx.enter_context(nc.Block())

        ROT = 7
        KV_PAIRS = dict(zip(range(11, 15), range(4)))
        K_SCALE = 15

        def exists(s, last):
            return 0 <= s < (STEPS if last else 2 * STEPS)

        @block.sync
        def _(sp):
            sp.wait_ge(wset_lo[0], 4)
            operands.load_set(sp, d, 0, 1)
            with sp.Fori(1, NKV) as g:
                sp.wait_ge(wkv_lo, g)
                operands.load_kv(sp, d, g)
                sp.wait_ge(wset_lo[1], 4 * g)
                operands.load_set(sp, d, g, 0)
                sp.wait_ge(wset_lo[0], 4 * g + 4)
                operands.load_set(sp, d, g, 1)
        @block.gpsimd
        def _(pool):
            pool.memset(power[:], -0.5).then_inc(power_set, 1)
            pool.wait_ge(power_set, 1)

            def wait(signal, count):
                count = pool.to_reg(count)
                pool.wait_ge(power_set, 1)
                pool.wait_ge(signal, count)

            def split_kv(g):
                wait(wkv_loaded, 16 * g + 16)
                pool.tensor_copy(wkv_h[:], wkv[:]).then_inc(wkv_hi, 1)
                wait(wkv_hi, g + 1)
                pool.tensor_tensor(wkv_l[:], wkv[:], wkv_h[:].bitcast(F32), ALU.subtract).then_inc(wkv_lo, 1)

            def split_set(g, s, n):
                raw, high, low = operands.set_piece(s, n)
                wait(wset_loaded, g * (16 * SETS_PER_KV) + 16 * s + 16)
                pool.tensor_copy(high, raw).then_inc(wset_hi[s], 1)
                wait(wset_hi[s], 4 * g + n + 1)
                pool.tensor_tensor(low, raw, high.bitcast(F32), ALU.subtract).then_inc(wset_lo[s], 1)


            def key_sums(head, p):
                wait(kv_read, head * (NT // 2) + p + 1)
                pool.tensor_tensor(ksum[:, 2 * p:2 * p + 2, :], krot[:, p % 2, 0, :, :], krot[:, p % 2, 1, :, :],
                                   ALU.add).then_inc(k_sum, 1)

            def key_rms(head):
                wait(k_sq, head * NT + NT)
                pool.tensor_scalar(kvar[:], kss[:], 1.0 / HD, RMS_EPS, ALU.mult, ALU.add).then_inc(k_var, 1)
                wait(k_var, head + 1)
                pool.tensor_tensor(krs[:], kvar[:], power[:], ALU.pow).then_inc(k_rs, 1)

            def slot(g, s, last=False):
                def queries(s):
                    wait(q_sq, g * STEPS * SET + SET * s + SET)
                    pool.tensor_scalar(qvar[:, s % 2, :], qss[:, s % 2, :], HD * RMS_EPS, None, ALU.add)\
                        .then_inc(q_var, 1)
                    if s >= 1:
                        wait(qT_mm, g * STEPS + s)
                    wait(q_rope, g * STEPS + s + 1)
                    pool.tensor_tensor(qsum[:], qrot[:, 0, :], qrot[:, 1, :], ALU.add).then_inc(q_sum, 1)
                    wait(q_var, g * STEPS + s + 1)
                    pool.tensor_tensor(qpow[:], qvar[:, s % 2, :], power[:, 0:SET], ALU.pow).then_inc(q_pow, 1)
                    wait(q_pow, g * STEPS + s + 1)
                    pool.tensor_scalar(nqrs[:, s % 2, :], qpow[:], -1.0, None, ALU.mult).then_inc(q_rs, 1)

                def divide(s):
                    wait(oT_raw, g * STEPS + s + 1)
                    pool.tensor_tensor(oT[:], oT[:], recip[:], ALU.mult).then_inc(oT_done, 1)

                def output_high(s):
                    if s >= 2:
                        wait(wo_mm, g * STEPS + s - 1)
                    wait(oT_done, g * STEPS + s + 1)
                    pool.tensor_copy(oT_h[:, s % 2, :], oT[:]).then_inc(oT_hi, 1)

                def output_low(s):
                    wait(oT_hi, g * STEPS + s + 1)
                    pool.tensor_tensor(oT_l[:, s % 2, :], oT[:], oT_h[:, s % 2, :].bitcast(F32), ALU.subtract)\
                        .then_inc(oT_lo, 1)

                if s < 0:
                    return queries(0)
                if s == K_SCALE and not last:
                    key_rms(g + 1)
                if exists(s - 2, last):
                    divide(s - 2)
                if exists(s + 1, last):
                    queries(s + 1)
                if exists(s - 2, last):
                    output_high(s - 2)
                    output_low(s - 2)
                if last:
                    return
                if s == NT:
                    wait(kv_mm, (g + 1) * (NT // 2))
                    split_kv(g + 1)
                if s in KV_PAIRS:
                    key_sums(g + 1, KV_PAIRS[s])
                if NT + 3 <= s < NT + 7:
                    n = s - NT - 3
                    if n < 2:
                        wait(q_mm, g * STEPS + NT)
                    else:
                        wait(wo_mm, g * STEPS + NT)
                    split_set(g + 1, 0, n)
                if s < 4:
                    split_set(0, 1, s)
                if STEPS + 3 <= s < STEPS + 7:
                    n = s - STEPS - 3
                    if n < 2:
                        wait(q_mm, g * STEPS + STEPS)
                    else:
                        wait(wo_mm, g * STEPS + STEPS)
                    split_set(g + 1, 1, n)

            for p in range(NT // 2):
                key_sums(0, p)
            key_rms(0)
            slot(0, -1)
            for s in range(ROT):
                slot(0, s)
            with pool.Fori(0, NKV - 1) as g:
                for s in range(ROT, STEPS + ROT):
                    slot(g, s)
            for s in range(ROT, STEPS + 2):
                slot(NKV - 1, s, last=True)
            pool.wait_ge(y_done, NKV * STEPS)
            norm.pool(pool)

        @block.scalar
        def _(act):
            def key_squares(head, p, bank):
                act.wait_ge(kv_mm, head * (NT // 2) + p + 1)
                if p == 0 and not (isinstance(head, int) and head == 0):
                    act.wait_ge(k_rs, head)
                    act.wait_ge(v_lo, head)
                if p >= 2:
                    act.wait_ge(k_sq, head * NT + 2 * p - 2)
                pair = ps[:, bank, :].rearrange("p (t n) -> p t n", t=2)
                for j in range(2):
                    act.activation(ksquare[:, 2 * (p % 2) + j, :], pair[:, j, 0:HD], ACT.Square,
                                   accum_out=kss[:, 2 * p + j:2 * p + j + 1]).then_inc(k_sq, 1)
                act.activation(vraw[:, 2 * p:2 * p + 2, :], pair[:, :, HD:2 * HD], ACT.Copy).then_inc(v_raw, 1)

            def values_high(head):
                act.wait_ge(v_raw, head * (NT // 2) + NT // 2)
                act.activation(v_h[:], vraw[:], ACT.Copy).then_inc(v_hi, 1)

            def slot(g, s, last=False):
                def squares(s):
                    act.wait_ge(q_mm, g * STEPS + s + 1)
                    if s >= 2:
                        act.wait_ge(q_var, g * STEPS + s - 1)
                    for h in range(SET):
                        act.activation(square[:, s % 2, h, :], ps[:, 4, h * HD:(h + 1) * HD], ACT.Square,
                                       accum_out=qss[:, s % 2, h:h + 1]).then_inc(q_sq, 1)

                def query_high(s):
                    act.wait_ge(qT_mm, g * STEPS + s + 1)
                    if s >= 2:
                        act.wait_ge(score_mm, g * STEPS * SET + SET * (s - 1))
                    act.activation(qT_h[:, s % 2, :], turn_bank(("q", s)), ACT.Copy).then_inc(qT_hi, 1)

                def exp(s, h):
                    L = (tile_of(s) + 1) * P
                    act.wait_ge(nbias_done, g * STEPS * SET + SET * s + h + 1)
                    if s >= 2 and h == 0:
                        act.wait_ge(pT_mm, g * UNITS + first_unit[s - 1])
                    act.activation(probs[:, s % 2, h, 0:L], score_bank(s, h), ACT.Exp, scale=-1.0,
                                   bias=nbias[:, s % 2, h:h + 1], accum_out=total[:, s % 2, h:h + 1])\
                       .then_inc(exp_done, 1)

                def prob_high(s, tiles):
                    for kt in tiles:
                        u = first_unit[s] + kt
                        act.wait_ge(pT_mm, g * UNITS + u + 1)
                        if u >= FBUF:
                            act.wait_ge(pv_mm, g * UNITS + u - FBUF + 1)
                        act.activation(pT_h[:, u % FBUF, :], turn_bank(("p", s, kt)), ACT.Copy).then_inc(pT_hi, 1)

                scored, values = exists(s, last), exists(s - 1, last)
                big = tile_of(s) >= NT // 2
                if values:
                    prob_high(s - 1, early(s - 1))
                if s % STEPS == 0 and scored:
                    for m in range(2):
                        act.wait_ge(kT_mm, 2 * (g + s // STEPS) + m + 1)
                        act.activation(kT_h[:, m * HALF:(m + 1) * HALF], ps[:, 2 * m, :], ACT.Copy).then_inc(kT_hi, 1)
                    squares(s + 1)
                    if values:
                        prob_high(s - 1, arrivals(s - 1, 0))
                    exp(s, 0)
                    exp(s, 1)
                else:
                    if scored:
                        exp(s, 0)
                    if exists(s + 1, last):
                        squares(s + 1)
                    if scored:
                        exp(s, 1)
                    if values:
                        prob_high(s - 1, arrivals(s - 1, 0))
                if scored:
                    exp(s, 2)
                if values:
                    prob_high(s - 1, arrivals(s - 1, 1))
                if exists(s + 1, last) and big:
                    query_high(s + 1)
                if scored:
                    exp(s, 3)
                if values:
                    prob_high(s - 1, arrivals(s - 1, 2))
                if s in KV_PAIRS and not last:
                    key_squares(g + 1, KV_PAIRS[s], 4)
                if exists(s + 1, last) and not big:
                    query_high(s + 1)
                if values:
                    prob_high(s - 1, arrivals(s - 1, 3))
                    act.wait_ge(recip_mm, g * STEPS + s)
                    if s >= 2:
                        act.wait_ge(oT_lo, g * STEPS + s - 1)
                    act.activation(recip[:], turn_bank(("r", s - 1)), ACT.Copy).then_inc(recip_done, 1)
                    act.wait_ge(pv_mm, g * UNITS + first_unit[s])
                    act.activation(oT[:], ps[:, 7, :], ACT.Copy).then_inc(oT_raw, 1)
                if s % STEPS == 0 and scored:
                    values_high(g + s // STEPS)

            def first_queries():
                act.wait_ge(q_mm, 1)
                for h in range(SET):
                    act.activation(square[:, 0, h, :], ps[:, 4, h * HD:(h + 1) * HD], ACT.Square,
                                   accum_out=qss[:, 0, h:h + 1]).then_inc(q_sq, 1)
                act.wait_ge(qT_mm, 1)
                act.activation(qT_h[:, 0, :], turn_bank(("q", 0)), ACT.Copy).then_inc(qT_hi, 1)

            for p in range(NT // 2):
                key_squares(0, p, p)
            first_queries()
            for s in range(ROT):
                slot(0, s)
            with act.Fori(0, NKV - 1) as g:
                for s in range(ROT, STEPS + ROT):
                    slot(g, s)
            for s in range(ROT, STEPS + 1):
                slot(NKV - 1, s, last=True)
            act.wait_ge(y_done, NKV * STEPS)
            norm.scalar_hi(act)

        @block.vector
        def _(dve):
            dve.wait_ge(operands.table_done, 6)

            def key_rope(head, p, bank):
                dve.wait_ge(v_raw, head * (NT // 2) + p + 1)
                if p >= 2:
                    dve.wait_ge(k_sum, head * (NT // 2) + p - 1)
                pair = ps[:, bank, :].rearrange("p (t n) -> p t n", t=2)
                two = slice(2 * p, 2 * p + 2)
                dve.tensor_tensor(krot[:, p % 2, 0, :, :], pair[:, :, 0:HD], cosw[:, 1, two, :], ALU.mult)
                swapped(krot[:, p % 2, 1, :, :], pair[:, :, 0:HD], sinw[:, 1, two, :], dve).then_inc(kv_read, 1)

            def key_scale(head):
                dve.wait_ge(k_sum, head * (NT // 2) + NT // 2)
                dve.wait_ge(k_rs, head + 1)
                for t in range(NT):
                    dve.tensor_scalar(ksum[:, t, :], ksum[:, t, :], krs[:, t:t + 1], None, ALU.mult)\
                       .then_inc(k_scaled, 1)

            def values_low(head):
                dve.wait_ge(v_hi, head + 1)
                dve.tensor_tensor(v_l[:], vraw[:], v_h[:].bitcast(F32), ALU.subtract).then_inc(v_lo, 1)

            def slot(g, s, last=False):
                def rope(s):
                    dve.wait_ge(q_sq, g * STEPS * SET + SET * s + SET)
                    if s >= 1:
                        dve.wait_ge(q_sum, g * STEPS + s)
                    q = ps[:, 4, :].rearrange("p (h n) -> p h n", h=SET)
                    t = tile_of(s)
                    out = qrot[:].rearrange("p a (h n) -> p a h n", h=SET)
                    dve.tensor_tensor(out[:, 0, :, :], q,
                                      cosw[:, 0, t:t + 1, :].broadcast_to([P, SET, HD]), ALU.mult)
                    swapped(out[:, 1, :, :], q, sinw[:, 0, t:t + 1, :].broadcast_to([P, SET, HD]), dve)\
                        .then_inc(q_rope, 1)

                def query_low(s):
                    dve.wait_ge(qT_hi, g * STEPS + s + 1)
                    dve.tensor_tensor(qT_l[:, s % 2, :], turn_bank(("q", s)), qT_h[:, s % 2, :].bitcast(F32),
                                      ALU.subtract).then_inc(qT_lo, 1)

                def scale_scores(s, hh):
                    dve.wait_ge(score_mm, g * STEPS * SET + SET * s + hh + 1)
                    if hh == 0:
                        dve.wait_ge(q_rs, g * STEPS + s + 1)
                    dve.tensor_scalar(score_bank(s, hh), score_bank(s, hh), nqrs[:, s % 2, hh:hh + 1], None,
                                      ALU.mult, ALU.min, accum_out=nbias[:, s % 2, hh:hh + 1]).then_inc(nbias_done, 1)

                def row_totals(s):
                    dve.wait_ge(exp_done, g * STEPS * SET + SET * s + SET)
                    dve.reciprocal(rtotal[:, s % 2, :], total[:, s % 2, :]).then_inc(rtotal_done, 1)

                def prob_low(s, tiles):
                    for kt in tiles:
                        u = first_unit[s] + kt
                        dve.wait_ge(pT_hi, g * UNITS + u + 1)
                        dve.tensor_tensor(pT_l[:, u % FBUF, :], turn_bank(("p", s, kt)),
                                          pT_h[:, u % FBUF, :].bitcast(F32), ALU.subtract).then_inc(pT_lo, 1)

                def add_output(s):
                    dve.wait_ge(wo_mm, g * STEPS + s + 1)
                    t = tile_of(s)
                    dve.tensor_tensor(x_tok[:, t, :], ps[:, 4, 0:D], x_tok[:, t, :], ALU.add).then_inc(y_done, 1)

                scored, values = exists(s, last), exists(s - 1, last)
                big = tile_of(s) >= NT // 2
                if s < 0:
                    rope(0)
                    query_low(0)
                    return
                if s % STEPS == 0 and scored:
                    if values:
                        prob_low(s - 1, early(s - 1))
                    for m in range(2):
                        dve.wait_ge(kT_hi, 2 * (g + s // STEPS) + m + 1)
                        dve.tensor_tensor(kT_l[:, m * HALF:(m + 1) * HALF], ps[:, 2 * m, :],
                                          kT_h[:, m * HALF:(m + 1) * HALF].bitcast(F32), ALU.subtract)\
                           .then_inc(kT_lo, 1)
                    if values:
                        row_totals(s - 1)
                        prob_low(s - 1, arrivals(s - 1, 0))
                    rope(s + 1)
                    scale_scores(s, 0)
                    scale_scores(s, 1)
                else:
                    if scored:
                        scale_scores(s, 0)
                    if values:
                        prob_low(s - 1, early(s - 1))
                    if scored:
                        scale_scores(s, 1)
                    if exists(s + 1, last):
                        rope(s + 1)
                    if s % STEPS == 1 and scored:
                        values_low(g + s // STEPS)
                    if values:
                        row_totals(s - 1)
                        prob_low(s - 1, arrivals(s - 1, 0))
                if scored:
                    scale_scores(s, 2)
                if values:
                    prob_low(s - 1, arrivals(s - 1, 1))
                if s == K_SCALE and not last:
                    key_scale(g + 1)
                if scored:
                    scale_scores(s, 3)
                if exists(s + 1, last) and big:
                    query_low(s + 1)
                if values:
                    prob_low(s - 1, arrivals(s - 1, 2))
                if exists(s - 3, last):
                    add_output(s - 3)
                    if last and s - 3 >= STEPS - NT:
                        dve.wait_ge(y_done, g * STEPS + s - 2)
                        norm.dve_stats(dve, tile_of(s - 3))
                if s in KV_PAIRS and not last:
                    key_rope(g + 1, KV_PAIRS[s], 4)
                if exists(s + 1, last) and not big:
                    query_low(s + 1)
                if values:
                    prob_low(s - 1, arrivals(s - 1, 3))

            for p in range(NT // 2):
                key_rope(0, p, p)
            key_scale(0)
            slot(0, -1)
            for s in range(ROT):
                slot(0, s)
            with dve.Fori(0, NKV - 1) as g:
                for s in range(ROT, STEPS + ROT):
                    slot(g, s)
            for s in range(ROT, STEPS + 3):
                slot(NKV - 1, s, last=True)
            dve.wait_ge(y_done, NKV * STEPS)
            norm.dve_moments(dve)
            norm.dve_scale(dve)
            norm.dve_lo(dve)

        @block.tensor
        def _(pe):
            def keys_values(head, p, bank):
                if p == 0:
                    pe.wait_ge(wkv_lo, head + 1)
                for j in range(2):
                    t = 2 * p + j
                    for k in range(KD):
                        last = split_matmul(pe, ps[:, bank, j * 2 * HD:(j + 1) * 2 * HD],
                                            xT_h[:, k, t * P:(t + 1) * P], xT_l[:, k, t * P:(t + 1) * P],
                                            wkv_h[:, k, :], wkv_l[:, k, :], k == 0, k == KD - 1)
                last.then_inc(kv_mm, 1)

            def slot(g, s, last=False):
                def project(s):
                    st, t = s // NT % SETS_PER_KV, tile_of(s)
                    if s % NT == 0:
                        pe.wait_ge(wset_lo[st], 4 * (g + s // STEPS) + 2)
                    if s - 2 in KV_PAIRS and not last:
                        pe.wait_ge(kv_read, (g + 1) * (NT // 2) + KV_PAIRS[s - 2] + 1)
                    elif s >= 5:
                        pe.wait_ge(y_done, g * STEPS + s - 4)
                    elif s >= 1:
                        pe.wait_ge(q_rope, g * STEPS + s)
                    for k in range(KD):
                        end = split_matmul(pe, ps[:, 4, :], xT_h[:, k, t * P:(t + 1) * P],
                                           xT_l[:, k, t * P:(t + 1) * P], wq_h[:, st, k, :], wq_l[:, st, k, :],
                                           k == 0, k == KD - 1)
                    end.then_inc(q_mm, 1)

                def take_turn(key):
                    before = turn_before(key, last)
                    if before is None:
                        return
                    if before[0] == "q":
                        pe.wait_ge(qT_lo, g * STEPS + before[1] + 1)
                    elif before[0] == "p":
                        pe.wait_ge(pT_lo, g * UNITS + first_unit[before[1]] + before[2] + 1)
                    else:
                        pe.wait_ge(recip_done, g * STEPS + before[1] + 1)

                def transpose_queries(s):
                    take_turn(("q", s))
                    pe.wait_ge(q_sum, g * STEPS + s + 1)
                    for h in range(SET):
                        end = pe.transpose(turn_bank(("q", s))[:, h * P:(h + 1) * P], qsum[:, h * HD:(h + 1) * HD], ident)
                    end.then_inc(qT_mm, 1)

                def scores(s, h):
                    n = SET * s + h
                    if n >= 2:
                        pe.wait_ge(exp_done, g * STEPS * SET + n - 1)
                    if s % STEPS == 0 and h < 2:
                        pe.wait_ge(kT_lo, 2 * (g + s // STEPS) + h + 1)
                    if h == 0:
                        pe.wait_ge(qT_lo, g * STEPS + s + 1)
                    L = (tile_of(s) + 1) * P
                    qh, ql = qT_h[:, s % 2, h * P:(h + 1) * P], qT_l[:, s % 2, h * P:(h + 1) * P]
                    for b in range((L + HALF - 1) // HALF):
                        w = min(HALF, L - b * HALF)
                        cols = slice(b * HALF, b * HALF + w)
                        out = ps[:, 2 * (h % 2) + b, 0:w]
                        end = split_matmul(pe, out, qh, ql, kT_h[:, cols], kT_l[:, cols], True, True)
                        if b * HALF + w == L:
                            end = pe.matmul(out[:, w - P:w], ident_r, mask_r, start=False, stop=True,
                                             skip_group_check=True)
                    end.then_inc(score_mm, 1)

                def transpose_probs(s, kt):
                    take_turn(("p", s, kt))
                    if kt == 0:
                        pe.wait_ge(exp_done, g * STEPS * SET + SET * s + SET)
                    for h in range(SET):
                        end = pe.transpose(turn_bank(("p", s, kt))[:, h * P:(h + 1) * P],
                                            probs[:, s % 2, h, kt * P:(kt + 1) * P], ident)
                    end.then_inc(pT_mm, 1)

                def weigh_values(s, j):
                    n = tile_of(s) + 1
                    if j == 0:
                        for kt in range(len(early(s)), min(AHEAD, n)):
                            transpose_probs(s, kt)
                    for kt in part(s, j):
                        if kt + AHEAD < n:
                            transpose_probs(s, kt + AHEAD)
                        u = first_unit[s] + kt
                        pe.wait_ge(pT_lo, g * UNITS + u + 1)
                        if kt == 0 and s >= 1:
                            pe.wait_ge(oT_raw, g * STEPS + s)
                        if kt == 0 and s % STEPS == 0:
                            pe.wait_ge(v_lo, g + s // STEPS + 1)
                        split_matmul(pe, ps[:, 7, :], v_h[:, kt, :], v_l[:, kt, :], pT_h[:, u % FBUF, :],
                                     pT_l[:, u % FBUF, :], kt == 0, kt == n - 1).then_inc(pv_mm, 1)

                def spread_recip(s):
                    take_turn(("r", s))
                    pe.wait_ge(rtotal_done, g * STEPS + s + 1)
                    for h in range(SET):
                        end = pe.transpose(turn_bank(("r", s))[:, h * P:(h + 1) * P],
                                            rtotal[:, s % 2, h:h + 1].broadcast_to([P, P]), ident)
                    end.then_inc(recip_mm, 1)

                def output(s):
                    st = s // NT % SETS_PER_KV
                    if exists(s + 4, last):
                        pe.wait_ge(q_rope, g * STEPS + s + 5)
                    elif s >= 1:
                        pe.wait_ge(y_done, g * STEPS + s)
                    pe.wait_ge(wset_lo[st], 4 * (g + s // STEPS) + 4)
                    pe.wait_ge(oT_lo, g * STEPS + s + 1)
                    for h in range(SET):
                        end = split_matmul(pe, ps[:, 4, 0:D], oT_h[:, s % 2, h * P:(h + 1) * P],
                                            oT_l[:, s % 2, h * P:(h + 1) * P], wo_h[:, st, h, :], wo_l[:, st, h, :],
                                            h == 0, h == SET - 1)
                    end.then_inc(wo_mm, 1)

                def transpose_keys(head):
                    for m in range(2):
                        if s > 0:
                            pe.wait_ge(exp_done, g * STEPS * SET + s * SET - 1 + m)
                        pe.wait_ge(k_scaled, head * NT + 4 * m + 4)
                        for j in range(4):
                            end = pe.transpose(ps[:, 2 * m, j * P:(j + 1) * P], ksum[:, 4 * m + j, :], ident)
                        end.then_inc(kT_mm, 1)

                scored, values = exists(s, last), exists(s - 1, last)
                big = tile_of(s) >= NT // 2
                if s < 0:
                    project(0)
                    transpose_queries(0)
                    return
                if s % STEPS == 0 and scored:
                    if values:
                        for kt in early(s - 1):
                            transpose_probs(s - 1, kt)
                    transpose_keys(g + s // STEPS)
                    project(s + 1)
                    if values:
                        weigh_values(s - 1, 0)
                    scores(s, 0)
                    scores(s, 1)
                else:
                    if scored:
                        scores(s, 0)
                    if values:
                        for kt in early(s - 1):
                            transpose_probs(s - 1, kt)
                    if exists(s + 1, last):
                        project(s + 1)
                    if scored:
                        scores(s, 1)
                    if values:
                        weigh_values(s - 1, 0)
                if scored:
                    scores(s, 2)
                if values:
                    weigh_values(s - 1, 1)
                if scored:
                    scores(s, 3)
                if exists(s + 1, last) and big:
                    transpose_queries(s + 1)
                if exists(s - 3, last):
                    output(s - 3)
                if values:
                    weigh_values(s - 1, 2)
                if s in KV_PAIRS and not last:
                    pe.wait_ge(y_done, g * STEPS + s - 2)
                    keys_values(g + 1, KV_PAIRS[s], 4)
                if exists(s + 1, last) and not big:
                    transpose_queries(s + 1)
                if values:
                    weigh_values(s - 1, 3)
                    spread_recip(s - 1)

            for p in range(NT // 2):
                keys_values(0, p, p)
            pe.wait_ge(operands.masks_set, 2)
            slot(0, -1)
            for s in range(ROT):
                slot(0, s)
            with pe.Fori(0, NKV - 1) as g:
                for s in range(ROT, STEPS + ROT):
                    slot(g, s)
            for s in range(ROT, STEPS + 3):
                slot(NKV - 1, s, last=True)
            pe.wait_ge(y_done, NKV * STEPS)
            norm.tensor(pe)


def moe_stage(nc, ps, x_tok, xT_h, xT_l, ident, d, out):
    with ExitStack() as ctx:
        sb = lambda n, s, dt=F32: ctx.enter_context(nc.sbuf_tensor(f"m_{n}", s, dt))
        sem = lambda n: ctx.enter_context(nc.semaphore(f"m_{n}"))
        gate_w = sb("gate_w", [P, KD, NE])
        gate_b = sb("gate_b", [P, NE])
        xT = sb("xT", [P, KD, S])
        logit = sb("logit", [P, NT, NE + 4])
        best = sb("best", [P, NT, 8])
        marked = sb("marked", [P, NT, NE + 4])
        nbest = sb("nbest", [P, NT])
        coef = sb("coef", [P, NT, NE])
        esum, rsum = sb("esum", [P, NT]), sb("rsum", [P, NT])
        coefT = sb("coefT", [NE, S])
        b_down = sb("b_down", [NE, D])
        EPB = 4
        W = 3 * D
        raw = sb("raw", [P, EPB, W + 2])
        b_gu = sb("b_gu", [P, EPB, 2])
        w_h, w_l = sb("w_h", [P, EPB, W], F32R), sb("w_l", [P, EPB, W], F32R)
        gate = sb("gate", [P, 2, HALF])
        glu = sb("glu", [P, 2, HALF])
        up = sb("up", [P, 2, HALF])
        act_f = sb("act_f", [P, 2, HALF])
        act_h, act_l = sb("act_h", [P, 4, HALF], F32R), sb("act_l", [P, 4, HALF], F32R)

        gate_loaded, down_loaded, w_loaded = sem("gate_loaded"), sem("down_loaded"), [sem(f"w_loaded{j}") for j in range(EPB)]
        x_joined, logit_mm, logit_done, absent_set, best_done, slots_set = (sem(n) for n in (
            "x_joined", "logit_mm", "logit_done", "absent_set", "best_done", "slots_set"))
        marked_done, nbest_done, exp_done, sel_done, masked_done, esum_done, rsum_done, coef_done = (sem(n) for n in (
            "marked_done", "nbest_done", "exp_done", "sel_done", "masked_done", "esum_done", "rsum_done", "coef_done"))
        coefT_mm, coefT_done, bias_mm, bias_done = (sem(n) for n in ("coefT_mm", "coefT_done", "bias_mm", "bias_done"))
        w_hi, w_lo = sem("w_hi"), sem("w_lo")
        gu_mm, gate_done, glu_done, up_done, act_done, act_hi, act_lo = (sem(n) for n in (
            "gu_mm", "gate_done", "glu_done", "up_done", "act_done", "act_hi", "act_lo"))
        clip_done = sem("clip_done")
        down_mm, y_done, stored = sem("down_mm"), sem("y_done"), sem("stored")
        norm = Norm(nc, ctx, "mn", x_tok, None, None, ident, (None, None))
        TPH = HALF // P
        PER = EPB * NHALF
        LATER = 2

        block = ctx.enter_context(nc.Block())

        @block.sync
        def _(sp):
            sp.dma_start(gate_w[:], d["m_gate_w"].rearrange("(k p) n -> p k n", p=P)).then_inc(gate_loaded, 16)
            sp.dma_start(gate_b[:], d["m_gate_b"].broadcast_to([P, NE])).then_inc(gate_loaded, 16)
            for e in range(EPB):
                sp.dma_start(raw[:, e, :], d["m_w"][e]).then_inc(w_loaded[e], 16)
            sp.dma_start(b_down[:], d["m_b_down"]).then_inc(down_loaded, 16)
            with sp.Fori(1, NE // EPB) as i:
                for j in range(EPB):
                    sp.wait_ge(w_lo, EPB * i + j - EPB + 1)
                    sp.dma_start(raw[:, j, :], d["m_w"][EPB * i + j]).then_inc(w_loaded[j], 16)
            for t in range(NT):
                sp.wait_ge(norm.s_x, t + 1)
                sp.dma_start(out[t * P:(t + 1) * P, :], x_tok[:, t, :]).then_inc(stored, 16)
            sp.wait_ge(stored, 16 * NT)

        @block.gpsimd
        def _(pool):
            def wait(signal, count):
                count = pool.to_reg(count)
                pool.wait_ge(w_loaded[0], 16)
                pool.wait_ge(signal, count)

            def weights_low(i, j):
                wait(w_hi, EPB * i + j + 1)
                pool.tensor_tensor(w_l[:, j % EPB, :], raw[:, j % EPB, 0:W], w_h[:, j % EPB, :].bitcast(F32),
                                   ALU.subtract).then_inc(w_lo, 1)

            def units(i, first=False, last=False):
                for m in range(PER):
                    n = PER * i + m
                    wait(act_hi, n + 1)
                    pool.tensor_tensor(act_l[:, m % 4, :], act_f[:, m % 2, :], act_h[:, m % 4, :].bitcast(F32),
                                       ALU.subtract).then_inc(act_lo, 1)
                    j = m // NHALF + 2
                    if m % NHALF == 0 and not (last and j >= EPB):
                        weights_low(i, j)

            for j in range(2):
                weights_low(0, j)
            units(0, first=True)
            with pool.Fori(1, NE // EPB - 1) as i:
                units(i)
            units(NE // EPB - 1, last=True)
            norm.pool(pool)

        @block.scalar
        def _(act):
            def first_weights():
                for j in range(2):
                    act.wait_ge(w_loaded[j], 16)
                    act.activation(b_gu[:, j, :], raw[:, j, W:W + 2], ACT.Copy)
                    act.activation(w_h[:, j, :], raw[:, j, 0:W], ACT.Copy).then_inc(w_hi, 1)

            first_weights()
            for t in range(NT):
                act.wait_ge(nbest_done, 1)
                act.wait_ge(logit_done, NT)
                act.activation(coef[:, t, :], logit[:, t, 0:NE], ACT.Exp, bias=nbest[:, t:t + 1]).then_inc(exp_done, 1)
            for th in range(NHALF):
                act.wait_ge(coefT_mm, th + 1)
                act.activation(coefT[:, th * HALF:(th + 1) * HALF], ps[0:NE, 6 + th, :], ACT.Copy)\
                   .then_inc(coefT_done, 1)

            def weights_high(i, j):
                act.wait_ge(w_loaded[j % EPB], 16 * (i + j // EPB) + 16)
                if not (isinstance(i, int) and i == 0 and j < EPB):
                    act.wait_ge(down_mm, PER * i + NHALF * (j - EPB + 1))
                act.activation(b_gu[:, j % EPB, :], raw[:, j % EPB, W:W + 2], ACT.Copy)
                act.activation(w_h[:, j % EPB, :], raw[:, j % EPB, 0:W], ACT.Copy).then_inc(w_hi, 1)

            def units(i, first=False, last=False):
                for m in range(PER):
                    n = PER * i + m
                    act.wait_ge(gu_mm, n + 1)
                    if not first or m >= 2:
                        act.wait_ge(act_done, n - 1)
                    act.activation(up[:, m % 2, :], ps[:, 2 * (m % 2) + 1, :], ACT.Identity,
                                   bias=b_gu[:, m // NHALF, 1:2]).then_inc(up_done, 1)
                    act.wait_ge(gate_done, n + 1)
                    act.activation(glu[:, m % 2, :], gate[:, m % 2, :], ACT.Gelu_apprx_sigmoid).then_inc(glu_done, 1)
                    j = m // NHALF + 2
                    if m % NHALF == 0 and not (last and j >= EPB):
                        weights_high(i, j)
                    act.wait_ge(act_done, n + 1)
                    if not first or m >= 4:
                        act.wait_ge(down_mm, n - 3)
                    act.activation(act_h[:, m % 4, :], act_f[:, m % 2, :], ACT.Copy).then_inc(act_hi, 1)

            units(0, first=True)
            with act.Fori(1, NE // EPB - 1) as i:
                units(i)
            units(NE // EPB - 1, last=True)

        @block.vector
        def _(dve):
            for th in range(NHALF):
                cols = slice(th * HALF, (th + 1) * HALF)
                dve.tensor_tensor(xT[:, :, cols], xT_h[:, :, cols].bitcast(F32), xT_l[:, :, cols].bitcast(F32),
                                  ALU.add).then_inc(x_joined, 1)
            dve.wait_ge(gate_loaded, 16 * 2)
            dve.memset(logit[:, :, NE:NE + 4], ABSENT).then_inc(absent_set, 1)
            for t in range(NT):
                dve.wait_ge(logit_mm, t + 1)
                dve.tensor_tensor(logit[:, t, 0:NE], ps[:, t % 2, 0:NE], gate_b[:], ALU.add).then_inc(logit_done, 1)
            dve.wait_ge(absent_set, 1)
            for t in range(NT):
                dve.wait_ge(logit_done, t + 1)
                dve.max(best[:, t, :], logit[:, t, 0:NE]).then_inc(best_done, 1)
            dve.wait_ge(best_done, NT)
            dve.memset(best[:, :, TOPK:8], ABSENT).then_inc(slots_set, 1)
            dve.tensor_scalar(nbest[:], best[:, :, 0], -1.0, None, ALU.mult).then_inc(nbest_done, 1)
            dve.wait_ge(slots_set, 1)
            for t in range(NT):
                dve.match_replace(marked[:, t, :], best[:, t, :], logit[:, t, :], -ABSENT).then_inc(marked_done, 1)
            dve.wait_ge(marked_done, NT)
            dve.tensor_tensor(marked[:, :, 0:NE], marked[:, :, 0:NE], logit[:, :, 0:NE], ALU.not_equal)\
               .then_inc(sel_done, 1)
            dve.wait_ge(sel_done, 1)
            dve.wait_ge(exp_done, NT)
            dve.tensor_tensor(coef[:], coef[:], marked[:, :, 0:NE], ALU.mult).then_inc(masked_done, 1)
            dve.wait_ge(masked_done, 1)
            dve.tensor_reduce(esum[:], coef[:], AX.X, ALU.add).then_inc(esum_done, 1)
            dve.wait_ge(esum_done, 1)
            dve.reciprocal(rsum[:], esum[:]).then_inc(rsum_done, 1)
            dve.wait_ge(rsum_done, 1)
            for t in range(NT):
                dve.tensor_scalar(coef[:, t, :], coef[:, t, :], rsum[:, t:t + 1], None, ALU.mult)\
                   .then_inc(coef_done, 1)

            def add_biases():
                for q in range(NT // 2):
                    dve.wait_ge(bias_mm, q + 1)
                    dve.tensor_tensor(x_tok[:, 2 * q:2 * q + 2, :], ps[:, 4 + q, :].rearrange("p (t n) -> p t n", t=2),
                                      x_tok[:, 2 * q:2 * q + 2, :], ALU.add).then_inc(bias_done, 1)

            def add_half(n, m, i, j):
                dve.wait_ge(down_mm, n + 1)
                th = m % 2
                for q in range(TPH):
                    t = th * TPH + q
                    e = EPB * i + j
                    c = coef[:, t, bass.ds(e, 1)] if not isinstance(e, int) else coef[:, t, e:e + 1]
                    last = dve.scalar_tensor_tensor(
                        out=x_tok[:, t, :], in0=ps[:, 4 + 2 * th + q // 2, (q % 2) * D:(q % 2 + 1) * D],
                        scalar=c, in1=x_tok[:, t, :], op0=ALU.mult, op1=ALU.add)
                last.then_inc(y_done, 1)

            def units(i, first=False):
                for m in range(PER):
                    n = PER * i + m
                    dve.wait_ge(gu_mm, n + 1)
                    if not first or m >= 2:
                        dve.wait_ge(glu_done, n - 1)
                    dve.tensor_scalar(gate[:, m % 2, :], ps[:, 2 * (m % 2), :], b_gu[:, m // NHALF, 0:1], LIMIT,
                                      ALU.add, ALU.min).then_inc(gate_done, 1)
                    dve.wait_ge(up_done, n + 1)
                    dve.tensor_scalar(up[:, m % 2, :], up[:, m % 2, :], LIMIT, -LIMIT, ALU.min, ALU.max)\
                       .then_inc(clip_done, 1)
                    dve.wait_ge(clip_done, n + 1)
                    dve.wait_ge(glu_done, n + 1)
                    if not first or m >= 2:
                        dve.wait_ge(act_lo, n - 1)
                    dve.scalar_tensor_tensor(out=act_f[:, m % 2, :], in0=up[:, m % 2, :], scalar=1.0,
                                             in1=glu[:, m % 2, :], op0=ALU.add, op1=ALU.mult).then_inc(act_done, 1)
                    if first and m == 0:
                        add_biases()
                    if first and m == LATER:
                        dve.wait_ge(bias_done, NT // 2)
                    if not first or m >= LATER:
                        pm = (m - LATER) % PER
                        add_half(n - LATER, pm, i if m >= LATER else i - 1, pm // NHALF)

            units(0, first=True)
            with dve.Fori(1, NE // EPB) as i:
                units(i)
            for m in range(PER - LATER, PER):
                n = NE * NHALF - PER + m
                add_half(n, m, NE // EPB - 1, m // NHALF)
                dve.wait_ge(y_done, n + 1)
                for q in range(TPH):
                    norm.dve_stats(dve, m % NHALF * TPH + q)
            norm.dve_moments(dve)
            norm.dve_scale(dve)

        @block.tensor
        def _(pe):
            pe.wait_ge(gate_loaded, 16 * 2)
            for t in range(NT):
                pe.wait_ge(x_joined, 1 + t // TPH)
                if t >= 2:
                    pe.wait_ge(logit_done, t - 1)
                for k in range(KD):
                    last = pe.matmul(ps[:, t % 2, 0:NE], xT[:, k, t * P:(t + 1) * P], gate_w[:, k, :],
                                     start=(k == 0), stop=(k == KD - 1))
                last.then_inc(logit_mm, 1)

            def bias_terms():
                for th in range(NHALF):
                    pe.wait_ge(coef_done, TPH * (th + 1))
                    for q in range(TPH):
                        t = th * TPH + q
                        last = pe.transpose(ps[0:NE, 6 + th, q * P:(q + 1) * P], coef[:, t, :], ident)
                    last.then_inc(coefT_mm, 1)
                pe.wait_ge(down_loaded, 16)
                pe.wait_ge(coefT_done, NHALF)
                for q in range(NT // 2):
                    for j in range(2):
                        t = 2 * q + j
                        last = pe.matmul(ps[:, 4 + q, j * D:(j + 1) * D], coefT[:, t * P:(t + 1) * P], b_down[:],
                                         start=True, stop=True)
                    last.then_inc(bias_mm, 1)

            def gate_up(i, m, first):
                n = PER * i + m
                j, th = m // NHALF, m % NHALF
                if first and m == 0:
                    pe.wait_ge(logit_done, NT)
                if th == 0:
                    pe.wait_ge(w_lo, EPB * i + j + 1)
                if not first or m >= 2:
                    pe.wait_ge(up_done, n - 1)
                    pe.wait_ge(gate_done, n - 1)
                cols = slice(th * HALF, (th + 1) * HALF)
                for a in range(2):
                    for k in range(KD):
                        w = slice(a * D + k * NI, a * D + (k + 1) * NI)
                        last = split_matmul(pe, ps[:, 2 * (m % 2) + a, :], w_h[:, j, w], w_l[:, j, w],
                                            xT_h[:, k, cols], xT_l[:, k, cols], k == 0, k == KD - 1)
                last.then_inc(gu_mm, 1)

            def down(n, m, first):
                j, th = m // NHALF, m % NHALF
                pe.wait_ge(act_lo, n + 1)
                if not first:
                    pe.wait_ge(y_done, n - 1)
                elif m == 0:
                    pe.wait_ge(bias_done, NT // 2)
                for q in range(TPH):
                    last = split_matmul(pe, ps[:, 4 + 2 * th + q // 2, (q % 2) * D:(q % 2 + 1) * D],
                                        act_h[:, m % 4, q * P:(q + 1) * P], act_l[:, m % 4, q * P:(q + 1) * P],
                                        w_h[:, j, 2 * D:3 * D], w_l[:, j, 2 * D:3 * D], True, True)
                last.then_inc(down_mm, 1)

            def units(i, first=False):
                for m in range(PER):
                    gate_up(i, m, first)
                    if first and m == 1:
                        bias_terms()
                    if not first or m >= LATER:
                        down(PER * i + m - LATER, (m - LATER) % PER, first and m < LATER + 2)

            units(0, first=True)
            with pe.Fori(1, NE // EPB) as i:
                units(i)
            for m in range(PER - LATER, PER):
                down(NE * NHALF - PER + m, m, False)


def build(nc, d, out):
    with ExitStack() as ctx:
        sb = lambda n, s, dt=F32: ctx.enter_context(nc.sbuf_tensor(n, s, dt))
        sem = lambda n: ctx.enter_context(nc.semaphore(n))
        ps = ctx.enter_context(nc.psum_tensor("ps", [P, 8, HALF], F32))
        x_tok = sb("x_tok", [P, NT, D])
        xT_h, xT_l = sb("xT_h", [P, KD, S], F32R), sb("xT_l", [P, KD, S], F32R)
        ident = sb("ident", [P, P])
        operands = AttentionOperands(nc, ctx)
        with ExitStack() as first_stages:
            ffn = FfnOperands(nc, first_stages)
            retention_stage(nc, ps, x_tok, xT_h, xT_l, ident[:], ffn, operands, d)
            ffn_stage(nc, ps, x_tok, xT_h, xT_l, ident[:], ffn, d)
        attention_stage(nc, ps, x_tok, xT_h, xT_l, ident[:], operands, d)
        moe_stage(nc, ps, x_tok, xT_h, xT_l, ident[:], d, out)


def constants():
    import numpy as np
    f = np.float32
    gamma = (1.0 - np.exp2(np.linspace(np.log2(1.0 / 32.0), np.log2(1.0 / 512.0), RH).astype(f))).astype(f)
    gamma = gamma.astype(np.float64)
    i = np.arange(P)
    decay = np.where(i[None, :] >= i[:, None], gamma[:, None, None] ** np.maximum(i[None, :] - i[:, None], 0), 0.0)
    head_of = np.arange(D) // RD
    c = {
        "c_decay": decay.reshape(2, 4, P, P).transpose(2, 1, 0, 3).astype(f),
        "c_qgain": (gamma[head_of][:, None] ** (i[None, :] + 1)).reshape(2, P, P).transpose(1, 0, 2).astype(f),
        "c_kgain": (gamma[head_of][None, :] ** (P - 1 - i[:, None])).astype(f),
        "c_blockdiag": np.tile((i[:, None] // RD == i[None, :] // RD).astype(f), (1, 2)),
        "c_chunkgain": (gamma[head_of] ** P).reshape(2, P).T.astype(f),
        "c_ident": np.eye(P, dtype=f),
        "c_mask": np.where(i[None, :] <= i[:, None], 0.0, MASKED).astype(f),
    }
    inv = (1.0 / (f(1000000.0) ** (np.arange(0, HD, 2).astype(f) / f(HD)))).astype(f)
    ang = (np.arange(S).astype(f)[:, None] * inv[None, :]).astype(f).astype(np.float64)
    c["c_cos"] = np.concatenate([np.cos(ang), np.cos(ang)], 1).astype(f)
    c["c_sin"] = np.concatenate([-np.sin(ang), np.sin(ang)], 1).astype(f)
    return {k: np.ascontiguousarray(v) for k, v in c.items()}


def kernel(**inputs):
    import numpy as np
    import concourse.bacc as bacc
    from concourse.bass_utils import run_bass_kernel_spmd

    a = {k: np.asarray(v) for k, v in inputs.items()}
    x = a["L0_attn_x"].reshape(S, D)
    bqk = np.concatenate([a["L0_attn_bq"], a["L0_attn_bk"]]).reshape(4, P).T
    wq = a["L1_attn_Wq"].reshape(KD, P, NKV, SETS_PER_KV, SET * HD).transpose(2, 3, 1, 0, 4)
    wo = a["L1_attn_Wo"].reshape(NKV, SETS_PER_KV, SET, HD, D).transpose(0, 1, 3, 2, 4)
    per_kv = lambda w: w.reshape(KD, P, NKV, HD).transpose(2, 1, 0, 3)
    per_expert = lambda w: w.reshape(NE, KD, P, NI).transpose(0, 2, 1, 3).reshape(NE, P, D)
    arrays = {
        "x": x, "xT": x.T,
        "r_wqk": np.concatenate([a["L0_attn_Wq"], a["L0_attn_Wk"]], 1),
        "r_wkv": np.concatenate([a["L0_attn_Wk"], a["L0_attn_Wv"]], 1),
        "r_bqk": bqk,
        "r_bkv": np.concatenate([a["L0_attn_bk"], a["L0_attn_bv"]]).reshape(1, 2 * D),
        "f_up_q": a["L0_ffn_w_up_q"].T, "f_up_scale": a["L0_ffn_w_up_scale"].T,
        "f_up_a": a["L0_ffn_w_up_lora_a"].T, "f_up_b": a["L0_ffn_w_up_lora_b"],
        "f_down_q": a["L0_ffn_w_down_q"].T, "f_down_scale": a["L0_ffn_w_down_scale"].T,
        "f_down_a": a["L0_ffn_w_down_lora_a"].T, "f_down_b": a["L0_ffn_w_down_lora_b"],
        "f_b_up": a["L0_ffn_b_up"].reshape(FT, P).T, "f_b_down": a["L0_ffn_b_down"].reshape(1, D),
        "a_wkv": np.concatenate([per_kv(a["L1_attn_Wk"]), per_kv(a["L1_attn_Wv"])], 3).reshape(NKV, P, KD * 2 * HD),
        "a_wset": np.concatenate([wq.reshape(NKV, SETS_PER_KV, P, -1), wo.reshape(NKV, SETS_PER_KV, P, -1)], 3),
        "a_normw": np.stack([a["L1_attn_q_norm_w"], a["L1_attn_k_norm_w"]]).reshape(1, 2, HD),
        "m_gate_w": a["L1_ffn_gate_w"].T, "m_gate_b": a["L1_ffn_gate_b"].reshape(1, NE),
        "m_w": np.concatenate([per_expert(a["L1_ffn_w_gate"]), per_expert(a["L1_ffn_w_up"]), a["L1_ffn_w_down"],
                               a["L1_ffn_b_gate"][:, :, None], a["L1_ffn_b_up"][:, :, None]], 2),
        "m_b_down": a["L1_ffn_b_down"],
        **constants(),
    }
    arrays = {f"in_{k}": np.ascontiguousarray(v) for k, v in arrays.items()}
    nc = bacc.Bacc("TRN2", target_bir_lowering=False, num_devices=1)
    d = {k[3:]: nc.dram_tensor(k, v.shape, mybir.dt.from_np(v.dtype), kind="ExternalInput").ap()
         for k, v in arrays.items()}
    out = nc.dram_tensor("out_x", (S, D), F32, kind="ExternalOutput").ap()
    build(nc, d, out)
    r = run_bass_kernel_spmd(nc, [arrays], core_ids=[0])
    return r.results[0]["out_x"].reshape(a["L0_attn_x"].shape)
```
